# Optimizing a Trainium2 kernel written in Bass

```python
import numpy as np
import jax
import jax.numpy as jnp

def _softmax(x, axis=-1):
    return jax.nn.softmax(x, axis=axis)

def _gelu(x):
    return jax.nn.gelu(x, approximate=True)

def _silu(x):
    return jax.nn.silu(x)

def _sigmoid(x):
    return jax.nn.sigmoid(x)

def _layernorm(x, axis=-1, eps=1e-05):
    m = jnp.mean(x, axis=axis, keepdims=True)
    v = jnp.var(x, axis=axis, keepdims=True)
    return (x - m) / jnp.sqrt(v + eps)

def _scatter_add(tgt, idx, src, axis=0):
    return tgt.at[idx].add(src)

def _segment_sum(src, seg, n):
    return jax.ops.segment_sum(src, seg, n)
kernel_name = 'mk_perceiver_d1_seqx_r4_0eb1a5'

def setup_inputs(seed: int=0):
    np.random.seed(seed)
    _w = jnp.asarray

    def _rec_inputs():
        import jax
        import jax.numpy as jnp
        _rk = jax.random.key(seed)
        x = -0.0003929 + 0.9999 * jax.random.normal(jax.random.fold_in(_rk, 1), (1, 256, 256), jnp.float32)
        _lenS = 256 - jax.random.randint(jax.random.fold_in(_rk, 7), (1,), 0, max(1, 256 // 4) + 1, jnp.int32)
        _lenS2 = 4096 - jax.random.randint(jax.random.fold_in(_rk, 8), (1,), 0, max(1, 4096 // 4) + 1, jnp.int32)
        _ctx_2048P = jax.random.normal(jax.random.fold_in(_rk, 11), (1, 16, 512), jnp.float32)
        _ctx_2048c = jax.random.dirichlet(jax.random.fold_in(_rk, 511), 0.3 * jnp.ones((16,), jnp.float32), (1, 4096))
        _ctx_2048t = jnp.einsum('bsk,bkd->bsd', _ctx_2048c, _ctx_2048P)
        _ctx_2048t = _ctx_2048t * jax.lax.rsqrt(jnp.mean(jnp.square(_ctx_2048t)) + 1e-12) * 0.953939
        ctx_2048 = 4.13588e-05 + 0.999923 * (_ctx_2048t + 0.3 * jax.random.normal(jax.random.fold_in(_rk, 611), (1, 4096, 512), jnp.float32))
        _validS = jnp.arange(256)[None, :] < _lenS[:, None]
        _validS2 = jnp.arange(4096)[None, :] < _lenS2[:, None]
        _causal = jnp.tril(jnp.ones((256, 256), dtype=bool))
        mask_BxS2_if0 = jnp.where(jnp.ones((1, 4096), dtype=bool), 4, 0).astype(jnp.int32)
        return (x, ctx_2048, mask_BxS2_if0)
    x, ctx_2048, mask_BxS2_if0 = _rec_inputs()

    def _L0_xattn_setup():
        import jax, jax.numpy as jnp
        import numpy as np
        B, L, P = (4, 1024, 256)
        D_MODEL = 256
        D_GLOBAL = 512
        HEADDIM = 32
        EPSILON = 0.001
        RMS_EPS = 1e-05

        def rmsnorm(x, g, eps=RMS_EPS):
            var = jnp.mean(jnp.square(x), axis=-1, keepdims=True)
            return x * jax.lax.rsqrt(var + eps) * g

        def _hnet_depool(h, h_patch_full, patch_lens):
            h_patch = h_patch_full[..., :D_MODEL]
            bsz, plen = (h_patch.shape[0], h_patch.shape[1])
            seqlen = h.shape[1]
            logp = jnp.full((bsz, plen), -EPSILON, dtype=jnp.float32)
            bidx = jnp.cumsum(patch_lens, axis=1) - 1
            boundary_mask = jnp.zeros((bsz, seqlen), dtype=jnp.int32)
            boundary_mask = boundary_mask.at[jnp.arange(bsz)[:, None], bidx].set(1)
            dt = (-jnp.log(-jnp.expm1(logp))).astype(h_patch.dtype)
            x = h_patch / dt[..., None]
            n_heads = D_MODEL // HEADDIM
            A = -jnp.ones((n_heads,), dtype=jnp.float32)
            bcoef = jnp.exp(logp).astype(h_patch.dtype)
            x4 = x.reshape(bsz, plen, n_heads, HEADDIM)
            a = jnp.exp(dt[:, :, None] * A[None, None, :])
            u = (dt * bcoef)[:, :, None, None] * x4
            a_b = jnp.broadcast_to(a[..., None], u.shape)

            def comb(lft, rgt):
                aL, uL = lft
                aR, uR = rgt
                return (aL * aR, uL * aR + uR)
            _, s = jax.lax.associative_scan(comb, (a_b, u), axis=1)
            depool = s.reshape(bsz, plen, D_MODEL)
            plug = jnp.clip(jnp.cumsum(boundary_mask, axis=1) - 1, 0, plen - 1)
            depool_out = depool[jnp.arange(bsz)[:, None], plug]
            return depool_out + h
        key = jax.random.key(seed)
        k1, k2, k3, k4 = jax.random.split(key, 4)
        embeds = jax.random.normal(k1, (B, L, D_MODEL), dtype=jnp.float32)
        patch_embeds = jax.random.normal(k2, (B, P, D_GLOBAL), dtype=jnp.float32)
        patch_lens = jnp.full((B, P), L // P, dtype=jnp.int64)
        W_in = jax.random.normal(k3, (D_MODEL, D_MODEL), dtype=jnp.float32) * 0.02
        b_in = jnp.zeros((D_MODEL,), dtype=jnp.float32)
        g_res = jnp.ones((D_MODEL,), dtype=jnp.float32)
        g_init = jnp.ones((D_GLOBAL,), dtype=jnp.float32)
        return {'embeds': embeds, 'patch_embeds': patch_embeds, 'patch_lens': patch_lens, 'W_in': W_in, 'b_in': b_in, 'g_res': g_res, 'g_init': g_init}
    _L0_xattn_all = _L0_xattn_setup()
    _L0_xattn_in = {k: v for k, v in _L0_xattn_all.items() if k in ('W_in', 'b_in', 'g_res', 'g_init')}
    del _L0_xattn_all

    def _L0_attn_setup():
        import jax, jax.numpy as jnp
        import numpy as np
        B, T, D = (4, 512, 256)
        H, Kd = (4, 64)
        Vd = 128
        KEY_DIM, VAL_DIM = (H * Kd, H * Vd)
        CONV = 4
        EPS = 1e-06
        LN_EPS = 1e-05

        def _layernorm(x, g, b):
            m = jnp.mean(x, -1, keepdims=True)
            v = jnp.mean((x - m) ** 2, -1, keepdims=True)
            return (x - m) * jax.lax.rsqrt(v + LN_EPS) * g + b

        def _rmsnorm(x, w):
            return x * jax.lax.rsqrt(jnp.mean(x * x, -1, keepdims=True) + EPS) * w

        def _l2norm(x):
            return x * jax.lax.rsqrt(jnp.sum(x * x, -1, keepdims=True) + EPS)

        def _causal_conv_silu(x, w):
            t = x.shape[1]
            xp = jnp.pad(x, ((0, 0), (CONV - 1, 0), (0, 0)))
            y = xp[:, 0:t, :] * w[:, 0]
            for i in range(1, CONV):
                y = y + xp[:, i:i + t, :] * w[:, i]
            return jax.nn.silu(y)

        def _gated_delta_rule(q, k, v, g, beta):
            qT = jnp.moveaxis(q, 1, 0)
            kT = jnp.moveaxis(k, 1, 0)
            vT = jnp.moveaxis(v, 1, 0)
            gT = jnp.moveaxis(g, 1, 0)
            bT = jnp.moveaxis(beta, 1, 0)
            S0 = jnp.zeros((q.shape[0], H, Kd, Vd), q.dtype)

            def step(S, inp):
                q_t, k_t, v_t, g_t, b_t = inp
                S = S * jnp.exp(g_t)[..., None, None]
                kv = jnp.einsum('bhk,bhkv->bhv', k_t, S)
                delta = (v_t - kv) * b_t[..., None]
                S = S + k_t[..., :, None] * delta[..., None, :]
                o = jnp.einsum('bhk,bhkv->bhv', q_t, S)
                return (S, o)
            _, o = jax.lax.scan(step, S0, (qT, kT, vT, gT, bT))
            return jnp.moveaxis(o, 0, 1)

        def _forward(x, ln1_g, ln1_b, ln2_g, ln2_b, rms_in_w, Wq, Wk, Wv, conv_q_w, conv_k_w, conv_v_w, Wa, dt_bias, A_log, Wb, Wg, o_norm_w, Wo, W2, b2):
            b, t, _ = x.shape
            h = _layernorm(x, ln1_g, ln1_b)
            h = _rmsnorm(h, rms_in_w)
            q = _causal_conv_silu(h @ Wq, conv_q_w).reshape(b, t, H, Kd)
            k = _causal_conv_silu(h @ Wk, conv_k_w).reshape(b, t, H, Kd)
            v = _causal_conv_silu(h @ Wv, conv_v_w).reshape(b, t, H, Vd)
            q = _l2norm(q) * Kd ** (-0.5)
            k = _l2norm(k)
            g = -jnp.exp(A_log) * jax.nn.softplus(h @ Wa + dt_bias)
            beta = jax.nn.sigmoid(h @ Wb)
            o = _gated_delta_rule(q, k, v, g, beta)
            gate = (h @ Wg).reshape(b, t, H, Vd)
            o = _rmsnorm(o, o_norm_w) * jax.nn.silu(gate)
            enc = o.reshape(b, t, VAL_DIM) @ Wo
            x = x + enc
            h2 = _layernorm(x, ln2_g, ln2_b)
            x_out = jax.nn.gelu(h2 @ W2 + b2, approximate=False) + x
            return x_out
        key = jax.random.key(seed)
        ks = jax.random.split(key, 16)
        r = lambda k, shp, s=0.02: jax.random.normal(k, shp, dtype=jnp.float32) * s
        return {'x': jax.random.normal(ks[0], (B, T, D), dtype=jnp.float32), 'ln1_g': jnp.ones((D,), jnp.float32), 'ln1_b': jnp.zeros((D,), jnp.float32), 'ln2_g': jnp.ones((D,), jnp.float32), 'ln2_b': jnp.zeros((D,), jnp.float32), 'rms_in_w': jnp.ones((D,), jnp.float32), 'Wq': r(ks[1], (D, KEY_DIM)), 'Wk': r(ks[2], (D, KEY_DIM)), 'Wv': r(ks[3], (D, VAL_DIM)), 'conv_q_w': r(ks[4], (KEY_DIM, CONV), 0.3), 'conv_k_w': r(ks[5], (KEY_DIM, CONV), 0.3), 'conv_v_w': r(ks[6], (VAL_DIM, CONV), 0.3), 'Wa': r(ks[7], (D, H)), 'dt_bias': r(ks[8], (H,), 0.5), 'A_log': jnp.log(jax.random.uniform(ks[9], (H,), minval=1.0, maxval=16.0)), 'Wb': r(ks[10], (D, H)), 'Wg': r(ks[11], (D, VAL_DIM)), 'o_norm_w': jnp.ones((Vd,), jnp.float32), 'Wo': r(ks[12], (VAL_DIM, D)), 'W2': r(ks[13], (D, D)), 'b2': jnp.zeros((D,), jnp.float32)}
    _L0_attn_all = _L0_attn_setup()
    _L0_attn_in = {k: v for k, v in _L0_attn_all.items() if k in ('ln1_g', 'ln1_b', 'ln2_g', 'ln2_b', 'rms_in_w', 'Wq', 'Wk', 'Wv', 'conv_q_w', 'conv_k_w', 'conv_v_w', 'Wa', 'dt_bias', 'A_log', 'Wb', 'Wg', 'o_norm_w', 'Wo', 'W2', 'b2')}
    del _L0_attn_all

    def _L0_ffn_setup():
        import jax, jax.numpy as jnp
        import numpy as np
        B, S, D, H, DOUT, E, K = (4, 512, 256, 256, 256, 8, 2)
        key = jax.random.key(seed)
        k1, k2, k3, k4 = jax.random.split(key, 4)
        x = jax.random.normal(k1, (B, S, D), dtype=jnp.float32)
        Wr = jax.random.normal(k2, (D, E), dtype=jnp.float32) * 0.02
        Wi = jax.random.normal(k3, (E, D, H), dtype=jnp.float32) * 0.02
        Wo = jax.random.normal(k4, (E, H, DOUT), dtype=jnp.float32) * 0.02
        return {'x': x, 'Wr': Wr, 'Wi': Wi, 'Wo': Wo}
    _L0_ffn_all = _L0_ffn_setup()
    _L0_ffn_in = {k: v for k, v in _L0_ffn_all.items() if k in ('Wr', 'Wi', 'Wo')}
    del _L0_ffn_all
    return {'x': x, 'ctx_2048': ctx_2048, 'mask_BxS2_if0': mask_BxS2_if0, 'L0_xattn_W_in': _L0_xattn_in['W_in'], 'L0_xattn_b_in': _L0_xattn_in['b_in'], 'L0_xattn_g_res': _L0_xattn_in['g_res'], 'L0_xattn_g_init': _L0_xattn_in['g_init'], 'L0_attn_ln1_g': _L0_attn_in['ln1_g'], 'L0_attn_ln1_b': _L0_attn_in['ln1_b'], 'L0_attn_ln2_g': _L0_attn_in['ln2_g'], 'L0_attn_ln2_b': _L0_attn_in['ln2_b'], 'L0_attn_rms_in_w': _L0_attn_in['rms_in_w'], 'L0_attn_Wq': _L0_attn_in['Wq'], 'L0_attn_Wk': _L0_attn_in['Wk'], 'L0_attn_Wv': _L0_attn_in['Wv'], 'L0_attn_conv_q_w': _L0_attn_in['conv_q_w'], 'L0_attn_conv_k_w': _L0_attn_in['conv_k_w'], 'L0_attn_conv_v_w': _L0_attn_in['conv_v_w'], 'L0_attn_Wa': _L0_attn_in['Wa'], 'L0_attn_dt_bias': _L0_attn_in['dt_bias'], 'L0_attn_A_log': _L0_attn_in['A_log'], 'L0_attn_Wb': _L0_attn_in['Wb'], 'L0_attn_Wg': _L0_attn_in['Wg'], 'L0_attn_o_norm_w': _L0_attn_in['o_norm_w'], 'L0_attn_Wo': _L0_attn_in['Wo'], 'L0_attn_W2': _L0_attn_in['W2'], 'L0_attn_b2': _L0_attn_in['b2'], 'L0_ffn_Wr': _L0_ffn_in['Wr'], 'L0_ffn_Wi': _L0_ffn_in['Wi'], 'L0_ffn_Wo': _L0_ffn_in['Wo']}

def reference(x, ctx_2048, mask_BxS2_if0, L0_xattn_W_in, L0_xattn_b_in, L0_xattn_g_res, L0_xattn_g_init, L0_attn_ln1_g, L0_attn_ln1_b, L0_attn_ln2_g, L0_attn_ln2_b, L0_attn_rms_in_w, L0_attn_Wq, L0_attn_Wk, L0_attn_Wv, L0_attn_conv_q_w, L0_attn_conv_k_w, L0_attn_conv_v_w, L0_attn_Wa, L0_attn_dt_bias, L0_attn_A_log, L0_attn_Wb, L0_attn_Wg, L0_attn_o_norm_w, L0_attn_Wo, L0_attn_W2, L0_attn_b2, L0_ffn_Wr, L0_ffn_Wi, L0_ffn_Wo):
    import jax
    import jax.numpy as jnp

    def _L0_xattn_ref(embeds, patch_embeds, patch_lens, W_in, b_in, g_res, g_init):
        import jax, jax.numpy as jnp
        import numpy as np
        B, L, P = (4, 1024, 256)
        D_MODEL = 256
        D_GLOBAL = 512
        HEADDIM = 32
        EPSILON = 0.001
        RMS_EPS = 1e-05

        def rmsnorm(x, g, eps=RMS_EPS):
            var = jnp.mean(jnp.square(x), axis=-1, keepdims=True)
            return x * jax.lax.rsqrt(var + eps) * g

        def _hnet_depool(h, h_patch_full, patch_lens):
            h_patch = h_patch_full[..., :D_MODEL]
            bsz, plen = (h_patch.shape[0], h_patch.shape[1])
            seqlen = h.shape[1]
            logp = jnp.full((bsz, plen), -EPSILON, dtype=jnp.float32)
            bidx = jnp.cumsum(patch_lens, axis=1) - 1
            boundary_mask = jnp.zeros((bsz, seqlen), dtype=jnp.int32)
            boundary_mask = boundary_mask.at[jnp.arange(bsz)[:, None], bidx].set(1)
            dt = (-jnp.log(-jnp.expm1(logp))).astype(h_patch.dtype)
            x = h_patch / dt[..., None]
            n_heads = D_MODEL // HEADDIM
            A = -jnp.ones((n_heads,), dtype=jnp.float32)
            bcoef = jnp.exp(logp).astype(h_patch.dtype)
            x4 = x.reshape(bsz, plen, n_heads, HEADDIM)
            a = jnp.exp(dt[:, :, None] * A[None, None, :])
            u = (dt * bcoef)[:, :, None, None] * x4
            a_b = jnp.broadcast_to(a[..., None], u.shape)

            def comb(lft, rgt):
                aL, uL = lft
                aR, uR = rgt
                return (aL * aR, uL * aR + uR)
            _, s = jax.lax.associative_scan(comb, (a_b, u), axis=1)
            depool = s.reshape(bsz, plen, D_MODEL)
            plug = jnp.clip(jnp.cumsum(boundary_mask, axis=1) - 1, 0, plen - 1)
            depool_out = depool[jnp.arange(bsz)[:, None], plug]
            return depool_out + h
        h = rmsnorm(embeds, g_res)
        h = jnp.einsum('bld,ed->ble', h, W_in) + b_in
        h_patch = rmsnorm(patch_embeds, g_init)
        return _hnet_depool(h, h_patch, patch_lens)

    def _L0_attn_ref(x, ln1_g, ln1_b, ln2_g, ln2_b, rms_in_w, Wq, Wk, Wv, conv_q_w, conv_k_w, conv_v_w, Wa, dt_bias, A_log, Wb, Wg, o_norm_w, Wo, W2, b2):
        import jax, jax.numpy as jnp
        import numpy as np
        B, T, D = (4, 512, 256)
        H, Kd = (4, 64)
        Vd = 128
        KEY_DIM, VAL_DIM = (H * Kd, H * Vd)
        CONV = 4
        EPS = 1e-06
        LN_EPS = 1e-05

        def _layernorm(x, g, b):
            m = jnp.mean(x, -1, keepdims=True)
            v = jnp.mean((x - m) ** 2, -1, keepdims=True)
            return (x - m) * jax.lax.rsqrt(v + LN_EPS) * g + b

        def _rmsnorm(x, w):
            return x * jax.lax.rsqrt(jnp.mean(x * x, -1, keepdims=True) + EPS) * w

        def _l2norm(x):
            return x * jax.lax.rsqrt(jnp.sum(x * x, -1, keepdims=True) + EPS)

        def _causal_conv_silu(x, w):
            t = x.shape[1]
            xp = jnp.pad(x, ((0, 0), (CONV - 1, 0), (0, 0)))
            y = xp[:, 0:t, :] * w[:, 0]
            for i in range(1, CONV):
                y = y + xp[:, i:i + t, :] * w[:, i]
            return jax.nn.silu(y)

        def _gated_delta_rule(q, k, v, g, beta):
            qT = jnp.moveaxis(q, 1, 0)
            kT = jnp.moveaxis(k, 1, 0)
            vT = jnp.moveaxis(v, 1, 0)
            gT = jnp.moveaxis(g, 1, 0)
            bT = jnp.moveaxis(beta, 1, 0)
            S0 = jnp.zeros((q.shape[0], H, Kd, Vd), q.dtype)

            def step(S, inp):
                q_t, k_t, v_t, g_t, b_t = inp
                S = S * jnp.exp(g_t)[..., None, None]
                kv = jnp.einsum('bhk,bhkv->bhv', k_t, S)
                delta = (v_t - kv) * b_t[..., None]
                S = S + k_t[..., :, None] * delta[..., None, :]
                o = jnp.einsum('bhk,bhkv->bhv', q_t, S)
                return (S, o)
            _, o = jax.lax.scan(step, S0, (qT, kT, vT, gT, bT))
            return jnp.moveaxis(o, 0, 1)

        def _forward(x, ln1_g, ln1_b, ln2_g, ln2_b, rms_in_w, Wq, Wk, Wv, conv_q_w, conv_k_w, conv_v_w, Wa, dt_bias, A_log, Wb, Wg, o_norm_w, Wo, W2, b2):
            b, t, _ = x.shape
            h = _layernorm(x, ln1_g, ln1_b)
            h = _rmsnorm(h, rms_in_w)
            q = _causal_conv_silu(h @ Wq, conv_q_w).reshape(b, t, H, Kd)
            k = _causal_conv_silu(h @ Wk, conv_k_w).reshape(b, t, H, Kd)
            v = _causal_conv_silu(h @ Wv, conv_v_w).reshape(b, t, H, Vd)
            q = _l2norm(q) * Kd ** (-0.5)
            k = _l2norm(k)
            g = -jnp.exp(A_log) * jax.nn.softplus(h @ Wa + dt_bias)
            beta = jax.nn.sigmoid(h @ Wb)
            o = _gated_delta_rule(q, k, v, g, beta)
            gate = (h @ Wg).reshape(b, t, H, Vd)
            o = _rmsnorm(o, o_norm_w) * jax.nn.silu(gate)
            enc = o.reshape(b, t, VAL_DIM) @ Wo
            x = x + enc
            h2 = _layernorm(x, ln2_g, ln2_b)
            x_out = jax.nn.gelu(h2 @ W2 + b2, approximate=False) + x
            return x_out
        return _forward(x, ln1_g, ln1_b, ln2_g, ln2_b, rms_in_w, Wq, Wk, Wv, conv_q_w, conv_k_w, conv_v_w, Wa, dt_bias, A_log, Wb, Wg, o_norm_w, Wo, W2, b2)

    def _L0_ffn_ref(x, Wr, Wi, Wo):
        import jax, jax.numpy as jnp
        import numpy as np
        B, S, D, H, DOUT, E, K = (4, 512, 256, 256, 256, 8, 2)
        b, s, d = x.shape
        e_cnt, _, h = Wi.shape
        dout = Wo.shape[2]
        xf = x.reshape(-1, d)
        T = xf.shape[0]
        probs = jax.nn.softmax(xf @ Wr, axis=-1)
        topk_p, topk_i = jax.lax.top_k(probs, K)
        mask = topk_i[:, :, None] == jnp.arange(e_cnt)[None, None, :]
        hmix = jnp.zeros((T, K, h), dtype=xf.dtype)
        for e in range(e_cnt):
            he = xf @ Wi[e]
            hmix = hmix + jnp.where(mask[:, :, e][:, :, None], he[:, None, :], 0.0)
        o = jnp.zeros((T, K, dout), dtype=xf.dtype)
        for e in range(e_cnt):
            oe = jnp.einsum('tkh,hd->tkd', hmix, Wo[e])
            o = o + jnp.where(mask[:, :, e][:, :, None], oe, 0.0)
        out = jnp.sum(o * topk_p[:, :, None], axis=1)
        return out.reshape(b, s, dout)
    x = x + _L0_xattn_ref(_layernorm(x, axis=-1), ctx_2048, mask_BxS2_if0, L0_xattn_W_in, L0_xattn_b_in, L0_xattn_g_res, L0_xattn_g_init)
    x = x + _L0_attn_ref(_layernorm(x, axis=-1), L0_attn_ln1_g, L0_attn_ln1_b, L0_attn_ln2_g, L0_attn_ln2_b, L0_attn_rms_in_w, L0_attn_Wq, L0_attn_Wk, L0_attn_Wv, L0_attn_conv_q_w, L0_attn_conv_k_w, L0_attn_conv_v_w, L0_attn_Wa, L0_attn_dt_bias, L0_attn_A_log, L0_attn_Wb, L0_attn_Wg, L0_attn_o_norm_w, L0_attn_Wo, L0_attn_W2, L0_attn_b2)
    x = x + _L0_ffn_ref(_layernorm(x, axis=-1), L0_ffn_Wr, L0_ffn_Wi, L0_ffn_Wo)
    return x

_drawn_inputs = setup_inputs


def setup_inputs(seed=0):
    import zlib

    import numpy as np

    out = dict(_drawn_inputs(seed))
    spreads = {'L0_xattn_b_in': (0.0, 0.1),
     'L0_xattn_g_res': (1.0, 0.2),
     'L0_xattn_g_init': (1.0, 0.2),
     'L0_attn_ln1_g': (1.0, 0.6),
     'L0_attn_ln1_b': (0.0, 0.8),
     'L0_attn_ln2_g': (1.0, 0.6),
     'L0_attn_ln2_b': (0.0, 0.8),
     'L0_attn_rms_in_w': (1.0, 0.6),
     'L0_attn_o_norm_w': (1.0, 0.6),
     'L0_attn_b2': (0.0, 0.335)}
    factors = {'L0_attn_Wq': 3.499,
     'L0_attn_Wk': 3.578,
     'L0_attn_Wv': 3.507,
     'L0_attn_conv_q_w': 3.34,
     'L0_attn_conv_k_w': 3.357,
     'L0_attn_conv_v_w': 3.353,
     'L0_attn_Wa': 8.0,
     'L0_attn_dt_bias': 8.0,
     'L0_attn_A_log': 8.0,
     'L0_attn_Wb': 8.0,
     'L0_attn_Wg': 3.536,
     'L0_attn_Wo': 3.445,
     'L0_ffn_Wr': 6.034,
     'L0_ffn_Wi': 5.451,
     'L0_ffn_Wo': 5.384}
    for name, (base, spread) in spreads.items():
        noise = np.random.default_rng([zlib.crc32(name.encode()), seed]).standard_normal(out[name].shape)
        drawn = base * np.exp(spread * noise) if base else spread * noise
        out[name] = jnp.asarray(drawn.astype(out[name].dtype))
    for name, factor in factors.items():
        out[name] = (out[name] * factor).astype(out[name].dtype)
    return out
```

```python
import concourse.bass as bass
from concourse import mybir
from contextlib import ExitStack
import numpy as np

T, D, P = 256, 256, 128
H, KD, VD, TAPS = 4, 64, 128, 4
E, LENS, CTXD = 8, 4096, 512
NBLK = T // P
LCOL = LENS // P
LN_EPS, RMS_EPS, QK_EPS = 1e-5, 1e-5, 1e-6
QC, KC, VC, GC, ABC, WCOLS = 0, 256, 512, 1024, 1536, 1544
LEVELS = (2, 4, 8, 16, 32)
ATANH = (1 / 15, 1 / 13, 1 / 11, 1 / 9, 1 / 7, 1 / 5, 1 / 3)

CONST = {}
_at = 0
for _name, _width in (("ident", P), ("tri_le", P), ("tri_gt", P), ("tri_lt", P), ("decay", 3 * P),
                      ("levels", 64 * (1 + len(LEVELS))), ("ident64", 64), ("headones", 2), ("scol", 2),
                      ("iota16", 16), ("idxdesc", E), ("mask_d", 16), ("mask_lt", 16), ("reset", 3 * LCOL)):
    CONST[_name] = (_at, _at + _width)
    _at += _width
NCONST = _at
G_RES, RMS_W, O_W, CONV, NCOLS = 0, 2, 4, 5, 5 + 8 * TAPS
R_GINIT, R_LN1G, R_LN1B, R_LN2G, R_LN2B, R_DTB, R_ALOG, NROWS = 0, 256, 512, 768, 1024, 1280, 1284, 1288


def shape_constants():
    c = np.zeros((P, NCONST), np.float32)

    def put(name, a):
        c[:a.shape[0], CONST[name][0]:CONST[name][1]] = a

    i = np.arange(P)
    put("ident", np.eye(P))
    put("tri_le", i[:, None] <= i[None])
    put("tri_gt", i[:, None] > i[None])
    put("tri_lt", i[:, None] < i[None])
    a, b = -np.expm1(-0.001), np.exp(-0.001)
    t = np.arange(T)
    lag = t[None, :] - t[:, None]
    L = np.where(lag >= 0, b * a ** np.maximum(lag, 0), 0.0)
    put("decay", np.concatenate([L[:P, :P], L[:P, P:], L[P:, P:]], 1))
    j = np.arange(64)
    masks = []
    for m in (1,) + LEVELS:
        up = (j[:, None] // m + 1 == j[None] // m) & (j[:, None] // m % 2 == 0)
        masks.append(np.tile(-up.astype(np.float32), (2, 1)))
    put("levels", np.concatenate(masks, 1))
    put("ident64", np.tile(np.eye(64), (2, 1)))
    put("headones", i[:, None] // KD == np.arange(2)[None])
    put("scol", i[:, None] + 1 + P * np.arange(2)[None])
    put("iota16", np.tile(np.arange(16), (P, 1)))
    put("idxdesc", np.tile(np.arange(E, 0, -1), (P, 1)))
    put("mask_d", np.eye(16))
    put("mask_lt", np.arange(16)[:, None] < np.arange(16)[None])
    put("reset", np.tile((np.arange(3 * LCOL) % LCOL != 0), (P, 1)))
    return c


def program(nc, A_x, A_ctx, A_lens, A_consts, A_cols, A_rows, A_brow, A_win, A_wcat, A_wo, A_w2, A_wr, A_wit, A_fwo, out):
    f32, bf16, i32 = mybir.dt.float32, mybir.dt.bfloat16, mybir.dt.int32
    ALU, ACT, AX = mybir.AluOpType, mybir.ActivationFunctionType, mybir.AxisListType

    ctx = ExitStack()
    with ctx:
        def sb(name, shape, dt=f32):
            return ctx.enter_context(nc.sbuf_tensor(name, shape, dt))

        def sem(name):
            return ctx.enter_context(nc.semaphore(name))

        x_in = sb("x_in", [P, NBLK, D])
        ctx_in = sb("ctx_in", [P, NBLK, CTXD])
        lens_in = sb("lens_in", [P, LCOL], i32)
        consts = sb("consts", [P, NCONST])
        cols = sb("cols", [P, NCOLS])
        rows = sb("rows", [P, NROWS])
        brow = sb("brow", [1, 2, D])
        win = sb("win", [P, 2, D])
        wcat = sb("wcat", [P, 2, WCOLS])
        wo = sb("wo", [P, H, D])
        w2 = sb("w2", [P, 2, D])
        wr = sb("wr", [P, 2, E])
        wit = sb("wit", [P, E, 2, D])
        fwo = sb("fwo", [P, E, 2, D])
        ones = sb("ones", [P, P])
        eps = sb("eps", [P, 3])

        def C(name, parts=P):
            return consts[0:parts, CONST[name][0]:CONST[name][1]]

        ident = C("ident")

        st = sb("st", [P, NBLK, 6])
        mv = sb("mv", [P, NBLK, 2])
        sd = sb("sd", [P, NBLK])
        rstd = sb("rstd", [P, NBLK])
        xn = sb("xn", [P, NBLK, D])
        xT = sb("xT", [P, 2, T])
        sqj = sb("sqj", [P, CTXD])
        sqj2 = sb("sqj2", [P, CTXD])
        css = sb("css", [P, NBLK])
        csd = sb("csd", [P, NBLK])
        crs = sb("crs", [P, NBLK])
        cs = sb("cs", [P, NBLK, D])
        dep = sb("dep", [P, NBLK, D])
        limb = sb("limb", [P, 3, LCOL], i32)
        lscan = sb("lscan", [P, 3, LCOL])
        csum = sb("csum", [P, 3, LCOL], i32)
        lo0 = sb("lo0", [P, LCOL], i32)
        ca0 = sb("ca0", [P, LCOL], i32)
        s1_ = sb("s1_", [P, LCOL], i32)
        lo1 = sb("lo1", [P, LCOL], i32)
        ca1 = sb("ca1", [P, LCOL], i32)
        s2_ = sb("s2_", [P, LCOL], i32)
        lo2 = sb("lo2", [P, LCOL], i32)
        tf = sb("tf", [P, 5, LCOL])
        pos = sb("pos", [P, LCOL], i32)
        pos_hi = sb("pos_hi", [P, LCOL], i32)
        pos_lo = sb("pos_lo", [P, LCOL], i32)
        oh_hi = sb("oh_hi", [P, LCOL, 16], bf16)
        oh_lo = sb("oh_lo", [P, LCOL, 16], bf16)
        bound = sb("bound", [16, 16])
        bscan = sb("bscan", [16, 16])
        prer = sb("prer", [16, 16, 16])
        cumr = sb("cumr", [16, 16, 16])
        gT = sb("gT", [P, 2, T])
        x1 = sb("x1", [P, NBLK, D])

        st1 = sb("st1", [P, NBLK, 6])
        mv1 = sb("mv1", [P, NBLK, 2])
        sd1 = sb("sd1", [P, 2, NBLK])
        rs1 = sb("rs1", [P, 2, NBLK])
        y = sb("y", [P, NBLK, D])
        z0 = sb("z0", [P, NBLK, D])
        z = sb("z", [P, NBLK, D])
        zss = sb("zss", [P, NBLK])
        zsd = sb("zsd", [P, NBLK])
        zrs = sb("zrs", [P, NBLK])
        hh = xn
        hT = sb("hT", [P, 2, T])
        cv = sb("cv", [P, 8, T])
        sv = sb("sv", [P, 8, T])
        ksq = sb("ksq", [P, 2, T])
        qsq = sb("qsq", [P, 2, T])
        xa = sb("xa", [P, NBLK, H])
        nx = sb("nx", [P, NBLK, H])
        ea = sb("ea", [P, NBLK, 8])
        ex = sb("ex", [P, NBLK, 8])
        expA = sb("expA", [P, H])
        sp = sb("sp", [P, 6, NBLK, H])
        poly = sb("poly", [P, 9, NBLK, H])
        g = sb("g", [P, NBLK, H])
        gM = sb("gM", [P, NBLK, H, P])
        E1 = sb("E1", [P, H, T])
        E2 = sb("E2", [P, H, P])
        kss = sb("kss", [P, NBLK, H])
        kse = sb("kse", [P, NBLK, H])
        half = sb("half", [P, NBLK, H])
        ksr = sb("ksr", [P, NBLK, H])
        cden = sb("cden", [P, NBLK, H])
        cfac = sb("cfac", [P, NBLK, H])
        AT1 = sb("AT1", [P, H, T])
        AT2 = sb("AT2", [P, H, P])
        PT1 = sb("PT1", [P, H, T])
        PT2 = sb("PT2", [P, H, P])
        Ats = sb("Ats", [P, NBLK, H, P])
        X = sb("X", [P, NBLK, H, 64])
        XT = sb("XT", [P, NBLK, H, 64])
        U = sb("U", [P, NBLK, H, 64])
        U128 = sb("U128", [64, NBLK, H, 64])
        XTF = sb("XTF", [P, NBLK, H, P])
        vp = sb("vp", [P, NBLK, H, VD])
        F = sb("F", [P, NBLK, H, VD])
        R2 = sb("R2", [P, H, VD])
        qe = sb("qe", [P, NBLK, H])
        sg = sb("sg", [P, NBLK, H, VD])
        osq = gM
        oms = sb("oms", [P, NBLK, H])
        omv = sb("omv", [P, NBLK, H])
        osd = sb("osd", [P, NBLK, H])
        ors = sb("ors", [P, NBLK, H])
        og = Ats
        ogT = vp
        w = sb("w", [P, NBLK, D])
        base = dep
        st2 = sb("st2", [P, NBLK, 6])
        mv2 = sb("mv2", [P, NBLK, 2])
        sd2 = sb("sd2", [P, NBLK])
        rs2 = sb("rs2", [P, NBLK])
        h0 = z0
        h2 = z
        h2T = xT
        ge = sb("ge", [P, NBLK, D])
        x2 = sb("x2", [P, NBLK, D])

        wp = sb("wp", [P, 2, E, D])
        st3 = sb("st3", [P, NBLK, 6])
        mv3 = sb("mv3", [P, NBLK, 2])
        sd3 = sb("sd3", [P, NBLK])
        rs3 = sb("rs3", [P, NBLK])
        x3 = xn
        x3T = hT
        lmax = sb("lmax", [P, NBLK])
        lsh = sb("lsh", [P, NBLK, E])
        pe_ = sb("pe_", [P, NBLK, E])
        psum_ = sb("psum_", [P, NBLK])
        prec = sb("prec", [P, NBLK])
        top = sb("top", [P, 2, NBLK])
        eqm = sb("eqm", [P, 2, NBLK, E])
        scr = sb("scr", [P, 2, NBLK, E])
        first = sb("first", [P, 2, NBLK])
        hot = sb("hot", [P, 2, NBLK, E])
        rest = sb("rest", [P, NBLK, E])
        both = sb("both", [P, NBLK, E])
        wgt0 = sb("wgt0", [P, NBLK, E])
        wgt = sb("wgt", [P, NBLK, E])
        acc = cs

        B = [ctx.enter_context(nc.psum_tensor(f"B{i}", [P, 512], f32)) for i in range(8)]

        names = """ld_x ld_ctx ld_lens ld_consts ld_cols ld_rows ld_brow ld_win ld_wcat ld_wo ld_w2 ld_wr st_out
            ones_set eps_set half_set
            var_a xn_ready cs_ready limbs_summed carries_ready onehots_ready bounds_ready plug_ready onehot_t dep_ready
            x1_ready var_1 z_ready hh_ready xT0 xT1 hT0 hT1 ctx_ss sd_ctx sd_a sd_b sd_z z_ss
            x_turned dep_done limb_offsets bound_counts cum_rows x1_done hh_turned ab_done
            tile_done tap_last conv_done silu_done gate_done v_silu
            ea_ready exp_a expA_ready g_masked decay_mm decay_exp masked_e
            ksq_ready ss_done kse_ready ksr_ready qsq_ready kk_done at_ready a_turned ats_ready
            x_base xt_base u_done u_ready x_done x_ready xt_ready xt64_done xt64_ready x64_ready
            u128_done u128_ready xt128_done xt128_ready xtf_diag
            v_turned vp_ready qk_done pt_ready qe_ready f_done f_ready r_done r_ready o_done osq_ready oms_ready
            sd_o og_ready og_turned ogt_ready enc_done w_ready var_2 sd_2 h2_ready h2_turned h2t0 h2t1 w2_done
            gelu_ready x2_ready var_3 sd_3 x3_ready x3_turned x3t0 x3t1 logits_done lsh_ready pe_ready
            moe_done moe_used out_ready wp_done wp_ready
            dve_step act_step pool_step""".split()
        S = {n: sem(n) for n in names}
        ld_moe = [sem(f"ld_moe{i}") for i in range(4)]
        block = ctx.enter_context(nc.Block())

        RING = (2, 3, 4)
        TILES = (2, 3, 4, 5, 6, 7, 0, 1)
        order = {tile: n for n, tile in enumerate(TILES)}
        tile_bank = {tile: B[RING[n % 3]] for n, tile in enumerate(TILES)}
        gate_bank = [B[RING[(8 + b) % 3]] for b in range(NBLK)]
        small = B[5]
        tile_col = {0: QC, 1: QC + P, 2: KC, 3: KC + P, 4: VC, 5: VC + P, 6: VC + 2 * P, 7: VC + 3 * P}
        EARLY = 2
        wp_bank = [B[6 + e] if e < EARLY else B[3 + e % 2] for e in range(E)]
        UB, XB = (B[1], B[6]), (B[7], B[0])
        kk_bank = (B[7], B[0], B[1], B[6])
        qk_bank = (B[2], B[3], B[4], B[5])
        moe_bank = [B[i] for i in (6, 0, 2, 3)]

        @block.sync
        def _(sp_):
            sp_.dma_start(x_in[:], A_x.rearrange("(b p) d -> p b d", p=P)).then_inc(S["ld_x"], 16)
            sp_.dma_start(ctx_in[:], A_ctx.rearrange("(b p) d -> p b d", p=P)).then_inc(S["ld_ctx"], 16)
            sp_.dma_start(win[:], A_win).then_inc(S["ld_win"], 16)
            sp_.dma_start(wcat[:], A_wcat).then_inc(S["ld_wcat"], 16)
            for i in range(4):
                sp_.dma_start(wit[:, 2 * i:2 * i + 2], A_wit[:, 2 * i:2 * i + 2]).then_inc(ld_moe[i], 16)
                sp_.dma_start(fwo[:, 2 * i:2 * i + 2], A_fwo[:, 2 * i:2 * i + 2]).then_inc(ld_moe[i], 16)
            sp_.dma_start(wo[:], A_wo).then_inc(S["ld_wo"], 16)
            sp_.dma_start(w2[:], A_w2).then_inc(S["ld_w2"], 16)
            sp_.dma_start(wr[:], A_wr).then_inc(S["ld_wr"], 16)
            for b in range(NBLK):
                sp_.wait_ge(S["out_ready"], b + 1)
                sp_.dma_start(out[b * P:(b + 1) * P, :], acc[:, b]).then_inc(S["st_out"], 16)
            sp_.wait_ge(S["st_out"], 16 * NBLK)

        @block.gpsimd
        def _(pool):
            pool.memset(ones[:], 1.0).then_inc(S["ones_set"], 1)
            pool.memset(eps[:, 0:1], RMS_EPS)
            pool.memset(eps[:, 1:2], LN_EPS * LN_EPS)
            pool.memset(eps[:, 2:3], QK_EPS).then_inc(S["eps_set"], 1)
            pool.memset(half[:], 0.5).then_inc(S["half_set"], 1)
            pool.wait_ge(S["half_set"], 1)
            pool.wait_ge(S["kse_ready"], 1)
            pool.tensor_tensor(ksr[:], kse[:], half[:], ALU.pow).then_inc(S["ksr_ready"], 1)
            for b in range(NBLK):
                pool.wait_ge(S["at_ready"], 4 * (b + 1))
                e = E1[:, :, 0:P] if b == 0 else E2[:]
                pool.tensor_tensor(e, e, C("tri_le").unsqueeze(1).broadcast_to([P, H, P]), ALU.mult)\
                    .then_inc(S["masked_e"], 1)
            for i in range(2):
                pool.wait_ge(S["silu_done"], order[i] + 1)
                pool.tensor_tensor(qsq[:, i], sv[:, i], sv[:, i], ALU.mult).then_inc(S["qsq_ready"], 1)

        @block.scalar
        def _(act):
            act.dma_start(consts[:], A_consts).then_inc(S["ld_consts"], 16)
            act.dma_start(lens_in[:], A_lens.rearrange("(p c) -> p c", p=P)).then_inc(S["ld_lens"], 16)
            act.dma_start(cols[:], A_cols).then_inc(S["ld_cols"], 16)
            act.dma_start(rows[:], A_rows.partition_broadcast(P)).then_inc(S["ld_rows"], 16)
            act.dma_start(brow[:], A_brow).then_inc(S["ld_brow"], 16)
            n = [0]

            def mark(ins):
                ins.then_inc(S["act_step"], 1)
                n[0] += 1
                return n[0]

            def need(k):
                act.wait_ge(S["act_step"], k)

            act.wait_ge(S["ld_ctx"], 16)
            act.activation(sqj[:], ctx_in[:, 0], ACT.Square, accum_out=css[:, 0:1]).then_inc(S["ctx_ss"], 1)
            act.activation(sqj2[:], ctx_in[:, 1], ACT.Square, accum_out=css[:, 1:2]).then_inc(S["ctx_ss"], 1)
            act.wait_ge(S["eps_set"], 1)
            act.wait_ge(S["var_a"], 1)
            act.activation(sd[:], mv[:, :, 1], ACT.Sqrt, scale=1.0 + RMS_EPS, bias=eps[:, 1:2]).then_inc(S["sd_a"], 1)
            act.wait_ge(S["ctx_ss"], 2)
            act.activation(csd[:], css[:], ACT.Sqrt, scale=1.0 / CTXD, bias=eps[:, 0:1]).then_inc(S["sd_ctx"], 1)
            act.wait_ge(S["x_turned"], 2)
            act.wait_ge(S["ld_cols"], 16)
            act.activation(xT[:, 1], B[1][:, 0:T], ACT.Copy, scale=cols[:, G_RES + 1:G_RES + 2]).then_inc(S["xT1"], 1)

            def evac_wp(e):
                act.wait_ge(S["wp_done"], e + 1)
                act.activation(wp[:, :, e], wp_bank[e][:].rearrange("p (m d) -> p m d", m=2), ACT.Copy)\
                    .then_inc(S["wp_ready"], 1)

            act.wait_ge(S["var_1"], 1)
            act.activation(sd1[:, 0], mv1[:, :, 1], ACT.Sqrt, bias=eps[:, 0:1]).then_inc(S["sd_b"], 1)
            act.activation(sd1[:, 1], mv1[:, :, 1], ACT.Sqrt, scale=1.0 + LN_EPS, bias=eps[:, 1:2]).then_inc(S["sd_b"], 1)
            for b in range(NBLK):
                act.wait_ge(S["z_ready"], b + 1)
                act.activation((sqj if b == 0 else sqj2)[:, 0:D], z[:, b], ACT.Square, accum_out=zss[:, b:b + 1])\
                    .then_inc(S["z_ss"], 1)
            act.wait_ge(S["z_ss"], 2)
            act.activation(zsd[:], zss[:], ACT.Sqrt, scale=1.0 / D, bias=eps[:, 2:3]).then_inc(S["sd_z"], 1)
            act.wait_ge(S["ld_rows"], 16)
            act.activation(expA[:], rows[:, R_ALOG:R_ALOG + H], ACT.Exp).then_inc(S["expA_ready"], 1)
            act.wait_ge(S["hh_turned"], 2)
            act.activation(hT[:, 1], B[1][:, 0:T], ACT.Copy, scale=cols[:, RMS_W + 1:RMS_W + 2]).then_inc(S["hT1"], 1)
            act.wait_ge(S["ea_ready"], 1)
            act.activation(ex[:], ea[:], ACT.Exp).then_inc(S["exp_a"], 1)

            def last_tap(tile):
                act.wait_ge(S["tile_done"], order[tile] + 1)
                act.activation(cv[:, tile], tile_bank[tile][:, 0:T], ACT.Copy,
                               scale=cols[:, CONV + TAPS * tile + 3:CONV + TAPS * tile + 4]).then_inc(S["tap_last"], 1)

            def silu(tile):
                act.wait_ge(S["conv_done"], order[tile] + 1)
                act.activation(sv[:, tile], cv[:, tile], ACT.Silu).then_inc(S["silu_done"], 1)

            def gate(b):
                act.wait_ge(S["tile_done"], 9 + b)
                act.activation(sg[:, b].rearrange("p h v -> p (h v)"), gate_bank[b][:], ACT.Silu)\
                    .then_inc(S["gate_done"], 1)

            def exp_decay(i):
                act.wait_ge(S["decay_mm"], i + 1)
                o, bank = ((E1[:, :, 0:P], B[0]), (E1[:, :, P:T], B[1]), (E2[:], B[6]))[i]
                act.activation(o, bank[:].rearrange("p (h t) -> p h t", h=H), ACT.Exp).then_inc(S["decay_exp"], 1)

            def copy_ats(b):
                act.wait_ge(S["a_turned"], b + 1)
                act.activation(Ats[:, b].rearrange("p h t -> p (h t)"), XB[b][:], ACT.Copy).then_inc(S["ats_ready"], 1)

            def copy_x(level, b):
                act.wait_ge(S["x_done"], 2 * level + b + 1)
                if level == len(LEVELS) - 1:
                    act.wait_ge(S["xt64_done"], b + 1)
                act.activation(X[:, b].rearrange("p h t -> p (h t)"), XB[b][:, 0:256], ACT.Copy)\
                    .then_inc(S["x_ready"], 1)

            last_tap(2)
            last_tap(3)
            for e in range(EARLY):
                evac_wp(e)
            silu(2)
            silu(3)
            last_tap(4)
            for i in range(3):
                exp_decay(i)
            last_tap(5)
            last_tap(6)
            for b in range(NBLK):
                copy_ats(b)
            last_tap(7)
            silu(4)
            for level in range(len(LEVELS)):
                for b in range(NBLK):
                    copy_x(level, b)
                if level == 0:
                    last_tap(0)
                    silu(5)
                    silu(6)
                if level == 1:
                    last_tap(1)
                    silu(7)
                if level == 2:
                    silu(0)
                    gate(0)
                if level == 3:
                    silu(1)
                    gate(1)
            for b in range(NBLK):
                act.wait_ge(S["xt64_ready"], b + 1)
                for i in range(2):
                    r = slice(64 * i, 64 * i + 64)
                    ins = act.activation(XTF[r, b, :, r], XT[r, b], ACT.Copy)
                ins.then_inc(S["xtf_diag"], 1)
            act.wait_ge(S["f_done"], 1)
            act.activation(F[:, 0].rearrange("p h v -> p (h v)"), B[7][:], ACT.Copy).then_inc(S["f_ready"], 1)
            evac_wp(2)
            act.wait_ge(S["f_done"], 2)
            act.activation(F[:, 1].rearrange("p h v -> p (h v)"), B[1][:], ACT.Copy).then_inc(S["f_ready"], 1)
            for b in range(NBLK):
                act.wait_ge(S["o_done"], b + 1)
                act.activation(osq[:, b].rearrange("p h v -> p (h v)"), (B[6], B[0])[b][:], ACT.Square)\
                    .then_inc(S["osq_ready"], 1)
            evac_wp(3)
            for b in range(NBLK):
                act.wait_ge(S["oms_ready"], b + 1)
                act.activation(osd[:, b], omv[:, b], ACT.Sqrt).then_inc(S["sd_o"], 1)
            for b in range(NBLK):
                act.wait_ge(S["og_turned"], b + 1)
                act.activation(ogT[:, b].rearrange("p h t -> p (h t)"), (B[7], B[1])[b][:], ACT.Copy,
                               scale=cols[:, O_W:O_W + 1]).then_inc(S["ogt_ready"], 1)
            evac_wp(4)
            evac_wp(5)
            for b in range(NBLK):
                act.wait_ge(S["var_2"], b + 1)
                act.activation(sd2[:, b:b + 1], mv2[:, b, 1:2], ACT.Sqrt, bias=eps[:, 0:1]).then_inc(S["sd_2"], 1)
            evac_wp(6)
            evac_wp(7)
            act.wait_ge(S["h2_turned"], 2)
            act.activation(h2T[:, 1], B[1][:, 0:T], ACT.Copy).then_inc(S["h2t1"], 1)
            for b in range(NBLK):
                act.wait_ge(S["w2_done"], b + 1)
                act.activation(ge[:, b], (B[6], B[0])[b][:, 0:D], ACT.Gelu).then_inc(S["gelu_ready"], 1)
            for b in range(NBLK):
                act.wait_ge(S["var_3"], b + 1)
                act.activation(sd3[:, b:b + 1], mv3[:, b, 1:2], ACT.Sqrt, bias=eps[:, 0:1]).then_inc(S["sd_3"], 1)
            act.wait_ge(S["x3_turned"], 2)
            act.activation(x3T[:, 1], B[1][:, 0:T], ACT.Copy).then_inc(S["x3t1"], 1)
            act.wait_ge(S["lsh_ready"], 1)
            act.activation(pe_[:], lsh[:], ACT.Exp).then_inc(S["pe_ready"], 1)

        @block.tensor
        def _(pe):
            mm = pe.matmul

            def turn(src, banks, ready, done):
                for k in range(2):
                    for b in range(NBLK):
                        if k == 0:
                            pe.wait_ge(S[ready], b + 1)
                        ins = pe.transpose(banks[k][:, b * P:(b + 1) * P], src[:, b, k * P:(k + 1) * P], ident)
                    ins.then_inc(S[done], 1)

            def moe_product(e):
                pe.wait_ge(ld_moe[e // 2], 32)
                if e >= 2:
                    if e >= EARLY + 2:
                        pe.wait_ge(S["wp_ready"], e - 1)
                for m in range(2):
                    for k in range(2):
                        ins = mm(wp_bank[e][:, m * D:(m + 1) * D], wit[:, e, k, m * P:(m + 1) * P], fwo[:, e, k],
                                 start=(k == 0), stop=(k == 1))
                ins.then_inc(S["wp_done"], 1)

            pe.wait_ge(S["ld_consts"], 16)
            pe.wait_ge(S["limbs_summed"], 1)
            mm(small[:, 0:3], C("tri_lt"), lscan[:, :, LCOL - 1], start=True, stop=True).then_inc(S["limb_offsets"], 1)
            turn(xn, (B[0], B[1]), "xn_ready", "x_turned")
            pe.wait_ge(S["cs_ready"], 2)
            mm(B[2][:, 0:D], C("decay")[:, 0:P], cs[:, 0], start=True, stop=True)
            mm(B[2][:, D:2 * D], C("decay")[:, P:2 * P], cs[:, 0], start=True, stop=False)
            mm(B[2][:, D:2 * D], C("decay")[:, 2 * P:3 * P], cs[:, 1], start=False, stop=True).then_inc(S["dep_done"], 1)
            pe.wait_ge(S["xT0"], 1)
            pe.wait_ge(S["xT1"], 1)
            pe.wait_ge(S["ld_win"], 16)
            pe.wait_ge(S["ld_brow"], 16)
            pe.wait_ge(S["ones_set"], 1)
            for b in range(NBLK):
                o = B[3 + b][:, 0:D]
                for k in range(2):
                    mm(o, xT[:, k, b * P:(b + 1) * P], win[:, k], start=(k == 0), stop=False)
                mm(o, ones[0:1, :], brow[0:1, 0], start=False, stop=False)
            pe.wait_ge(S["onehots_ready"], 2)
            for i in range(LCOL):
                ins = mm(small[0:16, 0:16], oh_hi[:, i], oh_lo[:, i], start=(i == 0), stop=(i == LCOL - 1))
            ins.then_inc(S["bound_counts"], 1)
            pe.wait_ge(S["bounds_ready"], 1)
            mm(small[:, 0:T], ones[0:16, :], cumr[:].rearrange("p a b -> p (a b)"), start=True, stop=True)\
                .then_inc(S["cum_rows"], 1)
            pe.wait_ge(S["onehot_t"], 2)
            pe.wait_ge(S["dep_ready"], 1)
            for b in range(NBLK):
                for k in range(2):
                    ins = mm(B[3 + b][:, 0:D], gT[:, k, b * P:(b + 1) * P], dep[:, k], start=False, stop=(k == 1))
                ins.then_inc(S["x1_done"], 1)
            for e in range(EARLY):
                moe_product(e)

            turn(hh, (B[0], B[1]), "hh_ready", "hh_turned")
            pe.wait_ge(S["hT0"], 1)
            pe.wait_ge(S["hT1"], 1)
            pe.wait_ge(S["ld_wcat"], 16)
            for b in range(NBLK):
                for k in range(2):
                    ins = mm(small[:, 8 * b:8 * b + 8], hT[:, k, b * P:(b + 1) * P], wcat[:, k, ABC:ABC + 8],
                             start=(k == 0), stop=(k == 1))
            ins.then_inc(S["ab_done"], 1)

            def project(tile):
                n = order[tile]
                if n >= 3:
                    pe.wait_ge(S["conv_done"], n - 2)
                for k in range(2):
                    c = tile_col[tile]
                    ins = mm(tile_bank[tile][:, 0:T], wcat[:, k, c:c + P], hT[:, k], start=(k == 0), stop=(k == 1))
                ins.then_inc(S["tile_done"], 1)

            def project_gate(b):
                pe.wait_ge(S["conv_done"], 6 + b)
                for k in range(2):
                    ins = mm(gate_bank[b][:], hT[:, k, b * P:(b + 1) * P], wcat[:, k, GC:GC + H * VD],
                             start=(k == 0), stop=(k == 1))
                ins.then_inc(S["tile_done"], 1)

            project(2)
            project(3)
            project(4)
            pe.wait_ge(S["g_masked"], 1)
            mm(B[0][:], C("tri_gt"), gM[:, 0].rearrange("p h t -> p (h t)"), start=True, stop=True)\
                .then_inc(S["decay_mm"], 1)
            mm(B[1][:], C("tri_gt"), g[:, 0].unsqueeze(2).broadcast_to([P, H, P]), start=True, stop=False)
            pe.wait_ge(S["g_masked"], 2)
            mm(B[1][:], ones[:], gM[:, 1].rearrange("p h t -> p (h t)"), start=False, stop=True)\
                .then_inc(S["decay_mm"], 1)
            pe.wait_ge(S["wp_ready"], 1)
            mm(B[6][:], C("tri_gt"), gM[:, 1].rearrange("p h t -> p (h t)"), start=True, stop=True)\
                .then_inc(S["decay_mm"], 1)

            def squares(sq, col):
                for b in range(NBLK):
                    for i in range(2):
                        at = col + H * b + 2 * i
                        ins = mm(small[:, at:at + 2], sq[:, i, b * P:(b + 1) * P], C("headones"), start=True, stop=True)
                ins.then_inc(S["ss_done"], 1)

            def gram(a0, banks, done, ready):
                for blk in range(NBLK):
                    for odd in range(2):
                        ready(blk, odd)
                        r = slice(64 * odd, 64 * odd + 64)
                        width = T - blk * P
                        for i in range(2):
                            ins = mm(banks[2 * blk + odd][:, i * width:(i + 1) * width],
                                     sv[r, 2 + i, blk * P:(blk + 1) * P], sv[r, a0 + i, blk * P:T],
                                     start=True, stop=True)
                        ins.then_inc(S[done], 1)

            pe.wait_ge(S["ksq_ready"], 2)
            squares(ksq, 16)

            def kk_ready(blk, odd):
                if (blk, odd) == (0, 0):
                    pe.wait_ge(S["wp_ready"], 2)
                else:
                    pe.wait_ge(S["decay_exp"], 2 * blk + odd)

            gram(2, kk_bank, "kk_done", kk_ready)
            project(5)
            project(6)
            for b in range(NBLK):
                pe.wait_ge(S["at_ready"], 4 * (b + 1))
                for h in range(H):
                    src = AT1[:, h, 0:P] if b == 0 else AT2[:, h]
                    ins = pe.transpose(XB[b][:, h * P:(h + 1) * P], src, ident)
                ins.then_inc(S["a_turned"], 1)
            project(7)
            for b in range(NBLK):
                pe.wait_ge(S["ats_ready"], b + 1)
                pe.wait_ge(S["x_base"], b + 1)
                mm(XB[b][:, 0:256], ident, X[:, b].rearrange("p h t -> p (h t)"), start=True, stop=True,
                   skip_group_check=True)

            def tiles64(b, fn):
                for h in range(H):
                    for i in range(2):
                        ins = fn(h, slice(64 * i, 64 * i + 64))
                return ins

            def double_u(level, b):
                if level == 0:
                    pe.wait_ge(S["xt_base"], b + 1)
                else:
                    pe.wait_ge(S["xt_ready"], 2 * (level - 1) + b + 1)
                tiles64(b, lambda h, r: mm(UB[b][r, 64 * h:64 * h + 64], Ats[r, b, h, r], XT[r, b, h],
                                           start=True, stop=True)).then_inc(S["u_done"], 1)

            def double_x(level, b):
                pe.wait_ge(S["u_ready"], 2 * level + b + 1)
                tiles64(b, lambda h, r: mm(XB[b][r, 64 * h:64 * h + 64], U[r, b, h], X[r, b, h],
                                           start=False, stop=True, skip_group_check=True))\
                    .then_inc(S["x_done"], 1)

            for level in range(len(LEVELS)):
                for b in range(NBLK):
                    double_u(level, b)
                if level == 0:
                    project(0)
                if level == 1:
                    project(1)
                if level == 2:
                    project_gate(0)
                if level == 3:
                    project_gate(1)
                for b in range(NBLK):
                    double_x(level, b)
                    if level == len(LEVELS) - 1:
                        tiles64(b, lambda h, r: mm(UB[b][r, 256 + 64 * h:256 + 64 * h + 64], X[r, b, h], U[r, b, h],
                                                   start=True, stop=True)).then_inc(S["xt64_done"], 1)
            for b in range(NBLK):
                pe.wait_ge(S["xt64_ready"], b + 1)
                for h in range(H):
                    ins = mm(UB[b][0:64, 64 * h:64 * h + 64], Ats[64:P, b, h, 0:64], XT[64:P, b, h],
                             start=True, stop=True)
                ins.then_inc(S["u128_done"], 1)
            pe.wait_ge(S["qsq_ready"], 2)
            squares(qsq, 24)
            for b in range(NBLK):
                pe.wait_ge(S["u128_ready"], b + 1)
                pe.wait_ge(S["x_ready"], 2 * len(LEVELS) - 1 + b)
                for h in range(H):
                    ins = mm(UB[b][0:64, 256 + 64 * h:256 + 64 * h + 64], X[0:64, b, h], U128[:, b, h],
                             start=True, stop=True)
                ins.then_inc(S["xt128_done"], 1)
            pe.wait_ge(S["silu_done"], order[7] + 1)
            pe.wait_ge(S["conv_done"], 8)
            pe.wait_ge(S["gate_done"], 2)
            for b in range(NBLK):
                for h in range(H):
                    ins = pe.transpose(B[3 + b][:, h * P:(h + 1) * P], sv[:, 4 + h, b * P:(b + 1) * P], ident)
                ins.then_inc(S["v_turned"], 1)
            pe.wait_ge(S["silu_done"], order[1] + 1)

            def qk_ready(blk, odd):
                if (blk, odd) == (0, 1) or (blk, odd) == (1, 0):
                    pe.wait_ge(S["vp_ready"], 1 + blk)
                if (blk, odd) == (1, 1):
                    pe.wait_ge(S["qe_ready"], 1)

            gram(0, qk_bank, "qk_done", qk_ready)

            def heads(bank, lhs, rhs, start=True, stop=True):
                for h in range(H):
                    ins = mm(bank[:, h * VD:(h + 1) * VD], lhs(h), rhs[:, h], start=start, stop=stop,
                             skip_group_check=True)
                return ins

            pe.wait_ge(S["xt128_ready"], 1)
            pe.wait_ge(S["xtf_diag"], 1)
            pe.wait_ge(S["x_ready"], 2 * len(LEVELS))
            heads(B[7], lambda h: XTF[:, 0, h], vp[:, 0]).then_inc(S["f_done"], 1)
            pe.wait_ge(S["f_ready"], 1)
            heads(B[0], lambda h: AT1[:, h, P:T], F[:, 0]).then_inc(S["r_done"], 1)
            pe.wait_ge(S["pt_ready"], 8)
            pe.wait_ge(S["xt128_ready"], 2)
            heads(B[6], lambda h: PT1[:, h, 0:P], F[:, 0]).then_inc(S["o_done"], 1)
            pe.wait_ge(S["r_ready"], 1)
            pe.wait_ge(S["xtf_diag"], 2)
            heads(B[1], lambda h: XTF[:, 1, h], R2).then_inc(S["f_done"], 1)
            moe_product(2)
            pe.wait_ge(S["f_ready"], 2)
            for h in range(H):
                o = B[0][:, h * VD:(h + 1) * VD]
                mm(o, PT1[:, h, P:T], F[:, 0, h], start=True, stop=False, skip_group_check=True)
                ins = mm(o, PT2[:, h], F[:, 1, h], start=False, stop=True, skip_group_check=True)
            ins.then_inc(S["o_done"], 1)
            moe_product(3)
            for b in range(NBLK):
                pe.wait_ge(S["og_ready"], 4 * (b + 1))
                for h in range(H):
                    ins = pe.transpose((B[7], B[1])[b][:, h * P:(h + 1) * P], og[:, b, h], ident)
                ins.then_inc(S["og_turned"], 1)
            pe.wait_ge(S["ld_wo"], 16)
            for b in range(NBLK):
                pe.wait_ge(S["ogt_ready"], b + 1)
                for h in range(H):
                    ins = mm((B[6], B[0])[b][:, 0:D], ogT[:, b, h], wo[:, h], start=(h == 0), stop=(h == H - 1))
                ins.then_inc(S["enc_done"], 1)
            for e in range(4, 8):
                moe_product(e)
            turn(h2, (B[7], B[1]), "h2_ready", "h2_turned")
            pe.wait_ge(S["ld_w2"], 16)
            pe.wait_ge(S["h2t0"], 1)
            pe.wait_ge(S["h2t1"], 1)
            for b in range(NBLK):
                o = (B[6], B[0])[b][:, 0:D]
                for k in range(2):
                    mm(o, h2T[:, k, b * P:(b + 1) * P], w2[:, k], start=(k == 0), stop=False)
                mm(o, ones[0:1, :], brow[0:1, 1], start=False, stop=True).then_inc(S["w2_done"], 1)

            turn(x3, (B[7], B[1]), "x3_ready", "x3_turned")
            pe.wait_ge(S["ld_wr"], 16)
            pe.wait_ge(S["x3t0"], 1)
            pe.wait_ge(S["x3t1"], 1)
            for b in range(NBLK):
                for k in range(2):
                    ins = mm(small[:, 8 * b:8 * b + 8], x3T[:, k, b * P:(b + 1) * P], wr[:, k],
                             start=(k == 0), stop=(k == 1))
            ins.then_inc(S["logits_done"], 1)
            pe.wait_ge(S["wp_ready"], 8)
            n = 0
            for b in range(NBLK):
                for pair in range(E // 2):
                    bank = moe_bank[n % 4]
                    if n >= 4:
                        pe.wait_ge(S["moe_used"], 2 * (n - 3))
                    for k in range(2):
                        ins = mm(bank[:], x3T[:, k, b * P:(b + 1) * P],
                                 wp[:, k, 2 * pair:2 * pair + 2].rearrange("p e d -> p (e d)"),
                                 start=(k == 0), stop=(k == 1))
                    ins.then_inc(S["moe_done"], 1)
                    n += 1

        @block.vector
        def _(dve):
            n = [0]

            def mark(ins):
                ins.then_inc(S["dve_step"], 1)
                n[0] += 1
                return n[0]

            def need(k):
                dve.wait_ge(S["dve_step"], k)

            def link(ins):
                need(mark(ins))

            ts, tt, stt = dve.tensor_scalar, dve.tensor_tensor, dve.scalar_tensor_tensor

            dve.wait_ge(S["ld_x"], 16)
            for b in range(NBLK):
                k = mark(dve.bn_stats(st[:, b], x_in[:, b]))
            need(k)
            dve.bn_aggr(mv[:, 0], st[:, 0])
            dve.bn_aggr(mv[:, 1], st[:, 1]).then_inc(S["var_a"], 1)
            dve.wait_ge(S["ld_lens"], 16)
            ts(limb[:, 0], lens_in[:], 2047, None, ALU.bitwise_and)
            ts(limb[:, 1], lens_in[:], 11, 2047, ALU.logical_shift_right, ALU.bitwise_and)
            k = mark(ts(limb[:, 2], lens_in[:], 22, 1023, ALU.logical_shift_right, ALU.bitwise_and))
            dve.wait_ge(S["ld_consts"], 16)
            need(k)
            dve.tensor_tensor_scan(lscan[:].rearrange("p l c -> p (l c)"), C("reset"),
                                   limb[:].rearrange("p l c -> p (l c)"), 0.0, ALU.mult, ALU.add)\
                .then_inc(S["limbs_summed"], 1)
            dve.wait_ge(S["sd_a"], 1)
            link(dve.reciprocal(rstd[:], sd[:]))
            dve.wait_ge(S["var_a"], 1)
            for b in range(NBLK):
                ts(xn[:, b], x_in[:, b], mv[:, b, 0:1], rstd[:, b:b + 1], ALU.subtract, ALU.mult)\
                    .then_inc(S["xn_ready"], 1)
            dve.wait_ge(S["limb_offsets"], 1)
            dve.wait_ge(S["limbs_summed"], 1)
            link(tt(csum[:], lscan[:], small[:, 0:3].unsqueeze(2).broadcast_to([P, 3, LCOL]), ALU.add))
            ts(lo0[:], csum[:, 0], 2047, None, ALU.bitwise_and)
            link(ts(ca0[:], csum[:, 0], 11, None, ALU.logical_shift_right))
            link(tt(s1_[:], csum[:, 1], ca0[:], ALU.add))
            dve.wait_ge(S["x_turned"], 1)
            dve.wait_ge(S["ld_cols"], 16)
            ts(xT[:, 0], B[0][:, 0:T], cols[:, G_RES:G_RES + 1], None, ALU.mult).then_inc(S["xT0"], 1)
            ts(lo1[:], s1_[:], 2047, None, ALU.bitwise_and)
            link(ts(ca1[:], s1_[:], 11, None, ALU.logical_shift_right))
            link(tt(s2_[:], csum[:, 2], ca1[:], ALU.add))
            link(ts(lo2[:], s2_[:], 1023, None, ALU.bitwise_and))
            link(ts(tf[:, 0], lo2[:], 512.0, -1024.0, ALU.is_ge, ALU.mult))
            link(tt(tf[:, 1], tf[:, 0], lo2[:], ALU.add))
            link(stt(tf[:, 2], tf[:, 1], 2048.0, lo1[:], ALU.mult, ALU.add))
            link(stt(tf[:, 3], tf[:, 2], 2048.0, lo0[:], ALU.mult, ALU.add))
            link(ts(tf[:, 4], tf[:, 3], 0.0, float(T), ALU.is_le, ALU.mult))
            link(stt(tf[:, 0], tf[:, 3], -1.0, tf[:, 4], ALU.add, ALU.add))
            link(ts(pos[:], tf[:, 0], float(2 * T), -1.0, ALU.min, ALU.max))
            ts(pos_hi[:], pos[:], 4, None, ALU.arith_shift_right)
            link(ts(pos_lo[:], pos[:], 15, None, ALU.bitwise_and))
            for oh, p_ in ((oh_hi, pos_hi), (oh_lo, pos_lo)):
                tt(oh[:], p_[:].unsqueeze(2).broadcast_to([P, LCOL, 16]),
                   C("iota16").unsqueeze(1).broadcast_to([P, LCOL, 16]), ALU.is_equal).then_inc(S["onehots_ready"], 1)
            dve.wait_ge(S["sd_ctx"], 1)
            link(dve.reciprocal(crs[:], csd[:]))
            for b in range(NBLK):
                ts(cs[:, b], ctx_in[:, b, 0:D], crs[:, b:b + 1], None, ALU.mult).then_inc(S["cs_ready"], 1)
            dve.wait_ge(S["bound_counts"], 1)
            link(ts(bound[:], small[0:16, 0:16], 1.0, None, ALU.min))
            dve.wait_ge(S["ones_set"], 1)
            link(dve.tensor_tensor_scan(bscan[:], ones[0:16, 0:16], bound[:], 0.0, ALU.mult, ALU.add))
            link(tt(prer[:], bscan[:].unsqueeze(1).broadcast_to([16, 16, 16]),
                    C("mask_d", 16).unsqueeze(2).broadcast_to([16, 16, 16]), ALU.mult))
            stt(cumr[:], C("mask_lt", 16).unsqueeze(2).broadcast_to([16, 16, 16]), bscan[:, 15:16], prer[:],
                ALU.mult, ALU.add).then_inc(S["bounds_ready"], 1)
            dve.wait_ge(S["dep_done"], 1)
            dve.wait_ge(S["ld_rows"], 16)
            tt(dep[:], B[2][:].rearrange("p (b d) -> p b d", b=2),
               rows[:, R_GINIT:R_GINIT + D].unsqueeze(1).broadcast_to([P, 2, D]), ALU.mult).then_inc(S["dep_ready"], 1)
            dve.wait_ge(S["cum_rows"], 1)
            for k in range(2):
                ts(gT[:, k], small[:, 0:T], 1.0, C("scol")[:, k:k + 1], ALU.max, ALU.is_equal)\
                    .then_inc(S["onehot_t"], 1)
            for b in range(NBLK):
                dve.wait_ge(S["x1_done"], b + 1)
                tt(x1[:, b], B[3 + b][:, 0:D], x_in[:, b], ALU.add).then_inc(S["x1_ready"], 1)
                dve.wait_ge(S["x1_ready"], b + 1)
                k = mark(dve.bn_stats(st1[:, b], x1[:, b]))
            need(k)
            dve.bn_aggr(mv1[:, 0], st1[:, 0])
            dve.bn_aggr(mv1[:, 1], st1[:, 1]).then_inc(S["var_1"], 1)
            dve.wait_ge(S["var_1"], 1)
            for b in range(NBLK):
                k = mark(stt(z0[:, b], x1[:, b], mv1[:, b, 0:1], rows[:, R_LN1G:R_LN1G + D], ALU.subtract, ALU.mult))
            dve.wait_ge(S["sd_b"], 2)
            k2 = mark(dve.reciprocal(rs1[:], sd1[:]))
            need(k2)
            for b in range(NBLK):
                stt(z[:, b], z0[:, b], rs1[:, 1, b:b + 1], rows[:, R_LN1B:R_LN1B + D], ALU.mult, ALU.add)\
                    .then_inc(S["z_ready"], 1)
            for b in range(NBLK):
                ts(y[:, b], x1[:, b], mv1[:, b, 0:1], rs1[:, 0, b:b + 1], ALU.subtract, ALU.mult)
            dve.wait_ge(S["sd_z"], 1)
            link(dve.reciprocal(zrs[:], zsd[:]))
            dve.wait_ge(S["z_ready"], 2)
            for b in range(NBLK):
                ts(hh[:, b], z[:, b], zrs[:, b:b + 1], None, ALU.mult).then_inc(S["hh_ready"], 1)
            dve.wait_ge(S["hh_turned"], 1)
            ts(hT[:, 0], B[0][:, 0:T], cols[:, RMS_W:RMS_W + 1], None, ALU.mult).then_inc(S["hT0"], 1)
            dve.wait_ge(S["ab_done"], 1)
            ab = small[:, 0:16].rearrange("p (b c) -> p b c", b=NBLK)
            ts(ea[:, :, H:2 * H], ab[:, :, H:2 * H], -1.0, None, ALU.mult)
            link(tt(xa[:], ab[:, :, 0:H], rows[:, R_DTB:R_DTB + H].unsqueeze(1).broadcast_to([P, NBLK, H]), ALU.add))
            link(ts(nx[:], xa[:], -1.0, None, ALU.mult))
            tt(ea[:, :, 0:H], xa[:], nx[:], ALU.min).then_inc(S["ea_ready"], 1)
            dve.wait_ge(S["exp_a"], 1)
            link(ts(sp[:, 0], ex[:, :, 0:H], 2.0, None, ALU.add))
            link(dve.reciprocal(sp[:, 1], sp[:, 0]))
            link(tt(sp[:, 2], ex[:, :, 0:H], sp[:, 1], ALU.mult))
            link(tt(sp[:, 3], sp[:, 2], sp[:, 2], ALU.mult))
            link(ts(poly[:, 0], sp[:, 3], ATANH[0], None, ALU.mult))
            for i, c in enumerate(ATANH[1:]):
                link(stt(poly[:, i + 1], poly[:, i], c, sp[:, 3], ALU.add, ALU.mult))
            link(stt(poly[:, 7], poly[:, 6], 1.0, sp[:, 2], ALU.add, ALU.mult))
            link(ts(sp[:, 4], xa[:], 0.0, None, ALU.max))
            link(stt(sp[:, 5], poly[:, 7], 2.0, sp[:, 4], ALU.mult, ALU.add))
            dve.wait_ge(S["expA_ready"], 1)
            link(stt(g[:], sp[:, 5], -1.0, expA[:].unsqueeze(1).broadcast_to([P, NBLK, H]), ALU.mult, ALU.mult))
            for b in range(NBLK):
                tt(gM[:, b], C("tri_le").unsqueeze(1).broadcast_to([P, H, P]),
                   g[:, b].unsqueeze(2).broadcast_to([P, H, P]), ALU.mult).then_inc(S["g_masked"], 1)

            def conv(tile):
                dve.wait_ge(S["tap_last"], order[tile] + 1)
                x_ = tile_bank[tile]
                for lag in range(1, TAPS):
                    c = CONV + TAPS * tile + TAPS - 1 - lag
                    ins = stt(cv[:, tile, lag:T], x_[:, 0:T - lag], cols[:, c:c + 1], cv[:, tile, lag:T],
                              ALU.mult, ALU.add)
                    if lag < TAPS - 1:
                        link(ins)
                ins.then_inc(S["conv_done"], 1)

            conv(2)
            conv(3)
            for i in range(2):
                dve.wait_ge(S["silu_done"], i + 1)
                tt(ksq[:, i], sv[:, 2 + i], sv[:, 2 + i], ALU.mult).then_inc(S["ksq_ready"], 1)
            dve.wait_ge(S["ss_done"], 1)
            ts(kse[:], small[:, 16:24].rearrange("p (b h) -> p b h", b=NBLK), QK_EPS, None, ALU.add)\
                .then_inc(S["kse_ready"], 1)
            dve.wait_ge(S["kse_ready"], 1)
            link(stt(cden[:], ex[:, :, H:2 * H], 1.0, kse[:], ALU.add, ALU.mult))
            link(dve.reciprocal(cfac[:], cden[:]))

            def scale_gram(banks, done, o1, o2, ready, e_ready):
                for blk in range(NBLK):
                    width = T - blk * P
                    e_ready(blk)
                    for odd in range(2):
                        dve.wait_ge(S[done], 2 * blk + odd + 1)
                        for i in range(2):
                            h = 2 * i + odd
                            o, e = (o1, E1) if blk == 0 else (o2, E2)
                            stt(o[:, h], banks[2 * blk + odd][:, i * width:(i + 1) * width],
                                cfac[:, blk, h:h + 1], e[:, h], ALU.mult, ALU.mult).then_inc(S[ready], 1)

            scale_gram(kk_bank, "kk_done", AT1, AT2, "at_ready",
                       lambda blk: dve.wait_ge(S["decay_exp"], 2 + blk))
            lv = CONST["levels"][0]

            def level_mask(i, r=slice(0, P)):
                return consts[r, lv + 64 * i:lv + 64 * i + 64].unsqueeze(1).broadcast_to([r.stop - r.start, H, 64])

            for b in range(NBLK):
                dve.wait_ge(S["at_ready"], 4 * (b + 1))
                for i in range(2):
                    r = slice(64 * i, 64 * i + 64)
                    src = AT1[r, :, r] if b == 0 else AT2[r, :, r]
                    k = mark(tt(U[r, b], src, level_mask(0, r), ALU.mult))
                need(k)
                tt(XT[:, b], U[:, b], C("ident64").unsqueeze(1).broadcast_to([P, H, 64]), ALU.add)\
                    .then_inc(S["xt_base"], 1)
                dve.wait_ge(S["xt_base"], b + 1)
                dve.transpose(X[:, b].rearrange("p h t -> p (h t)"),
                              XT[:, b].rearrange("p h t -> p (h t)")).then_inc(S["x_base"], 1)
            conv(4)

            for level in range(len(LEVELS)):
                last = level == len(LEVELS) - 1
                for b in range(NBLK):
                    dve.wait_ge(S["u_done"], 2 * level + b + 1)
                    if level >= 1:
                        dve.wait_ge(S["x_done"], 2 * (level - 1) + b + 1)
                    else:
                        dve.wait_ge(S["x_base"], b + 1)
                    tt(U[:, b], UB[b][:, 0:256].rearrange("p (h t) -> p h t", h=H), level_mask(level + 1), ALU.mult)\
                        .then_inc(S["u_ready"], 1)
                if level == 0:
                    conv(5)
                    conv(6)
                if level == 1:
                    conv(7)
                if level == 2:
                    conv(0)
                if level == 3:
                    conv(1)
                for b in range(NBLK):
                    if not last:
                        dve.wait_ge(S["x_ready"], 2 * level + b + 1)
                        dve.transpose(XT[:, b].rearrange("p h t -> p (h t)"),
                                      X[:, b].rearrange("p h t -> p (h t)")).then_inc(S["xt_ready"], 1)
                    else:
                        dve.wait_ge(S["xt64_done"], b + 1)
                        for i in range(2):
                            r = slice(64 * i, 64 * i + 32)
                            ins = dve.tensor_copy(XT[r, b, :, 32:64],
                                                  UB[b][r, 256:512].rearrange("p (h t) -> p h t", h=H)[:, :, 32:64])
                        ins.then_inc(S["xt64_ready"], 1)
            for b in range(NBLK):
                dve.memset(XTF[64:P, b, :, 0:64], 0.0)
            for b in range(NBLK):
                dve.wait_ge(S["u128_done"], b + 1)
                ts(U128[:, b], UB[b][0:64, 0:256].rearrange("p (h t) -> p h t", h=H), -1.0, None, ALU.mult)\
                    .then_inc(S["u128_ready"], 1)
            for b in range(NBLK):
                dve.wait_ge(S["xt128_done"], b + 1)
                dve.tensor_copy(XTF[0:64, b, :, 64:P], UB[b][0:64, 256:512].rearrange("p (h t) -> p h t", h=H))\
                    .then_inc(S["xt128_ready"], 1)
            dve.wait_ge(S["ksr_ready"], 1)
            for b in range(NBLK):
                dve.wait_ge(S["v_turned"], b + 1)
                tt(vp[:, b], B[3 + b][:].rearrange("p (h v) -> p h v", h=H),
                   ksr[:, b].unsqueeze(2).broadcast_to([P, H, VD]), ALU.mult).then_inc(S["vp_ready"], 1)
            dve.wait_ge(S["ss_done"], 2)
            ts(qe[:], small[:, 24:32].rearrange("p (b h) -> p b h", b=NBLK), QK_EPS, QK_EPS * KD, ALU.add, ALU.mult)\
                .then_inc(S["qe_ready"], 1)
            scale_gram(qk_bank, "qk_done", PT1, PT2, "pt_ready",
                       lambda blk: dve.wait_ge(S["masked_e"], 1 + blk))
            dve.wait_ge(S["r_done"], 1)
            dve.wait_ge(S["vp_ready"], 2)
            tt(R2[:], vp[:, 1], B[0][:].rearrange("p (h v) -> p h v", h=H), ALU.subtract).then_inc(S["r_ready"], 1)
            dve.wait_ge(S["qe_ready"], 1)
            for b in range(NBLK):
                dve.wait_ge(S["osq_ready"], b + 1)
                link(dve.tensor_reduce(oms[:, b], osq[:, b], AX.X, ALU.add))
                stt(omv[:, b], oms[:, b], 1.0 / VD, qe[:, b], ALU.mult, ALU.add).then_inc(S["oms_ready"], 1)
            for b in range(NBLK):
                dve.wait_ge(S["sd_o"], b + 1)
                link(dve.reciprocal(ors[:, b], osd[:, b]))
                dve.wait_ge(S["gate_done"], 2)
                for h in range(H):
                    stt(og[:, b, h], (B[6], B[0])[b][:, h * VD:(h + 1) * VD], ors[:, b, h:h + 1], sg[:, b, h],
                        ALU.mult, ALU.mult).then_inc(S["og_ready"], 1)
            for b in range(NBLK):
                dve.wait_ge(S["enc_done"], b + 1)
                tt(w[:, b], (B[6], B[0])[b][:, 0:D], y[:, b], ALU.add).then_inc(S["w_ready"], 1)
                dve.wait_ge(S["w_ready"], b + 1)
                link(dve.bn_stats(st2[:, b], w[:, b]))
                dve.bn_aggr(mv2[:, b], st2[:, b]).then_inc(S["var_2"], 1)
            for b in range(NBLK):
                dve.wait_ge(S["var_2"], b + 1)
                k = mark(stt(h0[:, b], w[:, b], mv2[:, b, 0:1], rows[:, R_LN2G:R_LN2G + D], ALU.subtract, ALU.mult))
                dve.wait_ge(S["sd_2"], b + 1)
                link(dve.reciprocal(rs2[:, b:b + 1], sd2[:, b:b + 1]))
                stt(h2[:, b], h0[:, b], rs2[:, b:b + 1], rows[:, R_LN2B:R_LN2B + D], ALU.mult, ALU.add)\
                    .then_inc(S["h2_ready"], 1)
            for b in range(NBLK):
                k = mark(tt(base[:, b], w[:, b], x1[:, b], ALU.add))
            dve.wait_ge(S["h2_turned"], 1)
            dve.tensor_copy(h2T[:, 0], B[7][:, 0:T]).then_inc(S["h2t0"], 1)
            need(k)
            for b in range(NBLK):
                dve.wait_ge(S["gelu_ready"], b + 1)
                tt(x2[:, b], ge[:, b], base[:, b], ALU.add).then_inc(S["x2_ready"], 1)
                dve.wait_ge(S["x2_ready"], b + 1)
                link(dve.bn_stats(st3[:, b], x2[:, b]))
                dve.bn_aggr(mv3[:, b], st3[:, b]).then_inc(S["var_3"], 1)
            for b in range(NBLK):
                dve.wait_ge(S["var_3"], b + 1)
                dve.wait_ge(S["sd_3"], b + 1)
                link(dve.reciprocal(rs3[:, b:b + 1], sd3[:, b:b + 1]))
                ts(x3[:, b], x2[:, b], mv3[:, b, 0:1], rs3[:, b:b + 1], ALU.subtract, ALU.mult)\
                    .then_inc(S["x3_ready"], 1)
            dve.wait_ge(S["x3_turned"], 1)
            dve.tensor_copy(x3T[:, 0], B[7][:, 0:T]).then_inc(S["x3t0"], 1)

            def over(a):
                return a.unsqueeze(2).broadcast_to([P, NBLK, E])

            dve.wait_ge(S["logits_done"], 1)
            lg = small[:, 0:16].rearrange("p (b e) -> p b e", b=NBLK)
            link(dve.tensor_reduce(lmax[:], lg, AX.X, ALU.max))
            tt(lsh[:], lg, over(lmax[:]), ALU.subtract).then_inc(S["lsh_ready"], 1)
            dve.wait_ge(S["pe_ready"], 1)
            k = mark(dve.tensor_reduce(psum_[:], pe_[:], AX.X, ALU.add))
            src = pe_
            for i in range(2):
                link(dve.tensor_reduce(top[:, i], src[:], AX.X, ALU.max))
                link(tt(eqm[:, i], src[:], over(top[:, i]), ALU.is_equal))
                link(tt(scr[:, i], eqm[:, i], C("idxdesc").unsqueeze(1).broadcast_to([P, NBLK, E]), ALU.mult))
                link(dve.tensor_reduce(first[:, i], scr[:, i], AX.X, ALU.max))
                link(tt(hot[:, i], scr[:, i], over(first[:, i]), ALU.is_equal))
                if i == 0:
                    link(stt(rest[:], hot[:, 0], -2.0, pe_[:], ALU.mult, ALU.add))
                    src = rest
            link(dve.reciprocal(prec[:], psum_[:]))
            link(tt(both[:], hot[:, 0], hot[:, 1], ALU.add))
            link(tt(wgt0[:], both[:], pe_[:], ALU.mult))
            link(tt(wgt[:], wgt0[:], over(prec[:]), ALU.mult))
            m = 0
            for b in range(NBLK):
                for pair in range(E // 2):
                    bank = moe_bank[m % 4]
                    dve.wait_ge(S["moe_done"], m + 1)
                    for i in range(2):
                        e = 2 * pair + i
                        if e > 0:
                            dve.wait_ge(S["moe_used"], E * b + e)
                        ins = stt(acc[:, b], bank[:, i * D:(i + 1) * D], wgt[:, b, e:e + 1],
                                  x2[:, b] if e == 0 else acc[:, b], ALU.mult, ALU.add)
                        ins.then_inc(S["moe_used"], 1)
                    m += 1
                dve.wait_ge(S["moe_used"], E * (b + 1))
                dve.nop().then_inc(S["out_ready"], 1)


def kernel(**inputs):
    import numpy as _np
    import concourse.bacc as _bacc
    from concourse import mybir as _mybir
    from concourse.bass_utils import run_bass_kernel_spmd as _run

    a = {k: _np.asarray(v) for k, v in inputs.items()}

    def tiles(m, n):
        return _np.ascontiguousarray(m.reshape(n, P, -1).transpose(1, 0, 2))

    def columns(v, n):
        return v.reshape(n, P).T

    def taps(m, n):
        return m.reshape(n, P, TAPS).transpose(1, 0, 2).reshape(P, n * TAPS)

    arrays = {
        "x": a["x"].reshape(T, D),
        "ctx": _np.ascontiguousarray(a["ctx_2048"].reshape(-1, CTXD)[:T]),
        "lens": a["mask_BxS2_if0"].reshape(LENS),
        "consts": shape_constants(),
        "cols": _np.ascontiguousarray(_np.concatenate([
            columns(a["L0_xattn_g_res"], 2), columns(a["L0_attn_rms_in_w"], 2), columns(a["L0_attn_o_norm_w"], 1),
            taps(a["L0_attn_conv_q_w"], 2), taps(a["L0_attn_conv_k_w"], 2), taps(a["L0_attn_conv_v_w"], 4)], 1)),
        "rows": _np.concatenate([a["L0_xattn_g_init"][:D], a["L0_attn_ln1_g"], a["L0_attn_ln1_b"],
                                 a["L0_attn_ln2_g"], a["L0_attn_ln2_b"], a["L0_attn_dt_bias"], a["L0_attn_A_log"]]),
        "brow": _np.stack([a["L0_xattn_b_in"], a["L0_attn_b2"]])[None],
        "win": tiles(a["L0_xattn_W_in"].T, 2),
        "wcat": tiles(_np.concatenate([a["L0_attn_Wq"], a["L0_attn_Wk"], a["L0_attn_Wv"], a["L0_attn_Wg"],
                                       a["L0_attn_Wa"], a["L0_attn_Wb"]], 1), 2),
        "wo": tiles(a["L0_attn_Wo"], H),
        "w2": tiles(a["L0_attn_W2"], 2),
        "wr": tiles(a["L0_ffn_Wr"], 2),
        "wit": _np.ascontiguousarray(a["L0_ffn_Wi"].reshape(E, D, 2, P).transpose(3, 0, 2, 1)),
        "fwo": _np.ascontiguousarray(a["L0_ffn_Wo"].reshape(E, 2, P, D).transpose(2, 0, 1, 3)),
    }
    nc = _bacc.Bacc("TRN2", target_bir_lowering=False, num_devices=1)
    args = [nc.dram_tensor(f"in_{k}", v.shape, _mybir.dt.from_np(v.dtype), kind="ExternalInput").ap()
            for k, v in arrays.items()]
    args.append(nc.dram_tensor("out_0", (T, D), _mybir.dt.float32, kind="ExternalOutput").ap())
    program(nc, *args)
    r = _run(nc, [{f"in_{k}": v for k, v in arrays.items()}], core_ids=[0])
    return r.results[0]["out_0"].reshape(1, T, D)
```

```python
import concourse.bass as bass
from concourse import mybir
from contextlib import ExitStack
import numpy as np

T, D, P = 256, 256, 128
H, KD, VD, TAPS = 4, 64, 128, 4
E, LENS, CTXD = 8, 4096, 512
NBLK = T // P
LCOL = LENS // P
LN_EPS, RMS_EPS, QK_EPS = 1e-5, 1e-5, 1e-6
QC, KC, VC, GC, ABC, WCOLS = 0, 256, 512, 1024, 1536, 1544
LEVELS = (2, 4, 8, 16, 32)
ATANH = (1 / 15, 1 / 13, 1 / 11, 1 / 9, 1 / 7, 1 / 5, 1 / 3)

CONST = {}
_at = 0
for _name, _width in (("reset", 3 * LCOL), ("tri_lt", P), ("ident", P), ("iota16", 16), ("scol", 2),
                      ("mask_d", 16), ("mask_lt", 16), ("idxdesc", E), ("headones", 2),
                      ("decay", 3 * P), ("tri_le", P), ("tri_gt", P),
                      ("levels", 64 * (1 + len(LEVELS))), ("ident64", 64)):
    CONST[_name] = (_at, _at + _width)
    _at += _width
NFIRST = CONST["decay"][0]
NCONST = _at
G_RES, RMS_W, O_W, CONV, NCOLS = 0, 2, 4, 5, 5 + 8 * TAPS
R_GINIT, R_LN1G, R_LN1B, R_LN2G, R_LN2B, R_DTB, R_ALOG, NROWS = 0, 256, 512, 768, 1024, 1280, 1284, 1288


def shape_constants():
    c = np.zeros((P, NCONST), np.float32)

    def put(name, a):
        c[:a.shape[0], CONST[name][0]:CONST[name][1]] = a

    i = np.arange(P)
    put("ident", np.eye(P))
    put("tri_le", i[:, None] <= i[None])
    put("tri_gt", i[:, None] > i[None])
    put("tri_lt", i[:, None] < i[None])
    a, b = -np.expm1(-0.001), np.exp(-0.001)
    t = np.arange(T)
    lag = t[None, :] - t[:, None]
    L = np.where(lag >= 0, b * a ** np.maximum(lag, 0), 0.0)
    put("decay", np.concatenate([L[:P, :P], L[:P, P:], L[P:, P:]], 1))
    j = np.arange(64)
    masks = []
    for m in (1,) + LEVELS:
        up = (j[:, None] // m + 1 == j[None] // m) & (j[:, None] // m % 2 == 0)
        masks.append(np.tile(-up.astype(np.float32), (2, 1)))
    put("levels", np.concatenate(masks, 1))
    put("ident64", np.tile(np.eye(64), (2, 1)))
    put("headones", i[:, None] // KD == np.arange(2)[None])
    put("scol", i[:, None] + 1 + P * np.arange(2)[None])
    put("iota16", np.tile(np.arange(16), (P, 1)))
    put("idxdesc", np.tile(np.arange(E, 0, -1), (P, 1)))
    put("mask_d", np.eye(16))
    put("mask_lt", np.arange(16)[:, None] < np.arange(16)[None])
    put("reset", np.tile((np.arange(3 * LCOL) % LCOL != 0), (P, 1)))
    return c


def program(nc, A_x, A_ctx, A_lens, A_consts, A_cols, A_rows, A_brow, A_win, A_wcat, A_wo, A_w2, A_wr, A_wit, A_fwo, out):
    f32, bf16, i32 = mybir.dt.float32, mybir.dt.bfloat16, mybir.dt.int32
    ALU, ACT, AX = mybir.AluOpType, mybir.ActivationFunctionType, mybir.AxisListType

    ctx = ExitStack()
    with ctx:
        def sb(name, shape, dt=f32):
            return ctx.enter_context(nc.sbuf_tensor(name, shape, dt))

        def sem(name):
            return ctx.enter_context(nc.semaphore(name))

        x_in = sb("x_in", [P, NBLK, D])
        ctx_in = sb("ctx_in", [P, NBLK, CTXD])
        lens_in = sb("lens_in", [P, LCOL], i32)
        consts = sb("consts", [P, NCONST])
        cols = sb("cols", [P, NCOLS])
        rows = sb("rows", [P, NROWS])
        brow = sb("brow", [1, 2, D])
        win = sb("win", [P, 2, D])
        wcat = sb("wcat", [P, 2, WCOLS])
        wo = sb("wo", [P, H, D])
        w2 = sb("w2", [P, 2, D])
        wr = sb("wr", [P, 2, E])
        wit = sb("wit", [P, E, 2, D])
        fwo = sb("fwo", [P, E, 2, D])
        ones = sb("ones", [P, P])
        eps = sb("eps", [P, 3])
        warm = sb("warm", [P, 1])

        def C(name, parts=P):
            return consts[0:parts, CONST[name][0]:CONST[name][1]]

        ident = C("ident")

        st = sb("st", [P, NBLK, 6])
        mv = sb("mv", [P, NBLK, 2])
        sd = sb("sd", [P, NBLK])
        rstd = sb("rstd", [P, NBLK])
        xn = sb("xn", [P, NBLK, D])
        xT = sb("xT", [P, 2, T])
        sqj = sb("sqj", [P, CTXD])
        sqj2 = sb("sqj2", [P, CTXD])
        css = sb("css", [P, NBLK])
        csd = sb("csd", [P, NBLK])
        crs = sb("crs", [P, NBLK])
        cs = sb("cs", [P, NBLK, D])
        dep = sb("dep", [P, NBLK, D])
        limb = sb("limb", [P, 3, LCOL], i32)
        lscan = sb("lscan", [P, 3, LCOL])
        csum = sb("csum", [P, 3, LCOL], i32)
        lo0 = sb("lo0", [P, LCOL], i32)
        ca0 = sb("ca0", [P, LCOL], i32)
        s1_ = sb("s1_", [P, LCOL], i32)
        lo1 = sb("lo1", [P, LCOL], i32)
        ca1 = sb("ca1", [P, LCOL], i32)
        s2_ = sb("s2_", [P, LCOL], i32)
        lo2 = sb("lo2", [P, LCOL], i32)
        tf = sb("tf", [P, 5, LCOL])
        pos = sb("pos", [P, LCOL], i32)
        pos_hi = sb("pos_hi", [P, LCOL], i32)
        pos_lo = sb("pos_lo", [P, LCOL], i32)
        oh_hi = sb("oh_hi", [P, LCOL, 16], bf16)
        oh_lo = sb("oh_lo", [P, LCOL, 16], bf16)
        bound = sb("bound", [16, 16])
        bscan = sb("bscan", [16, 16])
        prer = sb("prer", [16, 16, 16])
        cumr = sb("cumr", [16, 16, 16])
        gT = sb("gT", [P, 2, T])
        x1 = sb("x1", [P, NBLK, D])

        st1 = sb("st1", [P, NBLK, 6])
        mv1 = sb("mv1", [P, NBLK, 2])
        sd1 = sb("sd1", [P, 2, NBLK])
        rs1 = sb("rs1", [P, 2, NBLK])
        y = sb("y", [P, NBLK, D])
        z0 = sb("z0", [P, NBLK, D])
        z = sb("z", [P, NBLK, D])
        zss = sb("zss", [P, NBLK])
        zsd = sb("zsd", [P, NBLK])
        zrs = sb("zrs", [P, NBLK])
        hh = xn
        hT = sb("hT", [P, 2, T])
        cv = sb("cv", [P, 8, T])
        sv = sb("sv", [P, 8, T])
        vraw = sb("vraw", [P, 2, T])
        vtap = sb("vtap", [P, TAPS - 1, T])
        ksq = sb("ksq", [P, 2, T])
        qsq = sb("qsq", [P, 2, T])
        xa = sb("xa", [P, NBLK, H])
        nx = sb("nx", [P, NBLK, H])
        ea = sb("ea", [P, NBLK, 8])
        ex = sb("ex", [P, NBLK, 8])
        expA = sb("expA", [P, H])
        sp = sb("sp", [P, 6, NBLK, H])
        poly = sb("poly", [P, 9, NBLK, H])
        g = sb("g", [P, NBLK, H])
        gM = sb("gM", [P, NBLK, H, P])
        E1 = sb("E1", [P, H, T])
        E2 = sb("E2", [P, H, P])
        kss = sb("kss", [P, NBLK, H])
        kse = sb("kse", [P, NBLK, H])
        half = sb("half", [P, NBLK, H])
        ksr = sb("ksr", [P, NBLK, H])
        cden = sb("cden", [P, NBLK, H])
        cfac = sb("cfac", [P, NBLK, H])
        AT1 = sb("AT1", [P, H, T])
        AT2 = sb("AT2", [P, H, P])
        PT1 = sb("PT1", [P, H, T])
        PT2 = sb("PT2", [P, H, P])
        Ats = sb("Ats", [P, NBLK, H, P])
        X = sb("X", [P, NBLK, H, 64])
        XT = sb("XT", [P, NBLK, H, 64])
        U = sb("U", [P, NBLK, H, 64])
        U128 = sb("U128", [64, NBLK, H, 64])
        XTF = sb("XTF", [P, NBLK, H, P])
        vp = sb("vp", [P, NBLK, H, VD])
        F = sb("F", [P, NBLK, H, VD])
        R2 = sb("R2", [P, H, VD])
        qe = sb("qe", [P, NBLK, H])
        sg = sb("sg", [P, NBLK, H, VD])
        osq = gM
        oms = sb("oms", [P, NBLK, H])
        omv = sb("omv", [P, NBLK, H])
        osd = sb("osd", [P, NBLK, H])
        ors = sb("ors", [P, NBLK, H])
        og = Ats
        ogT = vp
        w = sb("w", [P, NBLK, D])
        base = dep
        st2 = sb("st2", [P, NBLK, 6])
        mv2 = sb("mv2", [P, NBLK, 2])
        sd2 = sb("sd2", [P, NBLK])
        rs2 = sb("rs2", [P, NBLK])
        h0 = z0
        h2 = z
        h2T = xT
        ge = sb("ge", [P, NBLK, D])
        x2 = sb("x2", [P, NBLK, D])

        wp = sb("wp", [P, 2, E, D])
        st3 = sb("st3", [P, NBLK, 6])
        mv3 = sb("mv3", [P, NBLK, 2])
        sd3 = sb("sd3", [P, NBLK])
        rs3 = sb("rs3", [P, NBLK])
        x3 = xn
        x3T = hT
        lmax = sb("lmax", [P, NBLK])
        lsh = sb("lsh", [P, NBLK, E])
        pe_ = sb("pe_", [P, NBLK, E])
        psum_ = sb("psum_", [P, NBLK])
        prec = sb("prec", [P, NBLK])
        top = sb("top", [P, 2, NBLK])
        eqm = sb("eqm", [P, 2, NBLK, E])
        scr = sb("scr", [P, 2, NBLK, E])
        first = sb("first", [P, 2, NBLK])
        hot = sb("hot", [P, 2, NBLK, E])
        rest = sb("rest", [P, NBLK, E])
        both = sb("both", [P, NBLK, E])
        wgt0 = sb("wgt0", [P, NBLK, E])
        wgt = sb("wgt", [P, NBLK, E])
        acc = cs

        B = [ctx.enter_context(nc.psum_tensor(f"B{i}", [P, 512], f32)) for i in range(8)]

        names = """ld_x ld_ctx ld_lens ld_consts ld_cols ld_rows ld_brow ld_win ld_wcat ld_wo ld_w2 ld_wr st_out 
            ones_set eps_set var_a xn_ready cs_ready limbs_summed onehots_ready bounds_ready onehot_t dep_ready 
            x1_ready var_1 z_ready hh_ready xT0 xT1 hT0 hT1 ctx_ss sd_ctx sd_a sd_b sd_z z_ss x_turned dep_done 
            limb_offsets bound_counts cum_rows x1_done hh_turned ab_done gate_done ea_ready exp_a expA_ready 
            decay_mm decay_exp masked_e ksq_ready kse_ready ksr_ready qsq_ready kk_done at_ready a_turned ats_ready 
            x_base xt_base u_done u_ready x_done x_ready xt_ready xt64_done xt64_ready u128_done u128_ready 
            xt128_done xt128_ready xtf_diag v_turned vp_ready qk_done pt_ready qe_ready f_done r_done r_ready 
            o_done osq_ready oms_ready sd_o og_ready og_turned ogt_ready enc_done w_ready var_2 sd_2 h2_ready 
            h2_turned h2t0 h2t1 w2_done gelu_ready x2_ready var_3 sd_3 x3_ready x3_turned x3t0 x3t1 logits_done 
            lsh_ready pe_ready moe_done moe_used wp_done wp_ready dve_step pool_step conv_pool conv_q 
            f_ready0 f_ready1 g_masked0 g_masked1 g_ready gate_mm k0_done k1_done kss_done ld_first pool_set 
            q0_done q1_done qss_done silu_k silu_q silu_v v01_done v23_done v_copied tap_last0 tap_last1 tap_last2 
            tap_last3 conv_k""".split()
        S = {n: sem(n) for n in names}
        ld_moe = [sem(f"ld_moe{i}") for i in range(4)]
        block = ctx.enter_context(nc.Block())

        tile_bank = {2: B[2], 3: B[3], 0: B[2], 1: B[3], 4: B[4], 5: B[4], 6: B[4], 7: B[4]}
        tile_at = {5: T, 7: T}
        tile_col = {0: QC, 1: QC + P, 2: KC, 3: KC + P, 4: VC, 5: VC + P, 6: VC + 2 * P, 7: VC + 3 * P}
        gate_bank = (B[4], B[7])
        small = B[5]
        EARLY = 3
        wp_bank = (B[6], B[7], B[6], B[5], B[6], B[4], B[5], B[4])
        UB, XB = (B[1], B[6]), (B[7], B[0])
        gram_bank = (B[2], B[3])
        cross_bank = (B[4], B[5])
        decay_bank = (B[0], B[1], B[6])
        v_bank = (B[2], B[3])
        f_bank = ((B[7], B[0]), (B[1], B[6]))
        r_bank = (B[4], B[5])
        o_bank = ((B[2], B[3]), (B[4], B[5]))
        turn_bank = (B[7], B[0])
        sum_bank = (B[1], B[6])
        moe_bank = (B[1], B[6], B[2], B[3])

        @block.sync
        def _(sp_):
            sp_.dma_start(x_in[:], A_x.rearrange("(b p) d -> p b d", p=P)).then_inc(S["ld_x"], 16)
            sp_.dma_start(consts[:, 0:NFIRST], A_consts[:, 0:NFIRST]).then_inc(S["ld_first"], 16)
            sp_.dma_start(ctx_in[:], A_ctx.rearrange("(b p) d -> p b d", p=P)).then_inc(S["ld_ctx"], 16)
            sp_.dma_start(win[:], A_win).then_inc(S["ld_win"], 16)
            sp_.dma_start(wit[:, 0:2], A_wit[:, 0:2]).then_inc(ld_moe[0], 16)
            sp_.dma_start(fwo[:, 0:2], A_fwo[:, 0:2]).then_inc(ld_moe[0], 16)
            sp_.dma_start(wcat[:], A_wcat).then_inc(S["ld_wcat"], 16)
            for i in range(1, 4):
                sp_.dma_start(wit[:, 2 * i:2 * i + 2], A_wit[:, 2 * i:2 * i + 2]).then_inc(ld_moe[i], 16)
                sp_.dma_start(fwo[:, 2 * i:2 * i + 2], A_fwo[:, 2 * i:2 * i + 2]).then_inc(ld_moe[i], 16)
            sp_.dma_start(wo[:], A_wo).then_inc(S["ld_wo"], 16)
            sp_.dma_start(w2[:], A_w2).then_inc(S["ld_w2"], 16)
            sp_.dma_start(wr[:], A_wr).then_inc(S["ld_wr"], 16)
            for b in range(NBLK):
                sp_.wait_ge(S["moe_used"], E * (b + 1))
                sp_.dma_start(out[b * P:(b + 1) * P, :], acc[:, b]).then_inc(S["st_out"], 16)
            sp_.wait_ge(S["st_out"], 16 * NBLK)

        @block.gpsimd
        def _(pool):
            n = [0]

            def link(ins):
                ins.then_inc(S["pool_step"], 1)
                n[0] += 1
                pool.wait_ge(S["pool_step"], n[0])

            pool.memset(eps[:, 0:1], RMS_EPS)
            pool.memset(eps[:, 1:2], LN_EPS * LN_EPS)
            pool.memset(eps[:, 2:3], QK_EPS).then_inc(S["eps_set"], 1)
            pool.memset(ones[:], 1.0).then_inc(S["ones_set"], 1)
            link(pool.memset(half[:], 0.5))
            for b in range(NBLK):
                pool.memset(XTF[64:P, b, :, 0:64], 0.0).then_inc(S["pool_set"], 1)
                pool.wait_ge(S["pool_set"], b + 1)
            for i in range(2):
                pool.wait_ge(S["silu_k"], i + 1)
                pool.tensor_tensor(ksq[:, i], sv[:, 2 + i], sv[:, 2 + i], ALU.mult).then_inc(S["ksq_ready"], 1)
            pool.wait_ge(S["ld_consts"], 16)
            pool.wait_ge(S["g_ready"], 1)
            pool.tensor_tensor(gM[:, 1], C("tri_le").unsqueeze(1).broadcast_to([P, H, P]),
                               g[:, 1].unsqueeze(2).broadcast_to([P, H, P]), ALU.mult).then_inc(S["g_masked1"], 1)

            def convolve(tile, i):
                for lag in range(TAPS):
                    c = CONV + TAPS * tile + TAPS - 1 - lag
                    o = cv[:, tile] if lag == 0 else vtap[:, lag - 1, lag:T]
                    mul = pool.tensor_scalar(o, vraw[:, i, 0:T - lag], cols[:, c:c + 1], 0.0, ALU.mult, ALU.add)
                    link(mul)
                    if lag == 0:
                        continue
                    add = pool.tensor_tensor(cv[:, tile, lag:T], cv[:, tile, lag:T], o, ALU.add)
                    if lag < TAPS - 1:
                        link(add)
                add.then_inc(S["conv_pool"], 1)

            pool.wait_ge(S["v_copied"], 1)
            convolve(6, 0)
            pool.wait_ge(S["conv_pool"], 1)
            convolve(7, 1)
            pool.wait_ge(S["kse_ready"], 1)
            pool.tensor_tensor(ksr[:], kse[:], half[:], ALU.pow).then_inc(S["ksr_ready"], 1)
            for b in range(NBLK):
                pool.wait_ge(S["at_ready"], 4 * (b + 1))
                e = E1[:, :, 0:P] if b == 0 else E2[:]
                pool.tensor_tensor(e, e, C("tri_le").unsqueeze(1).broadcast_to([P, H, P]), ALU.mult)\
                    .then_inc(S["masked_e"], 1)
            pool.wait_ge(S["v_copied"], 2)
            pool.wait_ge(S["conv_pool"], 2)
            convolve(4, 0)
            pool.wait_ge(S["conv_pool"], 3)
            convolve(5, 1)

        @block.scalar
        def _(act):
            act.dma_start(lens_in[:], A_lens.rearrange("(p c) -> p c", p=P)).then_inc(S["ld_lens"], 16)
            act.dma_start(cols[:], A_cols).then_inc(S["ld_cols"], 16)
            act.dma_start(brow[:], A_brow).then_inc(S["ld_brow"], 16)
            act.dma_start(consts[:, NFIRST:], A_consts[:, NFIRST:]).then_inc(S["ld_consts"], 16)
            act.dma_start(rows[:], A_rows.partition_broadcast(P)).then_inc(S["ld_rows"], 16)

            def evac_wp(e):
                act.wait_ge(S["wp_done"], e + 1)
                act.activation(wp[:, :, e], wp_bank[e][:].rearrange("p (m d) -> p m d", m=2), ACT.Copy)\
                    .then_inc(S["wp_ready"], 1)

            act.wait_ge(S["eps_set"], 1)
            act.activation(warm[:], eps[:, 0:1], ACT.Sqrt)
            act.wait_ge(S["var_a"], 1)
            act.activation(sd[:], mv[:, :, 1], ACT.Sqrt, scale=1.0 + RMS_EPS, bias=eps[:, 1:2]).then_inc(S["sd_a"], 1)
            act.wait_ge(S["ld_ctx"], 16)
            act.activation(sqj[:], ctx_in[:, 0], ACT.Square, accum_out=css[:, 0:1]).then_inc(S["ctx_ss"], 1)
            act.activation(sqj2[:], ctx_in[:, 1], ACT.Square, accum_out=css[:, 1:2]).then_inc(S["ctx_ss"], 1)
            act.wait_ge(S["ctx_ss"], 2)
            act.activation(csd[:], css[:], ACT.Sqrt, scale=1.0 / CTXD, bias=eps[:, 0:1]).then_inc(S["sd_ctx"], 1)
            act.wait_ge(S["x_turned"], 2)
            act.wait_ge(S["ld_cols"], 16)
            act.activation(xT[:, 1], B[1][:, 0:T], ACT.Copy, scale=cols[:, G_RES + 1:G_RES + 2]).then_inc(S["xT1"], 1)
            act.wait_ge(S["var_1"], 1)
            act.activation(sd1[:, 0], mv1[:, :, 1], ACT.Sqrt, bias=eps[:, 0:1]).then_inc(S["sd_b"], 1)
            act.activation(sd1[:, 1], mv1[:, :, 1], ACT.Sqrt, scale=1.0 + LN_EPS, bias=eps[:, 1:2]).then_inc(S["sd_b"], 1)
            for b in range(NBLK):
                act.wait_ge(S["z_ready"], b + 1)
                act.activation((sqj if b == 0 else sqj2)[:, 0:D], z[:, b], ACT.Square, accum_out=zss[:, b:b + 1])\
                    .then_inc(S["z_ss"], 1)
            act.wait_ge(S["z_ss"], 2)
            act.activation(zsd[:], zss[:], ACT.Sqrt, scale=1.0 / D, bias=eps[:, 2:3]).then_inc(S["sd_z"], 1)
            evac_wp(0)
            evac_wp(1)
            act.wait_ge(S["hh_turned"], 2)
            act.activation(hT[:, 1], B[1][:, 0:T], ACT.Copy, scale=cols[:, RMS_W + 1:RMS_W + 2]).then_inc(S["hT1"], 1)
            evac_wp(2)
            act.wait_ge(S["ld_rows"], 16)
            act.activation(expA[:], rows[:, R_ALOG:R_ALOG + H], ACT.Exp).then_inc(S["expA_ready"], 1)

            def last_tap(tile, done):
                act.wait_ge(S[done], 1)
                at = tile_at.get(tile, 0)
                act.activation(cv[:, tile], tile_bank[tile][:, at:at + T], ACT.Copy,
                               scale=cols[:, CONV + TAPS * tile + 3:CONV + TAPS * tile + 4]).then_inc(S[f"tap_last{tile}"], 1)

            def silu(tile, conv, done):
                act.wait_ge(S[conv[0]], conv[1])
                act.activation(sv[:, tile], cv[:, tile], ACT.Silu).then_inc(S[done], 1)

            act.wait_ge(S["ea_ready"], 1)
            act.activation(ex[:], ea[:], ACT.Exp).then_inc(S["exp_a"], 1)
            last_tap(2, "k0_done")
            last_tap(3, "k1_done")

            def silu_gate(b):
                act.wait_ge(S["gate_mm"], b + 1)
                act.activation(sg[:, b].rearrange("p h v -> p (h v)"), gate_bank[b][:], ACT.Silu)\
                    .then_inc(S["gate_done"], 1)

            def copy_v(i, done):
                act.wait_ge(S[done], 1)
                if i == 1:
                    act.wait_ge(S["conv_pool"], 2)
                act.activation(vraw[:].rearrange("p i t -> p (i t)"), B[4][:], ACT.Copy)\
                    .then_inc(S["v_copied"], 1)

            silu_gate(0)
            silu(2, ("conv_k", 1), "silu_k")
            silu(3, ("conv_k", 2), "silu_k")
            silu_gate(1)
            for i, o in enumerate((E1[:, :, 0:P], E2[:], E1[:, :, P:T])):
                if i == 2:
                    copy_v(0, "v23_done")
                act.wait_ge(S["decay_mm"], i + 1)
                act.activation(o, decay_bank[i][:].rearrange("p (h t) -> p h t", h=H), ACT.Exp)\
                    .then_inc(S["decay_exp"], 1)
            for b in range(NBLK):
                act.wait_ge(S["a_turned"], b + 1)
                act.activation(Ats[:, b].rearrange("p h t -> p (h t)"), XB[b][:], ACT.Copy).then_inc(S["ats_ready"], 1)
            last_tap(0, "q0_done")
            last_tap(1, "q1_done")

            for level in range(len(LEVELS)):
                for b in range(NBLK):
                    act.wait_ge(S["x_done"], 2 * level + b + 1)
                    if level == len(LEVELS) - 1:
                        act.wait_ge(S["xt64_done"], b + 1)
                    act.activation(X[:, b].rearrange("p h t -> p (h t)"), XB[b][:, 0:256], ACT.Copy)\
                        .then_inc(S["x_ready"], 1)
                if level == 1:
                    copy_v(1, "v01_done")
                if level == 2:
                    evac_wp(3)
                    silu(0, ("conv_q", 1), "silu_q")
                    silu(1, ("conv_q", 2), "silu_q")
                    silu(6, ("conv_pool", 1), "silu_v")
                    silu(7, ("conv_pool", 2), "silu_v")
            silu(4, ("conv_pool", 3), "silu_v")
            silu(5, ("conv_pool", 4), "silu_v")
            act.wait_ge(S["pool_set"], 2)
            for b in range(NBLK):
                act.wait_ge(S["xt64_ready"], b + 1)
                for i in range(2):
                    r = slice(64 * i, 64 * i + 64)
                    ins = act.activation(XTF[r, b, :, r], XT[r, b], ACT.Copy)
                ins.then_inc(S["xtf_diag"], 1)
            for b in range(NBLK):
                act.wait_ge(S["f_done"], 2 * b + 1)
                act.activation(F[:, b, 0:2].rearrange("p h v -> p (h v)"), f_bank[b][0][:, 0:256], ACT.Copy)\
                    .then_inc(S["f_ready0"], 1)
                if b == 0:
                    act.activation(warm[:], eps[:, 0:1], ACT.Sqrt)
            for b in range(NBLK):
                for p_ in range(2):
                    act.wait_ge(S["o_done"], 2 * b + p_ + 1)
                    act.activation(osq[:, b, 2 * p_:2 * p_ + 2].rearrange("p h v -> p (h v)"),
                                   o_bank[b][p_][:, 0:256], ACT.Square).then_inc(S["osq_ready"], 1)
            for b in range(NBLK):
                act.wait_ge(S["oms_ready"], b + 1)
                act.activation(osd[:, b], omv[:, b], ACT.Sqrt).then_inc(S["sd_o"], 1)
            evac_wp(4)
            for b in range(NBLK):
                act.wait_ge(S["og_turned"], b + 1)
                act.activation(ogT[:, b].rearrange("p h t -> p (h t)"), turn_bank[b][:], ACT.Copy,
                               scale=cols[:, O_W:O_W + 1]).then_inc(S["ogt_ready"], 1)
            for b in range(NBLK):
                act.wait_ge(S["var_2"], b + 1)
                act.activation(sd2[:, b:b + 1], mv2[:, b, 1:2], ACT.Sqrt, bias=eps[:, 0:1]).then_inc(S["sd_2"], 1)
            act.activation(warm[:], eps[:, 0:1], ACT.Gelu)
            evac_wp(5)
            act.wait_ge(S["h2_turned"], 2)
            act.activation(h2T[:, 1], turn_bank[1][:, 0:T], ACT.Copy).then_inc(S["h2t1"], 1)
            evac_wp(6)
            for b in range(NBLK):
                act.wait_ge(S["w2_done"], b + 1)
                act.activation(ge[:, b], sum_bank[b][:, 0:D], ACT.Gelu).then_inc(S["gelu_ready"], 1)
            for b in range(NBLK):
                act.wait_ge(S["var_3"], b + 1)
                act.activation(sd3[:, b:b + 1], mv3[:, b, 1:2], ACT.Sqrt, bias=eps[:, 0:1]).then_inc(S["sd_3"], 1)
            act.activation(warm[:], eps[:, 0:1], ACT.Exp)
            evac_wp(7)
            act.wait_ge(S["x3_turned"], 2)
            act.activation(x3T[:, 1], turn_bank[1][:, 0:T], ACT.Copy).then_inc(S["x3t1"], 1)
            act.wait_ge(S["lsh_ready"], 1)
            act.activation(pe_[:], lsh[:], ACT.Exp).then_inc(S["pe_ready"], 1)

        @block.tensor
        def _(pe):
            mm = pe.matmul

            def turn(src, banks, ready, done):
                for k in range(2):
                    for b in range(NBLK):
                        if k == 0:
                            pe.wait_ge(S[ready], b + 1)
                        ins = pe.transpose(banks[k][:, b * P:(b + 1) * P], src[:, b, k * P:(k + 1) * P], ident)
                    ins.then_inc(S[done], 1)

            def moe_product(e, halves=(0, 1)):
                pe.wait_ge(ld_moe[e // 2], 32)
                if e in (2, 7):
                    pe.wait_ge(S["wp_ready"], e - 1)
                for m in halves:
                    for k in range(2):
                        ins = mm(wp_bank[e][:, m * D:(m + 1) * D], wit[:, e, k, m * P:(m + 1) * P], fwo[:, e, k],
                                 start=(k == 0), stop=(k == 1))
                if m == 1:
                    ins.then_inc(S["wp_done"], 1)

            pe.wait_ge(S["ld_first"], 16)
            pe.wait_ge(S["limbs_summed"], 1)
            mm(small[:, 0:3], C("tri_lt"), lscan[:, :, LCOL - 1], start=True, stop=True).then_inc(S["limb_offsets"], 1)
            pe.wait_ge(S["ones_set"], 1)
            pe.wait_ge(S["ld_brow"], 16)
            for b in range(NBLK):
                mm(B[3 + b][:, 0:D], ones[0:1, :], brow[0:1, 0], start=True, stop=False)
            turn(xn, (B[0], B[1]), "xn_ready", "x_turned")
            pe.wait_ge(S["xT0"], 1)
            pe.wait_ge(S["xT1"], 1)
            pe.wait_ge(S["ld_win"], 16)
            for b in range(NBLK):
                for k in range(2):
                    mm(B[3 + b][:, 0:D], xT[:, k, b * P:(b + 1) * P], win[:, k], start=False, stop=False)
            pe.wait_ge(S["onehots_ready"], 2)
            for i in range(LCOL):
                ins = mm(small[0:16, 0:16], oh_hi[:, i], oh_lo[:, i], start=(i == 0), stop=(i == LCOL - 1))
            ins.then_inc(S["bound_counts"], 1)
            pe.wait_ge(S["ld_consts"], 16)
            pe.wait_ge(S["cs_ready"], 2)
            mm(B[2][:, 0:D], C("decay")[:, 0:P], cs[:, 0], start=True, stop=True)
            mm(B[2][:, D:2 * D], C("decay")[:, P:2 * P], cs[:, 0], start=True, stop=False)
            mm(B[2][:, D:2 * D], C("decay")[:, 2 * P:3 * P], cs[:, 1], start=False, stop=True).then_inc(S["dep_done"], 1)
            pe.wait_ge(S["bounds_ready"], 1)
            mm(small[:, 0:T], ones[0:16, :], cumr[:].rearrange("p a b -> p (a b)"), start=True, stop=True)\
                .then_inc(S["cum_rows"], 1)
            pe.wait_ge(S["onehot_t"], 2)
            pe.wait_ge(S["dep_ready"], 1)
            for b in range(NBLK):
                for k in range(2):
                    ins = mm(B[3 + b][:, 0:D], gT[:, k, b * P:(b + 1) * P], dep[:, k], start=False, stop=(k == 1))
                ins.then_inc(S["x1_done"], 1)
            moe_product(0)
            moe_product(1)

            moe_product(2, (0,))
            turn(hh, (B[0], B[1]), "hh_ready", "hh_turned")
            moe_product(2, (1,))
            pe.wait_ge(S["hT0"], 1)
            pe.wait_ge(S["hT1"], 1)
            pe.wait_ge(S["ld_wcat"], 16)
            for b in range(NBLK):
                for k in range(2):
                    ins = mm(small[:, 8 * b:8 * b + 8], hT[:, k, b * P:(b + 1) * P], wcat[:, k, ABC:ABC + 8],
                             start=(k == 0), stop=(k == 1))
            ins.then_inc(S["ab_done"], 1)

            def project(tile):
                at, c = tile_at.get(tile, 0), tile_col[tile]
                for k in range(2):
                    ins = mm(tile_bank[tile][:, at:at + T], wcat[:, k, c:c + P], hT[:, k], start=(k == 0), stop=(k == 1))
                return ins

            project(2).then_inc(S["k0_done"], 1)
            project(3).then_inc(S["k1_done"], 1)
            for b in range(NBLK):
                if b == 1:
                    pe.wait_ge(S["wp_ready"], 2)
                for k in range(2):
                    ins = mm(gate_bank[b][:], hT[:, k, b * P:(b + 1) * P], wcat[:, k, GC:GC + H * VD],
                             start=(k == 0), stop=(k == 1))
                ins.then_inc(S["gate_mm"], 1)

            def squares(sq, col, done):
                for b in range(NBLK):
                    for i in range(2):
                        at = col + H * b + 2 * i
                        ins = mm(small[:, at:at + 2], sq[:, i, b * P:(b + 1) * P], C("headones"), start=True, stop=True)
                ins.then_inc(S[done], 1)

            def gram(a0, done, parities=(0, 1)):
                for odd in parities:
                    r = slice(64 * odd, 64 * odd + 64)
                    for blk in range(NBLK):
                        for i in range(2):
                            at, t = (2 * blk + i) * P, slice(blk * P, (blk + 1) * P)
                            ins = mm(gram_bank[odd][:, at:at + P], sv[r, 2 + i, t], sv[r, a0 + i, t],
                                     start=True, stop=True)
                    ins.then_inc(S[done], 1)

            def cross_gram(a0, done):
                for odd in range(2):
                    r = slice(64 * odd, 64 * odd + 64)
                    for i in range(2):
                        ins = mm(cross_bank[odd][:, i * P:(i + 1) * P], sv[r, 2 + i, 0:P], sv[r, a0 + i, P:T],
                                 start=True, stop=True)
                    ins.then_inc(S[done], 1)

            pe.wait_ge(S["silu_k"], 2)
            gram(2, "kk_done")
            pe.wait_ge(S["g_masked0"], 1)
            mm(decay_bank[0][:], C("tri_gt"), gM[:, 0].rearrange("p h t -> p (h t)"), start=True, stop=True)\
                .then_inc(S["decay_mm"], 1)
            pe.wait_ge(S["ksq_ready"], 2)
            squares(ksq, 16, "kss_done")
            pe.wait_ge(S["g_masked1"], 1)
            mm(decay_bank[1][:], C("tri_gt"), gM[:, 1].rearrange("p h t -> p (h t)"), start=True, stop=True)\
                .then_inc(S["decay_mm"], 1)
            pe.wait_ge(S["gate_done"], 1)
            project(6)
            project(7).then_inc(S["v23_done"], 1)
            pe.wait_ge(S["wp_ready"], 3)
            mm(decay_bank[2][:], C("tri_gt"), g[:, 0].unsqueeze(2).broadcast_to([P, H, P]), start=True, stop=False)
            mm(decay_bank[2][:], ones[:], gM[:, 1].rearrange("p h t -> p (h t)"), start=False, stop=True)\
                .then_inc(S["decay_mm"], 1)
            for b in range(NBLK):
                pe.wait_ge(S["at_ready"], 4 * (b + 1))
                if b == 0:
                    pe.wait_ge(S["gate_done"], 2)
                for h in range(H):
                    src = AT1[:, h, 0:P] if b == 0 else AT2[:, h]
                    ins = pe.transpose(XB[b][:, h * P:(h + 1) * P], src, ident)
                ins.then_inc(S["a_turned"], 1)
                if b == 0:
                    pe.wait_ge(S["kse_ready"], 1)
                    pe.wait_ge(S["v_copied"], 1)
                    cross_gram(2, "kk_done")
            project(0).then_inc(S["q0_done"], 1)

            def tiles64(b, fn):
                for h in range(H):
                    for i in range(2):
                        ins = fn(h, slice(64 * i, 64 * i + 64))
                return ins

            def double_u(level, b):
                if level == 0:
                    pe.wait_ge(S["ats_ready"], b + 1)
                    pe.wait_ge(S["xt_base"], b + 1)
                else:
                    pe.wait_ge(S["xt_ready"], 2 * (level - 1) + b + 1)
                tiles64(b, lambda h, r: mm(UB[b][r, 64 * h:64 * h + 64], Ats[r, b, h, r], XT[r, b, h],
                                           start=True, stop=True)).then_inc(S["u_done"], 1)

            def double_x(level, b):
                pe.wait_ge(S["u_ready"], 2 * level + b + 1)
                tiles64(b, lambda h, r: mm(XB[b][r, 64 * h:64 * h + 64], U[r, b, h], X[r, b, h],
                                           start=False, stop=True, skip_group_check=True))\
                    .then_inc(S["x_done"], 1)

            for level in range(len(LEVELS)):
                for b in range(NBLK):
                    double_u(level, b)
                    if level == 0:
                        pe.wait_ge(S["x_base"], b + 1)
                        mm(XB[b][:, 0:256], ident, X[:, b].rearrange("p h t -> p (h t)"), start=True, stop=True,
                           skip_group_check=True)
                if level == 0:
                    project(1).then_inc(S["q1_done"], 1)
                if level == 1:
                    pe.wait_ge(S["at_ready"], 12)
                    project(4)
                if level == 2:
                    moe_product(3, (0,))
                if level == 4:
                    gram(0, "qk_done", (1,))
                    pe.wait_ge(S["qe_ready"], 1)
                    pe.wait_ge(S["wp_ready"], 4)
                    pe.wait_ge(S["v_copied"], 2)
                    cross_gram(0, "qk_done")
                for b in range(NBLK):
                    double_x(level, b)
                    if level == len(LEVELS) - 1:
                        tiles64(b, lambda h, r: mm(UB[b][r, 256 + 64 * h:256 + 64 * h + 64], X[r, b, h], U[r, b, h],
                                                   start=True, stop=True)).then_inc(S["xt64_done"], 1)
                if level == 1:
                    project(5).then_inc(S["v01_done"], 1)
                if level == 2:
                    moe_product(3, (1,))
                if level == 3:
                    pe.wait_ge(S["silu_q"], 2)
                    gram(0, "qk_done", (0,))
                    pe.wait_ge(S["qsq_ready"], 2)
                    pe.wait_ge(S["wp_ready"], 4)
                    squares(qsq, 24, "qss_done")
            for b in range(NBLK):
                pe.wait_ge(S["xt64_ready"], b + 1)
                for h in range(H):
                    ins = mm(UB[b][0:64, 64 * h:64 * h + 64], Ats[64:P, b, h, 0:64], XT[64:P, b, h],
                             start=True, stop=True)
                ins.then_inc(S["u128_done"], 1)
            pe.wait_ge(S["silu_v"], 4)
            pe.wait_ge(S["pt_ready"], 8)
            for b in range(NBLK):
                for h in range(H):
                    ins = pe.transpose(v_bank[b][:, h * P:(h + 1) * P], sv[:, 4 + h, b * P:(b + 1) * P], ident)
                ins.then_inc(S["v_turned"], 1)
            for b in range(NBLK):
                pe.wait_ge(S["u128_ready"], b + 1)
                pe.wait_ge(S["x_ready"], 2 * len(LEVELS) - 1 + b)
                for h in range(H):
                    ins = mm(UB[b][0:64, 256 + 64 * h:256 + 64 * h + 64], X[0:64, b, h], U128[:, b, h],
                             start=True, stop=True)
                ins.then_inc(S["xt128_done"], 1)

            def heads(banks, p_, lhs, rhs, start=True, stop=True):
                for i in range(2):
                    h = 2 * p_ + i
                    ins = mm(banks[p_][:, i * VD:(i + 1) * VD], lhs(h), rhs[:, h], start=start, stop=stop,
                             skip_group_check=True)
                return ins

            pe.wait_ge(S["xt128_ready"], 1)
            pe.wait_ge(S["xtf_diag"], 1)
            pe.wait_ge(S["x_ready"], 2 * len(LEVELS))
            pe.wait_ge(S["vp_ready"], 1)
            for p_ in range(2):
                heads(f_bank[0], p_, lambda h: XTF[:, 0, h], vp[:, 0]).then_inc(S["f_done"], 1)

            pe.wait_ge(S["pt_ready"], 12)
            for p_ in range(2):
                pe.wait_ge(S[f"f_ready{p_}"], 1)
                heads(r_bank, p_, lambda h: AT1[:, h, P:T], F[:, 0]).then_inc(S["r_done"], 1)
            pe.wait_ge(S["vp_ready"], 2)
            for p_ in range(2):
                heads(o_bank[0], p_, lambda h: PT1[:, h, 0:P], F[:, 0]).then_inc(S["o_done"], 1)
            pe.wait_ge(S["xtf_diag"], 2)
            pe.wait_ge(S["xt128_ready"], 2)
            for p_ in range(2):
                pe.wait_ge(S["r_ready"], p_ + 1)
                heads(f_bank[1], p_, lambda h: XTF[:, 1, h], R2).then_inc(S["f_done"], 1)
            for p_ in range(2):
                pe.wait_ge(S[f"f_ready{p_}"], 2)
                for i in range(2):
                    h = 2 * p_ + i
                    o = o_bank[1][p_][:, i * VD:(i + 1) * VD]
                    mm(o, PT1[:, h, P:T], F[:, 0, h], start=True, stop=False, skip_group_check=True)
                    ins = mm(o, PT2[:, h], F[:, 1, h], start=False, stop=True, skip_group_check=True)
                ins.then_inc(S["o_done"], 1)
            moe_product(4)
            for b in range(NBLK):
                pe.wait_ge(S["og_ready"], 4 * (b + 1))
                for h in range(H):
                    ins = pe.transpose(turn_bank[b][:, h * P:(h + 1) * P], og[:, b, h], ident)
                ins.then_inc(S["og_turned"], 1)
            pe.wait_ge(S["ld_wo"], 16)
            pe.wait_ge(S["wp_ready"], 5)
            for b in range(NBLK):
                pe.wait_ge(S["ogt_ready"], b + 1)
                for h in range(H):
                    ins = mm(sum_bank[b][:, 0:D], ogT[:, b, h], wo[:, h], start=(h == 0), stop=(h == H - 1))
                ins.then_inc(S["enc_done"], 1)
            moe_product(5)
            for b in range(NBLK):
                pe.wait_ge(S["w_ready"], b + 1)
                mm(sum_bank[b][:, 0:D], ones[0:1, :], brow[0:1, 1], start=True, stop=False)
            turn(h2, turn_bank, "h2_ready", "h2_turned")
            pe.wait_ge(S["ld_w2"], 16)
            pe.wait_ge(S["h2t0"], 1)
            pe.wait_ge(S["h2t1"], 1)
            for b in range(NBLK):
                for k in range(2):
                    ins = mm(sum_bank[b][:, 0:D], h2T[:, k, b * P:(b + 1) * P], w2[:, k], start=False, stop=(k == 1))
                ins.then_inc(S["w2_done"], 1)
            moe_product(6)
            moe_product(7)

            turn(x3, turn_bank, "x3_ready", "x3_turned")
            pe.wait_ge(S["ld_wr"], 16)
            pe.wait_ge(S["wp_ready"], 8)
            pe.wait_ge(S["x3t0"], 1)
            pe.wait_ge(S["x3t1"], 1)
            for b in range(NBLK):
                for k in range(2):
                    ins = mm(small[:, 8 * b:8 * b + 8], x3T[:, k, b * P:(b + 1) * P], wr[:, k],
                             start=(k == 0), stop=(k == 1))
            ins.then_inc(S["logits_done"], 1)
            n = 0
            for b in range(NBLK):
                for pair in range(E // 2):
                    bank = moe_bank[n % 4]
                    if n >= 4:
                        pe.wait_ge(S["moe_used"], 2 * (n - 3))
                    for k in range(2):
                        ins = mm(bank[:], x3T[:, k, b * P:(b + 1) * P],
                                 wp[:, k, 2 * pair:2 * pair + 2].rearrange("p e d -> p (e d)"),
                                 start=(k == 0), stop=(k == 1))
                    ins.then_inc(S["moe_done"], 1)
                    n += 1

        @block.vector
        def _(dve):
            n = [0]

            def mark(ins):
                ins.then_inc(S["dve_step"], 1)
                n[0] += 1
                return n[0]

            def need(k):
                dve.wait_ge(S["dve_step"], k)

            def link(ins):
                need(mark(ins))

            ts, tt, stt = dve.tensor_scalar, dve.tensor_tensor, dve.scalar_tensor_tensor

            dve.wait_ge(S["ld_x"], 16)
            for b in range(NBLK):
                k = mark(dve.bn_stats(st[:, b], x_in[:, b]))
            dve.wait_ge(S["ld_lens"], 16)
            ts(limb[:, 0], lens_in[:], 2047, None, ALU.bitwise_and)
            need(k)
            dve.bn_aggr(mv[:, 0], st[:, 0])
            dve.bn_aggr(mv[:, 1], st[:, 1]).then_inc(S["var_a"], 1)
            ts(limb[:, 1], lens_in[:], 11, 2047, ALU.logical_shift_right, ALU.bitwise_and)
            k = mark(ts(limb[:, 2], lens_in[:], 22, 1023, ALU.logical_shift_right, ALU.bitwise_and))
            dve.wait_ge(S["ld_first"], 16)
            need(k)
            dve.tensor_tensor_scan(lscan[:].rearrange("p l c -> p (l c)"), C("reset"),
                                   limb[:].rearrange("p l c -> p (l c)"), 0.0, ALU.mult, ALU.add)\
                .then_inc(S["limbs_summed"], 1)
            dve.wait_ge(S["sd_a"], 1)
            link(dve.reciprocal(rstd[:], sd[:]))
            dve.wait_ge(S["var_a"], 1)
            ts(xn[:, 0], x_in[:, 0], mv[:, 0, 0:1], rstd[:, 0:1], ALU.subtract, ALU.mult).then_inc(S["xn_ready"], 1)
            dve.wait_ge(S["limb_offsets"], 1)
            dve.wait_ge(S["limbs_summed"], 1)
            k = mark(tt(csum[:], lscan[:], small[:, 0:3].unsqueeze(2).broadcast_to([P, 3, LCOL]), ALU.add))
            ts(xn[:, 1], x_in[:, 1], mv[:, 1, 0:1], rstd[:, 1:2], ALU.subtract, ALU.mult).then_inc(S["xn_ready"], 1)
            need(k)
            k = mark(ts(ca0[:], csum[:, 0], 11, None, ALU.logical_shift_right))
            ts(lo0[:], csum[:, 0], 2047, None, ALU.bitwise_and)
            need(k)
            k = mark(tt(s1_[:], csum[:, 1], ca0[:], ALU.add))
            need(k)
            k = mark(ts(ca1[:], s1_[:], 11, None, ALU.logical_shift_right))
            ts(lo1[:], s1_[:], 2047, None, ALU.bitwise_and)
            need(k)
            k = mark(tt(s2_[:], csum[:, 2], ca1[:], ALU.add))
            dve.wait_ge(S["x_turned"], 1)
            dve.wait_ge(S["ld_cols"], 16)
            ts(xT[:, 0], B[0][:, 0:T], cols[:, G_RES:G_RES + 1], None, ALU.mult).then_inc(S["xT0"], 1)
            need(k)
            link(ts(lo2[:], s2_[:], 1023, None, ALU.bitwise_and))
            link(ts(tf[:, 0], lo2[:], 512.0, -1024.0, ALU.is_ge, ALU.mult))
            link(tt(tf[:, 1], tf[:, 0], lo2[:], ALU.add))
            link(stt(tf[:, 2], tf[:, 1], 2048.0, lo1[:], ALU.mult, ALU.add))
            link(stt(tf[:, 3], tf[:, 2], 2048.0, lo0[:], ALU.mult, ALU.add))
            link(ts(tf[:, 4], tf[:, 3], 0.0, float(T), ALU.is_le, ALU.mult))
            link(stt(tf[:, 0], tf[:, 3], -1.0, tf[:, 4], ALU.add, ALU.add))
            link(ts(pos[:], tf[:, 0], float(2 * T), -1.0, ALU.min, ALU.max))
            ts(pos_hi[:], pos[:], 4, None, ALU.arith_shift_right)
            link(ts(pos_lo[:], pos[:], 15, None, ALU.bitwise_and))
            for oh, p_ in ((oh_hi, pos_hi), (oh_lo, pos_lo)):
                tt(oh[:], p_[:].unsqueeze(2).broadcast_to([P, LCOL, 16]),
                   C("iota16").unsqueeze(1).broadcast_to([P, LCOL, 16]), ALU.is_equal).then_inc(S["onehots_ready"], 1)
            dve.wait_ge(S["sd_ctx"], 1)
            link(dve.reciprocal(crs[:], csd[:]))
            for b in range(NBLK):
                ts(cs[:, b], ctx_in[:, b, 0:D], crs[:, b:b + 1], None, ALU.mult).then_inc(S["cs_ready"], 1)
            dve.wait_ge(S["bound_counts"], 1)
            link(ts(bound[:], small[0:16, 0:16], 1.0, None, ALU.min))
            dve.wait_ge(S["ones_set"], 1)
            link(dve.tensor_tensor_scan(bscan[:], ones[0:16, 0:16], bound[:], 0.0, ALU.mult, ALU.add))
            link(tt(prer[:], bscan[:].unsqueeze(1).broadcast_to([16, 16, 16]),
                    C("mask_d", 16).unsqueeze(2).broadcast_to([16, 16, 16]), ALU.mult))
            stt(cumr[:], C("mask_lt", 16).unsqueeze(2).broadcast_to([16, 16, 16]), bscan[:, 15:16], prer[:],
                ALU.mult, ALU.add).then_inc(S["bounds_ready"], 1)
            dve.wait_ge(S["dep_done"], 1)
            dve.wait_ge(S["ld_rows"], 16)
            tt(dep[:], B[2][:].rearrange("p (b d) -> p b d", b=2),
               rows[:, R_GINIT:R_GINIT + D].unsqueeze(1).broadcast_to([P, 2, D]), ALU.mult).then_inc(S["dep_ready"], 1)
            dve.wait_ge(S["cum_rows"], 1)
            for k in range(2):
                ts(gT[:, k], small[:, 0:T], 1.0, C("scol")[:, k:k + 1], ALU.max, ALU.is_equal)\
                    .then_inc(S["onehot_t"], 1)
            for b in range(NBLK):
                dve.wait_ge(S["x1_done"], b + 1)
                tt(x1[:, b], B[3 + b][:, 0:D], x_in[:, b], ALU.add).then_inc(S["x1_ready"], 1)
                dve.wait_ge(S["x1_ready"], b + 1)
                k = mark(dve.bn_stats(st1[:, b], x1[:, b]))
            need(k)
            dve.bn_aggr(mv1[:, 0], st1[:, 0])
            dve.bn_aggr(mv1[:, 1], st1[:, 1]).then_inc(S["var_1"], 1)
            dve.wait_ge(S["var_1"], 1)
            for b in range(NBLK):
                k = mark(stt(z0[:, b], x1[:, b], mv1[:, b, 0:1], rows[:, R_LN1G:R_LN1G + D], ALU.subtract, ALU.mult))
            dve.wait_ge(S["sd_b"], 2)
            link(dve.reciprocal(rs1[:], sd1[:]))
            for b in range(NBLK):
                stt(z[:, b], z0[:, b], rs1[:, 1, b:b + 1], rows[:, R_LN1B:R_LN1B + D], ALU.mult, ALU.add)\
                    .then_inc(S["z_ready"], 1)
            for b in range(NBLK):
                ts(y[:, b], x1[:, b], mv1[:, b, 0:1], rs1[:, 0, b:b + 1], ALU.subtract, ALU.mult)
            dve.wait_ge(S["sd_z"], 1)
            link(dve.reciprocal(zrs[:], zsd[:]))
            dve.wait_ge(S["z_ready"], 2)
            for b in range(NBLK):
                ts(hh[:, b], z[:, b], zrs[:, b:b + 1], None, ALU.mult).then_inc(S["hh_ready"], 1)
            dve.wait_ge(S["hh_turned"], 1)
            ts(hT[:, 0], B[0][:, 0:T], cols[:, RMS_W:RMS_W + 1], None, ALU.mult).then_inc(S["hT0"], 1)
            dve.wait_ge(S["ab_done"], 1)
            ab = small[:, 0:16].rearrange("p (b c) -> p b c", b=NBLK)
            k = mark(tt(xa[:], ab[:, :, 0:H], rows[:, R_DTB:R_DTB + H].unsqueeze(1).broadcast_to([P, NBLK, H]), ALU.add))
            ts(ea[:, :, H:2 * H], ab[:, :, H:2 * H], -1.0, None, ALU.mult)
            need(k)
            link(ts(nx[:], xa[:], -1.0, None, ALU.mult))
            tt(ea[:, :, 0:H], xa[:], nx[:], ALU.min).then_inc(S["ea_ready"], 1)

            tap_at = {}

            def tap(tile, lag, done=None):
                if lag == 1:
                    dve.wait_ge(S[f"tap_last{tile}"], 1)
                else:
                    need(tap_at[tile])
                c, at = CONV + TAPS * tile + TAPS - 1 - lag, tile_at.get(tile, 0)
                ins = stt(cv[:, tile, lag:T], tile_bank[tile][:, at:at + T - lag], cols[:, c:c + 1], cv[:, tile, lag:T],
                          ALU.mult, ALU.add)
                if lag < TAPS - 1:
                    tap_at[tile] = mark(ins)
                else:
                    ins.then_inc(S[done], 1)

            dve.wait_ge(S["exp_a"], 1)
            k = mark(ts(sp[:, 0], ex[:, :, 0:H], 2.0, None, ALU.add))
            ts(sp[:, 4], xa[:], 0.0, None, ALU.max)
            need(k)
            k = mark(dve.reciprocal(sp[:, 1], sp[:, 0]))
            tap(2, 1)
            need(k)
            k = mark(tt(sp[:, 2], ex[:, :, 0:H], sp[:, 1], ALU.mult))
            tap(3, 1)
            need(k)
            k = mark(tt(sp[:, 3], sp[:, 2], sp[:, 2], ALU.mult))
            tap(2, 2)
            need(k)
            k = mark(ts(poly[:, 0], sp[:, 3], ATANH[0], None, ALU.mult))
            tap(3, 2)
            need(k)
            k = mark(stt(poly[:, 1], poly[:, 0], ATANH[1], sp[:, 3], ALU.add, ALU.mult))
            tap(2, 3, "conv_k")
            need(k)
            k = mark(stt(poly[:, 2], poly[:, 1], ATANH[2], sp[:, 3], ALU.add, ALU.mult))
            tap(3, 3, "conv_k")
            need(k)
            for i in range(3, len(ATANH)):
                link(stt(poly[:, i], poly[:, i - 1], ATANH[i], sp[:, 3], ALU.add, ALU.mult))
            link(stt(poly[:, 7], poly[:, 6], 1.0, sp[:, 2], ALU.add, ALU.mult))
            link(stt(sp[:, 5], poly[:, 7], 2.0, sp[:, 4], ALU.mult, ALU.add))
            dve.wait_ge(S["expA_ready"], 1)
            stt(g[:], sp[:, 5], -1.0, expA[:].unsqueeze(1).broadcast_to([P, NBLK, H]), ALU.mult, ALU.mult)\
                .then_inc(S["g_ready"], 1)
            dve.wait_ge(S["g_ready"], 1)
            tt(gM[:, 0], C("tri_le").unsqueeze(1).broadcast_to([P, H, P]),
               g[:, 0].unsqueeze(2).broadcast_to([P, H, P]), ALU.mult).then_inc(S["g_masked0"], 1)
            dve.wait_ge(S["kss_done"], 1)
            ts(kse[:], small[:, 16:24].rearrange("p (b h) -> p b h", b=NBLK), QK_EPS, None, ALU.add)\
                .then_inc(S["kse_ready"], 1)
            dve.wait_ge(S["kse_ready"], 1)
            link(stt(cden[:], ex[:, :, H:2 * H], 1.0, kse[:], ALU.add, ALU.mult))
            link(dve.reciprocal(cfac[:], cden[:]))

            def scale_gram(blk, done, o, ready):
                if blk == 0:
                    dve.wait_ge(S[done], 2)
                for h in range(H):
                    at = (2 * blk + h // 2) * P
                    stt(o[:, h, 0:P], gram_bank[h % 2][:, at:at + P], cfac[:, blk, h:h + 1],
                        (E1, E2)[blk][:, h, 0:P], ALU.mult, ALU.mult).then_inc(S[ready], 1)

            def scale_cross(done, o, ready):
                dve.wait_ge(S[done], 4)
                for h in range(H):
                    at = h // 2 * P
                    stt(o[:, h, P:T], cross_bank[h % 2][:, at:at + P], cfac[:, 0, h:h + 1],
                        E1[:, h, P:T], ALU.mult, ALU.mult).then_inc(S[ready], 1)

            lv = CONST["levels"][0]

            def level_mask(i, r=slice(0, P)):
                return consts[r, lv + 64 * i:lv + 64 * i + 64].unsqueeze(1).broadcast_to([r.stop - r.start, H, 64])

            for b in range(NBLK):
                dve.wait_ge(S["decay_exp"], b + 1)
                scale_gram(b, "kk_done", (AT1, AT2)[b], "at_ready")
                dve.wait_ge(S["at_ready"], 4 * (b + 1))
                for i in range(2):
                    r = slice(64 * i, 64 * i + 64)
                    src = AT1[r, :, r] if b == 0 else AT2[r, :, r]
                    k = mark(tt(U[r, b], src, level_mask(0, r), ALU.mult))
                need(k)
                tt(XT[:, b], U[:, b], C("ident64").unsqueeze(1).broadcast_to([P, H, 64]), ALU.add)\
                    .then_inc(S["xt_base"], 1)
                dve.wait_ge(S["xt_base"], b + 1)
                dve.transpose(X[:, b].rearrange("p h t -> p (h t)"),
                              XT[:, b].rearrange("p h t -> p (h t)")).then_inc(S["x_base"], 1)

            for level in range(len(LEVELS)):
                last = level == len(LEVELS) - 1
                for b in range(NBLK):
                    dve.wait_ge(S["u_done"], 2 * level + b + 1)
                    if level >= 1:
                        dve.wait_ge(S["x_done"], 2 * (level - 1) + b + 1)
                    else:
                        dve.wait_ge(S["x_base"], b + 1)
                    tt(U[:, b], UB[b][:, 0:256].rearrange("p (h t) -> p h t", h=H), level_mask(level + 1), ALU.mult)\
                        .then_inc(S["u_ready"], 1)
                if level == 0:
                    dve.wait_ge(S["decay_exp"], 3)
                    scale_cross("kk_done", AT1, "at_ready")
                if level == 1:
                    for lag in (1, 2):
                        tap(0, lag)
                        tap(1, lag)
                if level == 2:
                    tap(0, 3, "conv_q")
                    tap(1, 3, "conv_q")
                if level == 3:
                    for i in range(2):
                        dve.wait_ge(S["silu_q"], i + 1)
                        tt(qsq[:, i], sv[:, i], sv[:, i], ALU.mult).then_inc(S["qsq_ready"], 1)
                if last:
                    dve.wait_ge(S["qss_done"], 1)
                    ts(qe[:], small[:, 24:32].rearrange("p (b h) -> p b h", b=NBLK), QK_EPS, QK_EPS * KD, ALU.add,
                       ALU.mult).then_inc(S["qe_ready"], 1)
                    dve.wait_ge(S["masked_e"], 2)
                    scale_gram(0, "qk_done", PT1, "pt_ready")
                    scale_gram(1, "qk_done", PT2, "pt_ready")
                for b in range(NBLK):
                    if not last:
                        dve.wait_ge(S["x_ready"], 2 * level + b + 1)
                        dve.transpose(XT[:, b].rearrange("p h t -> p (h t)"),
                                      X[:, b].rearrange("p h t -> p (h t)")).then_inc(S["xt_ready"], 1)
                    else:
                        dve.wait_ge(S["xt64_done"], b + 1)
                        for i in range(2):
                            r = slice(64 * i, 64 * i + 32)
                            ins = dve.tensor_copy(XT[r, b, :, 32:64],
                                                  UB[b][r, 256:512].rearrange("p (h t) -> p h t", h=H)[:, :, 32:64])
                        ins.then_inc(S["xt64_ready"], 1)
            for b in range(NBLK):
                dve.wait_ge(S["u128_done"], b + 1)
                ts(U128[:, b], UB[b][0:64, 0:256].rearrange("p (h t) -> p h t", h=H), -1.0, None, ALU.mult)\
                    .then_inc(S["u128_ready"], 1)
            dve.wait_ge(S["ksr_ready"], 1)
            for b in range(NBLK):
                dve.wait_ge(S["v_turned"], b + 1)
                tt(vp[:, b], v_bank[b][:].rearrange("p (h v) -> p h v", h=H),
                   ksr[:, b].unsqueeze(2).broadcast_to([P, H, VD]), ALU.mult).then_inc(S["vp_ready"], 1)
                dve.wait_ge(S["xt128_done"], b + 1)
                dve.tensor_copy(XTF[0:64, b, :, 64:P], UB[b][0:64, 256:512].rearrange("p (h t) -> p h t", h=H))\
                    .then_inc(S["xt128_ready"], 1)
            scale_cross("qk_done", PT1, "pt_ready")

            def copy_f(b):
                dve.wait_ge(S["f_done"], 2 * b + 2)
                dve.tensor_copy(F[:, b, 2:4].rearrange("p h v -> p (h v)"), f_bank[b][1][:, 0:256])\
                    .then_inc(S["f_ready1"], 1)

            copy_f(0)
            dve.wait_ge(S["vp_ready"], 2)
            for p_ in range(2):
                dve.wait_ge(S["r_done"], p_ + 1)
                tt(R2[:, 2 * p_:2 * p_ + 2], vp[:, 1, 2 * p_:2 * p_ + 2],
                   r_bank[p_][:, 0:256].rearrange("p (h v) -> p h v", h=2), ALU.subtract).then_inc(S["r_ready"], 1)
            copy_f(1)
            dve.wait_ge(S["qe_ready"], 1)
            for b in range(NBLK):
                dve.wait_ge(S["osq_ready"], 2 * (b + 1))
                link(dve.tensor_reduce(oms[:, b], osq[:, b], AX.X, ALU.add))
                stt(omv[:, b], oms[:, b], 1.0 / VD, qe[:, b], ALU.mult, ALU.add).then_inc(S["oms_ready"], 1)
            dve.wait_ge(S["gate_done"], 2)
            for b in range(NBLK):
                dve.wait_ge(S["sd_o"], b + 1)
                link(dve.reciprocal(ors[:, b], osd[:, b]))
                for h in range(H):
                    stt(og[:, b, h], o_bank[b][h // 2][:, h % 2 * VD:(h % 2 + 1) * VD], ors[:, b, h:h + 1], sg[:, b, h],
                        ALU.mult, ALU.mult).then_inc(S["og_ready"], 1)
            for b in range(NBLK):
                dve.wait_ge(S["enc_done"], b + 1)
                tt(w[:, b], sum_bank[b][:, 0:D], y[:, b], ALU.add).then_inc(S["w_ready"], 1)
                dve.wait_ge(S["w_ready"], b + 1)
                link(dve.bn_stats(st2[:, b], w[:, b]))
                dve.bn_aggr(mv2[:, b], st2[:, b]).then_inc(S["var_2"], 1)
                dve.wait_ge(S["var_2"], b + 1)
                stt(h0[:, b], w[:, b], mv2[:, b, 0:1], rows[:, R_LN2G:R_LN2G + D], ALU.subtract, ALU.mult)
                dve.wait_ge(S["sd_2"], b + 1)
                link(dve.reciprocal(rs2[:, b:b + 1], sd2[:, b:b + 1]))
                stt(h2[:, b], h0[:, b], rs2[:, b:b + 1], rows[:, R_LN2B:R_LN2B + D], ALU.mult, ALU.add)\
                    .then_inc(S["h2_ready"], 1)
            for b in range(NBLK):
                k = mark(tt(base[:, b], w[:, b], x1[:, b], ALU.add))
            dve.wait_ge(S["h2_turned"], 1)
            dve.tensor_copy(h2T[:, 0], turn_bank[0][:, 0:T]).then_inc(S["h2t0"], 1)
            need(k)
            for b in range(NBLK):
                dve.wait_ge(S["gelu_ready"], b + 1)
                tt(x2[:, b], ge[:, b], base[:, b], ALU.add).then_inc(S["x2_ready"], 1)
                dve.wait_ge(S["x2_ready"], b + 1)
                link(dve.bn_stats(st3[:, b], x2[:, b]))
                dve.bn_aggr(mv3[:, b], st3[:, b]).then_inc(S["var_3"], 1)
            for b in range(NBLK):
                dve.wait_ge(S["var_3"], b + 1)
                dve.wait_ge(S["sd_3"], b + 1)
                link(dve.reciprocal(rs3[:, b:b + 1], sd3[:, b:b + 1]))
                ts(x3[:, b], x2[:, b], mv3[:, b, 0:1], rs3[:, b:b + 1], ALU.subtract, ALU.mult)\
                    .then_inc(S["x3_ready"], 1)
            dve.wait_ge(S["x3_turned"], 1)
            dve.tensor_copy(x3T[:, 0], turn_bank[0][:, 0:T]).then_inc(S["x3t0"], 1)

            def over(a):
                return a.unsqueeze(2).broadcast_to([P, NBLK, E])

            dve.wait_ge(S["logits_done"], 1)
            lg = small[:, 0:16].rearrange("p (b e) -> p b e", b=NBLK)
            link(dve.tensor_reduce(lmax[:], lg, AX.X, ALU.max))
            tt(lsh[:], lg, over(lmax[:]), ALU.subtract).then_inc(S["lsh_ready"], 1)
            dve.wait_ge(S["pe_ready"], 1)
            k = mark(dve.tensor_reduce(psum_[:], pe_[:], AX.X, ALU.add))
            src = pe_
            for i in range(2):
                link(dve.tensor_reduce(top[:, i], src[:], AX.X, ALU.max))
                link(tt(eqm[:, i], src[:], over(top[:, i]), ALU.is_equal))
                link(tt(scr[:, i], eqm[:, i], C("idxdesc").unsqueeze(1).broadcast_to([P, NBLK, E]), ALU.mult))
                link(dve.tensor_reduce(first[:, i], scr[:, i], AX.X, ALU.max))
                link(tt(hot[:, i], scr[:, i], over(first[:, i]), ALU.is_equal))
                if i == 0:
                    link(stt(rest[:], hot[:, 0], -2.0, pe_[:], ALU.mult, ALU.add))
                    src = rest
            link(dve.reciprocal(prec[:], psum_[:]))
            link(tt(both[:], hot[:, 0], hot[:, 1], ALU.add))
            link(tt(wgt0[:], both[:], pe_[:], ALU.mult))
            link(tt(wgt[:], wgt0[:], over(prec[:]), ALU.mult))
            m = 0
            for b in range(NBLK):
                for pair in range(E // 2):
                    bank = moe_bank[m % 4]
                    dve.wait_ge(S["moe_done"], m + 1)
                    for i in range(2):
                        e = 2 * pair + i
                        if e > 0:
                            dve.wait_ge(S["moe_used"], E * b + e)
                        ins = stt(acc[:, b], bank[:, i * D:(i + 1) * D], wgt[:, b, e:e + 1],
                                  x2[:, b] if e == 0 else acc[:, b], ALU.mult, ALU.add)
                        ins.then_inc(S["moe_used"], 1)
                    m += 1


def kernel(**inputs):
    import numpy as _np
    import concourse.bacc as _bacc
    from concourse import mybir as _mybir
    from concourse.bass_utils import run_bass_kernel_spmd as _run

    a = {k: _np.asarray(v) for k, v in inputs.items()}

    def tiles(m, n):
        return _np.ascontiguousarray(m.reshape(n, P, -1).transpose(1, 0, 2))

    def columns(v, n):
        return v.reshape(n, P).T

    def taps(m, n):
        return m.reshape(n, P, TAPS).transpose(1, 0, 2).reshape(P, n * TAPS)

    arrays = {
        "x": a["x"].reshape(T, D),
        "ctx": _np.ascontiguousarray(a["ctx_2048"].reshape(-1, CTXD)[:T]),
        "lens": a["mask_BxS2_if0"].reshape(LENS),
        "consts": shape_constants(),
        "cols": _np.ascontiguousarray(_np.concatenate([
            columns(a["L0_xattn_g_res"], 2), columns(a["L0_attn_rms_in_w"], 2), columns(a["L0_attn_o_norm_w"], 1),
            taps(a["L0_attn_conv_q_w"], 2), taps(a["L0_attn_conv_k_w"], 2), taps(a["L0_attn_conv_v_w"], 4)], 1)),
        "rows": _np.concatenate([a["L0_xattn_g_init"][:D], a["L0_attn_ln1_g"], a["L0_attn_ln1_b"],
                                 a["L0_attn_ln2_g"], a["L0_attn_ln2_b"], a["L0_attn_dt_bias"], a["L0_attn_A_log"]]),
        "brow": _np.stack([a["L0_xattn_b_in"], a["L0_attn_b2"]])[None],
        "win": tiles(a["L0_xattn_W_in"].T, 2),
        "wcat": tiles(_np.concatenate([a["L0_attn_Wq"], a["L0_attn_Wk"], a["L0_attn_Wv"], a["L0_attn_Wg"],
                                       a["L0_attn_Wa"], a["L0_attn_Wb"]], 1), 2),
        "wo": tiles(a["L0_attn_Wo"], H),
        "w2": tiles(a["L0_attn_W2"], 2),
        "wr": tiles(a["L0_ffn_Wr"], 2),
        "wit": _np.ascontiguousarray(a["L0_ffn_Wi"].reshape(E, D, 2, P).transpose(3, 0, 2, 1)),
        "fwo": _np.ascontiguousarray(a["L0_ffn_Wo"].reshape(E, 2, P, D).transpose(2, 0, 1, 3)),
    }
    nc = _bacc.Bacc("TRN2", target_bir_lowering=False, num_devices=1)
    args = [nc.dram_tensor(f"in_{k}", v.shape, _mybir.dt.from_np(v.dtype), kind="ExternalInput").ap()
            for k, v in arrays.items()]
    args.append(nc.dram_tensor("out_0", (T, D), _mybir.dt.float32, kind="ExternalOutput").ap())
    program(nc, *args)
    r = _run(nc, [{f"in_{k}": v for k, v in arrays.items()}], core_ids=[0])
    return r.results[0]["out_0"].reshape(1, T, D)
```

```python
import concourse.bass as bass
from concourse import mybir
from contextlib import ExitStack
import numpy as np

T, D, P = 256, 256, 128
H, KD, VD, TAPS = 4, 64, 128, 4
E, LENS, CTXD = 8, 4096, 512
NBLK = T // P
LCOL = LENS // P
LN_EPS, RMS_EPS, QK_EPS = 1e-5, 1e-5, 1e-6
QC, KC, VC, GC, ABC, WCOLS = 0, 256, 512, 1024, 1536, 1544
LEVELS = (2, 4, 8, 16, 32)
ATANH = (1 / 15, 1 / 13, 1 / 11, 1 / 9, 1 / 7, 1 / 5, 1 / 3)

CONST = {}
_at = 0
for _name, _width in (("reset", 3 * LCOL), ("tri_lt", P), ("ident", P), ("iota16", 16), ("scol", 2),
                      ("mask_d", 16), ("mask_lt", 16), ("earlier", E * E), ("headones", 2),
                      ("decay", 3 * P), ("tri_le", P), ("tri_gt", P),
                      ("levels", 64 * (1 + len(LEVELS))), ("ident64", 64)):
    CONST[_name] = (_at, _at + _width)
    _at += _width
NFIRST = CONST["decay"][0]
NCONST = _at
G_RES, RMS_W, O_W, CONV, NCOLS = 0, 2, 4, 5, 5 + 8 * TAPS
R_GINIT, R_BIN, R_LN1G, R_LN1B, R_LN2G, R_LN2B, R_DTB, R_ALOG, NROWS = 0, 256, 512, 768, 1024, 1280, 1536, 1540, 1544


def shape_constants():
    c = np.zeros((P, NCONST), np.float32)

    def put(name, a):
        c[:a.shape[0], CONST[name][0]:CONST[name][1]] = a

    i = np.arange(P)
    put("ident", np.eye(P))
    put("tri_le", i[:, None] <= i[None])
    put("tri_gt", i[:, None] > i[None])
    put("tri_lt", i[:, None] < i[None])
    a, b = -np.expm1(-0.001), np.exp(-0.001)
    t = np.arange(T)
    lag = t[None, :] - t[:, None]
    L = np.where(lag >= 0, b * a ** np.maximum(lag, 0), 0.0)
    put("decay", np.concatenate([L[:P, :P], L[:P, P:], L[P:, P:]], 1))
    j = np.arange(64)
    masks = []
    for m in (1,) + LEVELS:
        up = (j[:, None] // m + 1 == j[None] // m) & (j[:, None] // m % 2 == 0)
        masks.append(np.tile(-up.astype(np.float32), (2, 1)))
    put("levels", np.concatenate(masks, 1))
    put("ident64", np.tile(np.eye(64), (2, 1)))
    put("headones", i[:, None] // KD == np.arange(2)[None])
    put("scol", i[:, None] + 1 + P * np.arange(2)[None])
    put("iota16", np.tile(np.arange(16), (P, 1)))
    put("earlier", np.tile((np.arange(E)[None] < np.arange(E)[:, None]).reshape(-1), (P, 1)))
    put("mask_d", np.eye(16))
    put("mask_lt", np.arange(16)[:, None] < np.arange(16)[None])
    put("reset", np.tile((np.arange(3 * LCOL) % LCOL != 0), (P, 1)))
    return c


def program(nc, A_x, A_ctx, A_lens, A_consts, A_cols, A_rows, A_b2, A_win, A_wcat, A_wo, A_w2, A_wr, A_wit, A_fwo, out):
    f32, f32r, bf16, i32 = mybir.dt.float32, mybir.dt.float32r, mybir.dt.bfloat16, mybir.dt.int32
    ALU, ACT, AX = mybir.AluOpType, mybir.ActivationFunctionType, mybir.AxisListType

    ctx = ExitStack()
    with ctx:
        def sb(name, shape, dt=f32):
            return ctx.enter_context(nc.sbuf_tensor(name, shape, dt))

        def sem(name):
            return ctx.enter_context(nc.semaphore(name))

        def sb_twice(name, later, shape, later_dt):
            with nc.sbuf_tensor(name, shape, f32) as first:
                pass
            return first, sb(later, shape, later_dt)

        x_in = sb("x_in", [P, NBLK, D])
        ctx_in = sb("ctx_in", [P, NBLK, CTXD])
        lens_in = sb("lens_in", [P, LCOL], i32)
        consts = sb("consts", [P, NCONST])
        cols = sb("cols", [P, NCOLS])
        rows = sb("rows", [P, NROWS])
        b2row = sb("b2row", [1, D])
        win = sb("win", [P, 2, D])
        wcat = sb("wcat", [P, 2, WCOLS])
        wo = sb("wo", [P, H, D])
        w2 = sb("w2", [P, 2, D])
        wr = sb("wr", [P, 2, E])
        wit, wphi = sb_twice("wit", "wphi", [P, E, 2, D], f32r)
        fwo, wplo = sb_twice("fwo", "wplo", [P, E, 2, D], f32r)
        ones = sb("ones", [P, P])
        eps = sb("eps", [P, 3])
        warm = sb("warm", [P, 1])

        def C(name, parts=P):
            return consts[0:parts, CONST[name][0]:CONST[name][1]]

        ident = C("ident")

        def level_mask(i, r=slice(0, P)):
            at = CONST["levels"][0] + 64 * i
            return consts[r, at:at + 64].unsqueeze(1).broadcast_to([r.stop - r.start, H, 64])

        st = sb("st", [P, NBLK, 6])
        mv = sb("mv", [P, NBLK, 2])
        sd = sb("sd", [P, NBLK])
        rstd = sb("rstd", [P, NBLK])
        xn = sb("xn", [P, NBLK, D])
        xT = sb("xT", [P, 2, T])
        sqj = sb("sqj", [P, CTXD])
        sqj2 = sb("sqj2", [P, CTXD])
        css = sb("css", [P, NBLK])
        csd = sb("csd", [P, NBLK])
        crs = sb("crs", [P, NBLK])
        cs = sb("cs", [P, NBLK, D])
        dep = sb("dep", [P, NBLK, D])
        limb = sb("limb", [P, 3, LCOL], i32)
        lscan = sb("lscan", [P, 3, LCOL])
        csum = sb("csum", [P, 3, LCOL], i32)
        lo0 = sb("lo0", [P, LCOL], i32)
        ca0 = sb("ca0", [P, LCOL], i32)
        s1_ = sb("s1_", [P, LCOL], i32)
        lo1 = sb("lo1", [P, LCOL], i32)
        ca1 = sb("ca1", [P, LCOL], i32)
        s2_ = sb("s2_", [P, LCOL], i32)
        lo2 = sb("lo2", [P, LCOL], i32)
        tf = sb("tf", [P, 5, LCOL])
        pos = sb("pos", [P, LCOL], i32)
        pos_hi = sb("pos_hi", [P, LCOL], i32)
        pos_lo = sb("pos_lo", [P, LCOL], i32)
        oh_hi = sb("oh_hi", [P, LCOL, 16], bf16)
        oh_lo = sb("oh_lo", [P, LCOL, 16], bf16)
        bound = sb("bound", [16, 16])
        bscan = sb("bscan", [16, 16])
        prer = sb("prer", [16, 16, 16])
        cumr = sb("cumr", [16, 16, 16])
        gT = sb("gT", [P, 2, T], f32r)
        dephi = sb("dephi", [P, NBLK, D], f32r)
        deplo = sb("deplo", [P, NBLK, D], f32r)
        xb = sb("xb", [P, NBLK, D])
        x1 = sb("x1", [P, NBLK, D])

        st1 = sb("st1", [P, NBLK, 6])
        mv1 = sb("mv1", [P, NBLK, 2])
        sd1 = sb("sd1", [P, 2, NBLK])
        rs1 = sb("rs1", [P, 2, NBLK])
        y = sb("y", [P, NBLK, D])
        z0 = sb("z0", [P, NBLK, D])
        z = sb("z", [P, NBLK, D])
        zss = sb("zss", [P, NBLK])
        zsd = sb("zsd", [P, NBLK])
        zrs = sb("zrs", [P, NBLK])
        hh = xn
        hT, x3hi = sb_twice("hT", "x3hi", [P, 2, T], f32r)
        cv = sb("cv", [P, 8, T])
        sv = sb("sv", [P, 8, T])
        vraw = sb("vraw", [P, 2, T])
        vtap = sb("vtap", [P, TAPS - 1, T])
        ksq = sb("ksq", [P, 2, T])
        qsq = ksq
        xa = sb("xa", [P, NBLK, H])
        nx = sb("nx", [P, NBLK, H])
        ea = sb("ea", [P, NBLK, 8])
        ex = sb("ex", [P, NBLK, 8])
        expA = sb("expA", [P, H])
        sp = sb("sp", [P, 6, NBLK, H])
        poly = sb("poly", [P, 9, NBLK, H])
        g = sb("g", [P, NBLK, H])
        gM = sb("gM", [P, NBLK, H, P])
        E1 = sb("E1", [P, H, T])
        E2 = sb("E2", [P, H, P])
        kss = sb("kss", [P, NBLK, H])
        kse = sb("kse", [P, NBLK, H])
        half = sb("half", [P, NBLK, H])
        ksr = sb("ksr", [P, NBLK, H])
        cden = sb("cden", [P, NBLK, H])
        cfac = sb("cfac", [P, NBLK, H])
        AT1 = sb("AT1", [P, H, T])
        AT2 = sb("AT2", [P, H, P])
        PT1 = sb("PT1", [P, H, T])
        PT2 = sb("PT2", [P, H, P])
        Ats = sb("Ats", [P, NBLK, H, P])
        X = sb("X", [P, NBLK, H, 64])
        XT = sb("XT", [P, NBLK, H, 64])
        U = sb("U", [P, NBLK, H, 64])
        U128 = sb("U128", [64, NBLK, H, 64])
        XTF = sb("XTF", [P, NBLK, H, P])
        vp = sb("vp", [P, NBLK, H, VD])
        F = sb("F", [P, NBLK, H, VD])
        R2 = sb("R2", [P, H, VD])
        qe = sb("qe", [P, NBLK, H])
        sg = sb("sg", [P, NBLK, H, VD])
        osq = gM
        oms = sb("oms", [P, NBLK, H])
        omv = sb("omv", [P, NBLK, H])
        osd = sb("osd", [P, NBLK, H])
        ors = sb("ors", [P, NBLK, H])
        og = Ats
        ogT = vp
        base = dep
        st2 = sb("st2", [P, NBLK, 6])
        mv2 = sb("mv2", [P, NBLK, 2])
        sd2 = sb("sd2", [P, NBLK])
        rs2 = sb("rs2", [P, NBLK])
        h0 = z0
        h2 = z
        x3lo = gT
        h2T = xT
        ge = y
        x2 = sb("x2", [P, NBLK, D])

        wp = sb("wp", [P, 2, E, D])
        st3 = sb("st3", [P, NBLK, 6])
        mv3 = sb("mv3", [P, NBLK, 2])
        ve3 = sb("ve3", [P, NBLK])
        rs3 = sb("rs3", [P, NBLK])
        minus_half = sb("minus_half", [P, 1])
        x3 = xn
        wrparts = sb("wrparts", [P, 2, 2, E], f32r)
        lparts = sb("lparts", [P, NBLK, 2, E])
        logits = sb("logits", [P, NBLK, E])
        lmax = sb("lmax", [P, NBLK])
        lsh = sb("lsh", [P, NBLK, E])
        pe_ = sb("pe_", [P, NBLK, E])
        psum_ = sb("psum_", [P, NBLK])
        prec = sb("prec", [P, NBLK])
        equal = sb("equal", [P, NBLK, E, E])
        larger = sb("larger", [P, NBLK, E, E])
        tied = sb("tied", [P, NBLK, E, E])
        before = sb("before", [P, NBLK, E, E])
        rank = sb("rank", [P, NBLK, E])
        wgt0 = sb("wgt0", [P, NBLK, E])
        wgt = sb("wgt", [P, NBLK, E])
        acc = cs
        acc2 = base
        scaled = (z0, z)
        pair_sum = xb

        B = [ctx.enter_context(nc.psum_tensor(f"B{i}", [P, 512], f32)) for i in range(8)]

        names = """ld_x ld_ctx ld_lens ld_consts ld_cols ld_rows ld_b2 ld_win ld_wcat ld_wo ld_w2 ld_wr st_out 
            ones_set eps_set var_a xn_ready cs_ready limbs_summed onehots_ready bounds_ready onehot_t dep_ready dep_split 
            xb_ready x1_copied y_ready z0_ready var_1 z_ready hh_ready xT0 xT1 hT0 hT1 ctx_ss sd_ctx sd_a sd_b sd_z z_ss x_turned dep_done 
            limb_offsets bound_counts cum_rows x1_done hh_turned ab_done gate_done ea_ready exp_a expA_ready 
            decay_mm decay_exp masked_e ksq_ready kse_ready ksr_ready qsq_ready kk_done at_ready a_turned ats_ready 
            x_base0 x_base1 xt_base0 xt_base1 u_done u_ready x_done x_ready xt_ready xt64_done xt64_ready u128_done u128_ready 
            xt128_done xt128_ready xtf_diag v_turned vp_ready qk_done pt_ready qe_ready f_done r_done r_ready 
            o_done osq_ready oms_ready sd_o og_ready og_turned ogt_ready enc_done base_ready var_2 sd_2 h2_ready 
            h2_turned h2t0 h2t1 w2_done gelu_ready x2_ready var_3 rs_3 x3_ready x3_turned x3t0 x3t1 logits_done 
            lsh_ready pe_ready moe_done moe_used wp_split wr_split x3_lo wgt_ready scaled_ready pair_ready wp_done wp_ready dve_step pool_step conv_pool conv_q 
            f_ready0 f_ready1 g_masked0 g_masked1 g_ready gate_mm k0_done k1_done kss_done ld_first pool_set 
            q0_done q1_done qss_done silu_k silu_q silu_v v01_done v23_done v_copied last_tapped conv_k conv_v""".split()
        S = {n: sem(n) for n in names}
        ld_moe = [sem(f"ld_moe{i}") for i in range(4)]
        block = ctx.enter_context(nc.Block())

        tile_bank = {2: B[2], 3: B[3], 0: B[2], 1: B[3], 4: B[4], 5: B[4], 6: B[4], 7: B[4]}
        tile_at = {5: T, 7: T}
        tile_col = {0: QC, 1: QC + P, 2: KC, 3: KC + P, 4: VC, 5: VC + P, 6: VC + 2 * P, 7: VC + 3 * P}
        TAPPED = (2, 3, 0, 1, 5)
        gate_bank = (B[4], B[7])
        small = B[5]
        wp_bank = (B[6], B[7], B[6], B[5], B[0], B[4], B[5], B[3])
        UB, XB = (B[1], B[6]), (B[7], B[0])
        gram_bank = (B[2], B[3])
        cross_bank = (B[4], B[5])
        decay_bank = (B[0], B[1], B[6])
        v_bank = (B[4], B[5])
        f_bank = ((B[7], B[0]), (B[1], B[6]))
        norm_bank = B[2]
        r_bank = (B[1], B[6])
        o_bank = ((B[2], B[3]), (B[4], B[5]))
        turn_bank = (B[7], B[0])
        w2_bank = (B[2], B[3])
        sum_bank = (B[1], B[6])
        moe_bank = (B[1], B[6], B[2], B[3])
        last_bank = (B[3], B[4])
        logit_bank = (B[5], B[4])

        def both_tiles(b):
            return turn_bank[b][:, 0:T].rearrange("p (k t) -> p k t", k=2)

        ACT_PAIR = 1
        SUMS = E - 1

        @block.sync
        def _(sp_):
            sp_.dma_start(x_in[:], A_x.rearrange("(b p) d -> p b d", p=P)).then_inc(S["ld_x"], 16)
            sp_.dma_start(consts[:, 0:NFIRST], A_consts[:, 0:NFIRST]).then_inc(S["ld_first"], 16)
            sp_.dma_start(ctx_in[:], A_ctx.rearrange("(b p) d -> p b d", p=P)).then_inc(S["ld_ctx"], 16)
            sp_.dma_start(win[:], A_win).then_inc(S["ld_win"], 16)
            sp_.dma_start(wit[:, 0:2], A_wit[:, 0:2]).then_inc(ld_moe[0], 16)
            sp_.dma_start(fwo[:, 0:2], A_fwo[:, 0:2]).then_inc(ld_moe[0], 16)
            sp_.dma_start(wcat[:], A_wcat).then_inc(S["ld_wcat"], 16)
            for i in range(1, 4):
                sp_.dma_start(wit[:, 2 * i:2 * i + 2], A_wit[:, 2 * i:2 * i + 2]).then_inc(ld_moe[i], 16)
                sp_.dma_start(fwo[:, 2 * i:2 * i + 2], A_fwo[:, 2 * i:2 * i + 2]).then_inc(ld_moe[i], 16)
            sp_.dma_start(wo[:], A_wo).then_inc(S["ld_wo"], 16)
            sp_.dma_start(w2[:], A_w2).then_inc(S["ld_w2"], 16)
            sp_.dma_start(wr[:], A_wr).then_inc(S["ld_wr"], 16)
            for b in range(NBLK):
                sp_.wait_ge(S["moe_used"], SUMS * (b + 1))
                sp_.dma_start(out[b * P:(b + 1) * P, :], acc[:, b]).then_inc(S["st_out"], 16)
            sp_.wait_ge(S["st_out"], 16 * NBLK)

        @block.gpsimd
        def _(pool):
            n = [0]

            def link(ins):
                ins.then_inc(S["pool_step"], 1)
                n[0] += 1
                pool.wait_ge(S["pool_step"], n[0])

            pool.memset(eps[:, 0:1], RMS_EPS)
            pool.memset(eps[:, 1:2], LN_EPS * LN_EPS)
            pool.memset(eps[:, 2:3], QK_EPS).then_inc(S["eps_set"], 1)
            pool.memset(ones[:], 1.0).then_inc(S["ones_set"], 1)
            pool.memset(minus_half[:], -0.5)
            link(pool.memset(half[:], 0.5))
            for b in range(NBLK):
                pool.memset(XTF[64:P, b, :, 0:64], 0.0).then_inc(S["pool_set"], 1)
                pool.wait_ge(S["pool_set"], b + 1)

            def split(hi, lo, of):
                link(pool.tensor_scalar(hi, of, 1.0, 0.0, ALU.mult, ALU.add))
                return pool.tensor_tensor(lo, of, hi.bitcast(f32), ALU.subtract)

            def split_wp(e):
                pool.wait_ge(S["wp_ready"], e + 1)
                split(wphi[:, e], wplo[:, e], wp[:, :, e]).then_inc(S["wp_split"], 1)

            pool.wait_ge(S["ld_x"], 16)
            pool.wait_ge(S["ld_rows"], 16)
            for b in range(NBLK):
                pool.tensor_tensor(xb[:, b], x_in[:, b], rows[:, R_BIN:R_BIN + D], ALU.add).then_inc(S["xb_ready"], 1)
            for e in range(3):
                split_wp(e)
            for i in range(2):
                pool.wait_ge(S["silu_k"], i + 1)
                pool.tensor_tensor(ksq[:, i], sv[:, 2 + i], sv[:, 2 + i], ALU.mult).then_inc(S["ksq_ready"], 1)
            pool.wait_ge(S["ld_consts"], 16)
            pool.wait_ge(S["g_ready"], 1)
            pool.tensor_tensor(gM[:, 1], C("tri_le").unsqueeze(1).broadcast_to([P, H, P]),
                               g[:, 1].unsqueeze(2).broadcast_to([P, H, P]), ALU.mult).then_inc(S["g_masked1"], 1)

            def convolve(tile, i):
                for lag in range(TAPS):
                    c = CONV + TAPS * tile + TAPS - 1 - lag
                    o = cv[:, tile] if lag == 0 else vtap[:, lag - 1, lag:T]
                    mul = pool.tensor_scalar(o, vraw[:, i, 0:T - lag], cols[:, c:c + 1], 0.0, ALU.mult, ALU.add)
                    link(mul)
                    if lag == 0:
                        continue
                    add = pool.tensor_tensor(cv[:, tile, lag:T], cv[:, tile, lag:T], o, ALU.add)
                    if lag < TAPS - 1:
                        link(add)
                add.then_inc(S["conv_pool"], 1)

            pool.wait_ge(S["at_ready"], 4)
            for i in range(2):
                r = slice(64 * i, 64 * i + 64)
                link(pool.tensor_tensor(U[r, 0], AT1[r, :, r], level_mask(0, r), ALU.mult))
            pool.tensor_tensor(XT[:, 0], U[:, 0], C("ident64").unsqueeze(1).broadcast_to([P, H, 64]), ALU.add)\
                .then_inc(S["xt_base0"], 1)
            pool.wait_ge(S["v_copied"], 1)
            convolve(6, 0)
            pool.wait_ge(S["conv_pool"], 1)
            convolve(7, 1)
            pool.wait_ge(S["kse_ready"], 1)
            pool.tensor_tensor(ksr[:], kse[:], half[:], ALU.pow).then_inc(S["ksr_ready"], 1)
            for b in range(NBLK):
                pool.wait_ge(S["at_ready"], 4 * (b + 1))
                e = E1[:, :, 0:P] if b == 0 else E2[:]
                pool.tensor_tensor(e, e, C("tri_le").unsqueeze(1).broadcast_to([P, H, P]), ALU.mult)\
                    .then_inc(S["masked_e"], 1)
            pool.wait_ge(S["v_copied"], 2)
            pool.wait_ge(S["conv_pool"], 2)
            convolve(4, 0)
            pool.wait_ge(S["ld_wr"], 16)
            split(wrparts[:, :, 0], wrparts[:, :, 1], wr[:]).then_inc(S["wr_split"], 1)
            for e in range(3, 6):
                split_wp(e)
            for b in range(NBLK):
                pool.wait_ge(S["var_3"], b + 1)
                link(pool.tensor_tensor(ve3[:, b:b + 1], mv3[:, b, 1:2], eps[:, 0:1], ALU.add))
                pool.tensor_tensor(rs3[:, b:b + 1], ve3[:, b:b + 1], minus_half[:], ALU.pow).then_inc(S["rs_3"], 1)
            for e in range(6, E):
                split_wp(e)
            for b in range(NBLK):
                pool.wait_ge(S["scaled_ready"], 2 * (b + 1))
                pool.tensor_tensor(pair_sum[:, b], scaled[0][:, b], scaled[1][:, b], ALU.add)\
                    .then_inc(S["pair_ready"], 1)

        @block.scalar
        def _(act):
            act.dma_start(lens_in[:], A_lens.rearrange("(p c) -> p c", p=P)).then_inc(S["ld_lens"], 16)
            act.dma_start(cols[:], A_cols).then_inc(S["ld_cols"], 16)
            act.wait_ge(S["eps_set"], 1)
            act.activation(warm[:], eps[:, 0:1], ACT.Sqrt)
            act.dma_start(consts[:, NFIRST:], A_consts[:, NFIRST:]).then_inc(S["ld_consts"], 16)
            act.dma_start(rows[:], A_rows.partition_broadcast(P)).then_inc(S["ld_rows"], 16)
            act.dma_start(b2row[:], A_b2).then_inc(S["ld_b2"], 16)

            def evac_wp(e):
                act.wait_ge(S["wp_done"], e + 1)
                act.activation(wp[:, :, e], wp_bank[e][:].rearrange("p (m d) -> p m d", m=2), ACT.Copy)\
                    .then_inc(S["wp_ready"], 1)

            act.wait_ge(S["var_a"], 1)
            act.activation(sd[:], mv[:, :, 1], ACT.Sqrt, scale=1.0 + RMS_EPS, bias=eps[:, 1:2]).then_inc(S["sd_a"], 1)
            act.wait_ge(S["ld_ctx"], 16)
            act.activation(sqj[:], ctx_in[:, 0], ACT.Square, accum_out=css[:, 0:1]).then_inc(S["ctx_ss"], 1)
            act.activation(sqj2[:], ctx_in[:, 1], ACT.Square, accum_out=css[:, 1:2]).then_inc(S["ctx_ss"], 1)
            act.wait_ge(S["ctx_ss"], 2)
            act.activation(csd[:], css[:], ACT.Sqrt, scale=1.0 / CTXD, bias=eps[:, 0:1]).then_inc(S["sd_ctx"], 1)
            act.wait_ge(S["x_turned"], 2)
            act.wait_ge(S["ld_cols"], 16)
            act.activation(xT[:, 1], B[1][:, 0:T], ACT.Copy, scale=cols[:, G_RES + 1:G_RES + 2]).then_inc(S["xT1"], 1)
            act.wait_ge(S["dep_ready"], 1)
            act.activation(dephi[:], dep[:], ACT.Copy).then_inc(S["dep_split"], 1)
            act.wait_ge(S["var_1"], 1)
            act.activation(sd1[:, 0], mv1[:, :, 1], ACT.Sqrt, bias=eps[:, 0:1]).then_inc(S["sd_b"], 1)
            act.activation(sd1[:, 1], mv1[:, :, 1], ACT.Sqrt, scale=1.0 + LN_EPS, bias=eps[:, 1:2]).then_inc(S["sd_b"], 1)
            evac_wp(0)
            for b in range(NBLK):
                act.wait_ge(S["z_ready"], b + 1)
                act.activation((sqj if b == 0 else sqj2)[:, 0:D], z[:, b], ACT.Square, accum_out=zss[:, b:b + 1])\
                    .then_inc(S["z_ss"], 1)
            act.wait_ge(S["z_ss"], 2)
            act.activation(zsd[:], zss[:], ACT.Sqrt, scale=1.0 / D, bias=eps[:, 2:3]).then_inc(S["sd_z"], 1)
            for b in range(NBLK):
                act.wait_ge(S["z0_ready"], b + 1)
                act.activation(x1[:, b], B[3 + b][:, 0:D], ACT.Copy).then_inc(S["x1_copied"], 1)
            act.wait_ge(S["hh_turned"], 2)
            act.activation(hT[:, 1], B[1][:, 0:T], ACT.Copy, scale=cols[:, RMS_W + 1:RMS_W + 2]).then_inc(S["hT1"], 1)
            evac_wp(1)
            evac_wp(2)
            act.wait_ge(S["ld_rows"], 16)
            act.activation(expA[:], rows[:, R_ALOG:R_ALOG + H], ACT.Exp).then_inc(S["expA_ready"], 1)

            def last_tap(tile, done):
                act.wait_ge(S[done], 1)
                at = tile_at.get(tile, 0)
                act.activation(cv[:, tile], tile_bank[tile][:, at:at + T], ACT.Copy,
                               scale=cols[:, CONV + TAPS * tile + 3:CONV + TAPS * tile + 4]).then_inc(S["last_tapped"], 1)

            def silu(tile, conv, done):
                act.wait_ge(S[conv[0]], conv[1])
                act.activation(sv[:, tile], cv[:, tile], ACT.Silu).then_inc(S[done], 1)

            act.wait_ge(S["ea_ready"], 1)
            act.activation(ex[:], ea[:], ACT.Exp).then_inc(S["exp_a"], 1)
            last_tap(2, "k0_done")
            last_tap(3, "k1_done")

            def silu_gate(b):
                act.wait_ge(S["gate_mm"], b + 1)
                act.activation(sg[:, b].rearrange("p h v -> p (h v)"), gate_bank[b][:], ACT.Silu)\
                    .then_inc(S["gate_done"], 1)

            def copy_v(i, done):
                act.wait_ge(S[done], 1)
                if i == 1:
                    act.wait_ge(S["conv_pool"], 1)
                act.activation(vraw[:, 0:2 - i].rearrange("p i t -> p (i t)"), B[4][:, 0:(2 - i) * T], ACT.Copy)\
                    .then_inc(S["v_copied"], 1)

            silu_gate(0)
            silu(2, ("conv_k", 1), "silu_k")
            silu(3, ("conv_k", 2), "silu_k")
            silu_gate(1)
            def decay(i, o):
                act.wait_ge(S["decay_mm"], i + 1)
                act.activation(o, decay_bank[i][:].rearrange("p (h t) -> p h t", h=H), ACT.Exp)\
                    .then_inc(S["decay_exp"], 1)

            decay(0, E1[:, :, 0:P])
            decay(1, E2[:])
            copy_v(0, "v23_done")
            for b in range(NBLK):
                act.wait_ge(S["a_turned"], b + 1)
                act.activation(Ats[:, b].rearrange("p h t -> p (h t)"), XB[b][:], ACT.Copy).then_inc(S["ats_ready"], 1)
                if b == 0:
                    decay(2, E1[:, :, P:T])
            last_tap(0, "q0_done")

            for level in range(len(LEVELS)):
                for b in range(NBLK):
                    act.wait_ge(S["x_done"], 2 * level + b + 1)
                    if level == len(LEVELS) - 1:
                        act.wait_ge(S["xt64_done"], b + 1)
                    act.activation(X[:, b].rearrange("p h t -> p (h t)"), XB[b][:, 0:256], ACT.Copy)\
                        .then_inc(S["x_ready"], 1)
                if level == 0:
                    last_tap(1, "q1_done")
                if level == 1:
                    act.activation(warm[:], eps[:, 0:1], ACT.Silu)
                    copy_v(1, "v01_done")
                    last_tap(5, "v01_done")
                if level == 2:
                    silu(0, ("conv_q", 1), "silu_q")
                    silu(1, ("conv_q", 2), "silu_q")
                if level == 3:
                    silu(6, ("conv_pool", 1), "silu_v")
                    silu(7, ("conv_pool", 2), "silu_v")
                    silu(4, ("conv_pool", 3), "silu_v")
                    silu(5, ("conv_v", 1), "silu_v")
                    evac_wp(3)
            act.wait_ge(S["pool_set"], 2)
            for b in range(NBLK):
                act.wait_ge(S["xt64_ready"], b + 1)
                for i in range(2):
                    r = slice(64 * i, 64 * i + 64)
                    ins = act.activation(XTF[r, b, :, r], XT[r, b], ACT.Copy)
                ins.then_inc(S["xtf_diag"], 1)

            def square_o(b):
                for p_ in range(2):
                    act.wait_ge(S["o_done"], 2 * b + p_ + 1)
                    for i in range(2):
                        h = 2 * p_ + i
                        act.activation(osq[:, b, h], o_bank[b][p_][:, i * VD:(i + 1) * VD], ACT.Square,
                                       accum_out=oms[:, b, h:h + 1]).then_inc(S["osq_ready"], 1)

            for b in range(NBLK):
                for p_ in range(2):
                    act.wait_ge(S["f_done"], 2 * b + p_ + 1)
                    act.activation(F[:, b, 2 * p_:2 * p_ + 2].rearrange("p h v -> p (h v)"),
                                   f_bank[b][p_][:, 0:256], ACT.Copy).then_inc(S[f"f_ready{p_}"], 1)
                if b == 0:
                    act.activation(warm[:], eps[:, 0:1], ACT.Sqrt)
            for b in range(NBLK):
                square_o(b)
                act.wait_ge(S["oms_ready"], b + 1)
                act.activation(osd[:, b], omv[:, b], ACT.Sqrt).then_inc(S["sd_o"], 1)
            evac_wp(4)
            for b in range(NBLK):
                act.wait_ge(S["og_turned"], b + 1)
                act.activation(ogT[:, b].rearrange("p h t -> p (h t)"), turn_bank[b][:], ACT.Copy,
                               scale=cols[:, O_W:O_W + 1]).then_inc(S["ogt_ready"], 1)
            for b in range(NBLK):
                act.wait_ge(S["var_2"], b + 1)
                act.activation(sd2[:, b:b + 1], mv2[:, b, 1:2], ACT.Sqrt, bias=eps[:, 0:1]).then_inc(S["sd_2"], 1)
            act.activation(warm[:], eps[:, 0:1], ACT.Gelu)
            act.wait_ge(S["h2_turned"], 2)
            act.activation(h2T[:, :, P:T], both_tiles(1), ACT.Copy).then_inc(S["h2t1"], 1)
            evac_wp(5)
            for b in range(NBLK):
                act.wait_ge(S["w2_done"], b + 1)
                act.activation(ge[:, b], w2_bank[b][:, 0:D], ACT.Gelu).then_inc(S["gelu_ready"], 1)
            act.activation(warm[:], eps[:, 0:1], ACT.Exp)
            evac_wp(6)
            act.wait_ge(S["x3_turned"], 1)
            act.activation(x3hi[:, :, 0:P], both_tiles(0), ACT.Copy).then_inc(S["x3t0"], 1)
            evac_wp(7)
            act.wait_ge(S["lsh_ready"], 1)
            act.activation(pe_[:], lsh[:], ACT.Exp).then_inc(S["pe_ready"], 1)
            act.wait_ge(S["wgt_ready"], 1)
            for b in range(NBLK):
                act.wait_ge(S["moe_done"], E // 2 * b + ACT_PAIR + 1)
                for i in range(2):
                    e = 2 * ACT_PAIR + i
                    act.activation(scaled[i][:, b], moe_bank[ACT_PAIR][:, i * D:(i + 1) * D], ACT.Copy,
                                   scale=wgt[:, b, e:e + 1]).then_inc(S["scaled_ready"], 1)

        @block.tensor
        def _(pe):
            mm = pe.matmul

            def turn_block(src, b, ready, done):
                pe.wait_ge(S[ready], b + 1)
                for k in range(2):
                    ins = pe.transpose(turn_bank[b][:, k * P:(k + 1) * P], src[:, b, k * P:(k + 1) * P], ident)
                ins.then_inc(S[done], 1)

            def turn(src, banks, ready, done):
                for k in range(2):
                    for b in range(NBLK):
                        if k == 0:
                            pe.wait_ge(S[ready], b + 1)
                        ins = pe.transpose(banks[k][:, b * P:(b + 1) * P], src[:, b, k * P:(k + 1) * P], ident)
                    ins.then_inc(S[done], 1)

            def moe_product(e, halves=(0, 1)):
                if e == 2:
                    pe.wait_ge(S["wp_ready"], 1)
                pe.wait_ge(ld_moe[e // 2], 32)
                for m in halves:
                    for k in range(2):
                        ins = mm(wp_bank[e][:, m * D:(m + 1) * D], wit[:, e, k, m * P:(m + 1) * P], fwo[:, e, k],
                                 start=(k == 0), stop=(k == 1))
                if m == 1:
                    ins.then_inc(S["wp_done"], 1)

            pe.wait_ge(S["ld_first"], 16)
            pe.wait_ge(S["limbs_summed"], 1)
            mm(small[:, 0:3], C("tri_lt"), lscan[:, :, LCOL - 1], start=True, stop=True).then_inc(S["limb_offsets"], 1)
            turn(xn, (B[0], B[1]), "xn_ready", "x_turned")
            pe.wait_ge(S["xT0"], 1)
            pe.wait_ge(S["xT1"], 1)
            pe.wait_ge(S["ld_win"], 16)
            for b in range(NBLK):
                for k in range(2):
                    mm(B[3 + b][:, 0:D], xT[:, k, b * P:(b + 1) * P], win[:, k], start=(k == 0), stop=False)
            pe.wait_ge(S["onehots_ready"], 2)
            for i in range(LCOL):
                ins = mm(small[0:16, 0:16], oh_hi[:, i], oh_lo[:, i], start=(i == 0), stop=(i == LCOL - 1))
            ins.then_inc(S["bound_counts"], 1)
            pe.wait_ge(S["ld_consts"], 16)
            pe.wait_ge(S["cs_ready"], 2)
            mm(B[2][:, 0:D], C("decay")[:, 0:P], cs[:, 0], start=True, stop=True)
            mm(B[2][:, D:2 * D], C("decay")[:, P:2 * P], cs[:, 0], start=True, stop=False)
            mm(B[2][:, D:2 * D], C("decay")[:, 2 * P:3 * P], cs[:, 1], start=False, stop=True).then_inc(S["dep_done"], 1)
            pe.wait_ge(S["bounds_ready"], 1)
            mm(small[:, 0:T], ones[0:16, :], cumr[:].rearrange("p a b -> p (a b)"), start=True, stop=True)\
                .then_inc(S["cum_rows"], 1)
            for b in range(NBLK):
                pe.wait_ge(S["xb_ready"], b + 1)
                mm(B[3 + b][:, 0:D], ident, xb[:, b], start=False, stop=False)
            pe.wait_ge(S["onehot_t"], 2)
            for part, d in enumerate((dephi, deplo)):
                pe.wait_ge(S["dep_split"], part + 1)
                for b in range(NBLK):
                    for k in range(2):
                        ins = mm(B[3 + b][:, 0:D], gT[:, k, b * P:(b + 1) * P], d[:, k],
                                 start=False, stop=(part == 1 and k == 1))
                    if part == 1:
                        ins.then_inc(S["x1_done"], 1)
            moe_product(0)
            moe_product(1)

            moe_product(2, (0,))
            turn(hh, (B[0], B[1]), "hh_ready", "hh_turned")
            moe_product(2, (1,))
            pe.wait_ge(S["hT0"], 1)
            pe.wait_ge(S["hT1"], 1)
            pe.wait_ge(S["ld_wcat"], 16)
            for b in range(NBLK):
                for k in range(2):
                    ins = mm(small[:, 8 * b:8 * b + 8], hT[:, k, b * P:(b + 1) * P], wcat[:, k, ABC:ABC + 8],
                             start=(k == 0), stop=(k == 1))
            ins.then_inc(S["ab_done"], 1)

            def project(tile):
                at, c = tile_at.get(tile, 0), tile_col[tile]
                for k in range(2):
                    ins = mm(tile_bank[tile][:, at:at + T], wcat[:, k, c:c + P], hT[:, k], start=(k == 0), stop=(k == 1))
                return ins

            project(2).then_inc(S["k0_done"], 1)
            pe.wait_ge(S["y_ready"], 2)
            project(3).then_inc(S["k1_done"], 1)
            for b in range(NBLK):
                if b == 1:
                    pe.wait_ge(S["wp_ready"], 2)
                for k in range(2):
                    ins = mm(gate_bank[b][:], hT[:, k, b * P:(b + 1) * P], wcat[:, k, GC:GC + H * VD],
                             start=(k == 0), stop=(k == 1))
                ins.then_inc(S["gate_mm"], 1)

            def squares(sq, bank, col, done):
                for b in range(NBLK):
                    for i in range(2):
                        at = col + H * b + 2 * i
                        ins = mm(bank[:, at:at + 2], sq[:, i, b * P:(b + 1) * P], C("headones"), start=True, stop=True)
                ins.then_inc(S[done], 1)

            def gram(a0, done, parities=(0, 1)):
                for odd in parities:
                    r = slice(64 * odd, 64 * odd + 64)
                    for blk in range(NBLK):
                        for i in range(2):
                            at, t = (2 * blk + i) * P, slice(blk * P, (blk + 1) * P)
                            ins = mm(gram_bank[odd][:, at:at + P], sv[r, 2 + i, t], sv[r, a0 + i, t],
                                     start=True, stop=True)
                    ins.then_inc(S[done], 1)

            def cross_gram(a0, done):
                for odd in range(2):
                    r = slice(64 * odd, 64 * odd + 64)
                    for i in range(2):
                        ins = mm(cross_bank[odd][:, i * P:(i + 1) * P], sv[r, 2 + i, 0:P], sv[r, a0 + i, P:T],
                                 start=True, stop=True)
                    ins.then_inc(S[done], 1)

            pe.wait_ge(S["silu_k"], 2)
            gram(2, "kk_done")
            pe.wait_ge(S["g_masked0"], 1)
            mm(decay_bank[0][:], C("tri_gt"), gM[:, 0].rearrange("p h t -> p (h t)"), start=True, stop=True)\
                .then_inc(S["decay_mm"], 1)
            pe.wait_ge(S["ksq_ready"], 2)
            squares(ksq, small, 16, "kss_done")
            pe.wait_ge(S["g_masked1"], 1)
            mm(decay_bank[1][:], C("tri_gt"), gM[:, 1].rearrange("p h t -> p (h t)"), start=True, stop=True)\
                .then_inc(S["decay_mm"], 1)
            pe.wait_ge(S["gate_done"], 1)
            project(6)
            project(7).then_inc(S["v23_done"], 1)

            def turn_a(b):
                pe.wait_ge(S["at_ready"], 4 * (b + 1))
                if b == 0:
                    pe.wait_ge(S["gate_done"], 2)
                for h in range(H):
                    src = AT1[:, h, 0:P] if b == 0 else AT2[:, h]
                    ins = pe.transpose(XB[b][:, h * P:(h + 1) * P], src, ident)
                ins.then_inc(S["a_turned"], 1)

            turn_a(0)
            pe.wait_ge(S["wp_ready"], 3)
            mm(decay_bank[2][:], C("tri_gt"), g[:, 0].unsqueeze(2).broadcast_to([P, H, P]), start=True, stop=False)
            mm(decay_bank[2][:], ones[:], gM[:, 1].rearrange("p h t -> p (h t)"), start=False, stop=True)\
                .then_inc(S["decay_mm"], 1)
            turn_a(1)
            pe.wait_ge(S["kse_ready"], 1)
            pe.wait_ge(S["v_copied"], 1)
            cross_gram(2, "kk_done")

            def tiles64(b, fn):
                for h in range(H):
                    for i in range(2):
                        ins = fn(h, slice(64 * i, 64 * i + 64))
                return ins

            def double_u(level, b):
                if level == 0:
                    pe.wait_ge(S["ats_ready"], b + 1)
                    pe.wait_ge(S[f"xt_base{b}"], 1)
                else:
                    pe.wait_ge(S["xt_ready"], 2 * (level - 1) + b + 1)
                tiles64(b, lambda h, r: mm(UB[b][r, 64 * h:64 * h + 64], Ats[r, b, h, r], XT[r, b, h],
                                           start=True, stop=True)).then_inc(S["u_done"], 1)

            def double_x(level, b):
                pe.wait_ge(S["u_ready"], 2 * level + b + 1)
                tiles64(b, lambda h, r: mm(XB[b][r, 64 * h:64 * h + 64], U[r, b, h], X[r, b, h],
                                           start=False, stop=True, skip_group_check=True))\
                    .then_inc(S["x_done"], 1)

            def turn_v(b):
                pe.wait_ge(S["silu_v"], 4)
                if b == 1:
                    pe.wait_ge(S["wp_ready"], 4)
                for h in range(H):
                    ins = pe.transpose(v_bank[b][:, h * P:(h + 1) * P], sv[:, 4 + h, b * P:(b + 1) * P], ident)
                ins.then_inc(S["v_turned"], 1)

            for level in range(len(LEVELS)):
                for b in range(NBLK):
                    double_u(level, b)
                    if level == 0:
                        pe.wait_ge(S[f"x_base{b}"], 1)
                        mm(XB[b][:, 0:256], ident, X[:, b].rearrange("p h t -> p (h t)"), start=True, stop=True,
                           skip_group_check=True)
                if level == 0:
                    project(0).then_inc(S["q0_done"], 1)
                if level == 1:
                    pe.wait_ge(S["at_ready"], 12)
                    project(4)
                if level == 3:
                    pe.wait_ge(S["silu_q"], 2)
                    gram(0, "qk_done", (0,))
                if level == 4:
                    turn_v(0)
                for b in range(NBLK):
                    double_x(level, b)
                    if level == len(LEVELS) - 1:
                        tiles64(b, lambda h, r: mm(UB[b][r, 256 + 64 * h:256 + 64 * h + 64], X[r, b, h], U[r, b, h],
                                                   start=True, stop=True)).then_inc(S["xt64_done"], 1)
                if level == 0:
                    project(1).then_inc(S["q1_done"], 1)
                if level == 1:
                    project(5).then_inc(S["v01_done"], 1)
                if level == 2:
                    moe_product(3, (0,))
                if level == 3:
                    moe_product(3, (1,))
            def last_u(b):
                pe.wait_ge(S["xt64_ready"], b + 1)
                for h in range(H):
                    ins = mm(UB[b][0:64, 64 * h:64 * h + 64], Ats[64:P, b, h, 0:64], XT[64:P, b, h],
                             start=True, stop=True)
                ins.then_inc(S["u128_done"], 1)

            last_u(0)
            turn_v(1)
            last_u(1)
            for b in range(NBLK):
                pe.wait_ge(S["u128_ready"], b + 1)
                pe.wait_ge(S["x_ready"], 2 * len(LEVELS) - 1 + b)
                for h in range(H):
                    ins = mm(UB[b][0:64, 256 + 64 * h:256 + 64 * h + 64], X[0:64, b, h], U128[:, b, h],
                             start=True, stop=True)
                ins.then_inc(S["xt128_done"], 1)
            pe.wait_ge(S["qsq_ready"], 2)
            pe.wait_ge(S["pt_ready"], 4)
            squares(qsq, norm_bank, 0, "qss_done")

            def heads(banks, p_, lhs, rhs, start=True, stop=True):
                for i in range(2):
                    h = 2 * p_ + i
                    ins = mm(banks[p_][:, i * VD:(i + 1) * VD], lhs(h), rhs[:, h], start=start, stop=stop,
                             skip_group_check=True)
                return ins

            pe.wait_ge(S["xt128_ready"], 1)
            pe.wait_ge(S["xtf_diag"], 1)
            pe.wait_ge(S["x_ready"], 2 * len(LEVELS))
            pe.wait_ge(S["vp_ready"], 1)
            for p_ in range(2):
                heads(f_bank[0], p_, lambda h: XTF[:, 0, h], vp[:, 0]).then_inc(S["f_done"], 1)
            gram(0, "qk_done", (1,))
            pe.wait_ge(S["xt128_ready"], 2)
            for p_ in range(2):
                pe.wait_ge(S[f"f_ready{p_}"], 1)
                heads(r_bank, p_, lambda h: AT1[:, h, P:T], F[:, 0]).then_inc(S["r_done"], 1)
            pe.wait_ge(S["vp_ready"], 2)
            cross_gram(0, "qk_done")
            pe.wait_ge(S["xtf_diag"], 2)
            pe.wait_ge(S["xt128_ready"], 2)
            for p_ in range(2):
                pe.wait_ge(S["r_ready"], p_ + 1)
                heads(f_bank[1], p_, lambda h: XTF[:, 1, h], R2).then_inc(S["f_done"], 1)
            pe.wait_ge(S["pt_ready"], 8)
            pe.wait_ge(S["qe_ready"], 1)
            for p_ in range(2):
                heads(o_bank[0], p_, lambda h: PT1[:, h, 0:P], F[:, 0]).then_inc(S["o_done"], 1)
            pe.wait_ge(S["pt_ready"], 12)
            for p_ in range(2):
                pe.wait_ge(S[f"f_ready{p_}"], 2)
                for i in range(2):
                    h = 2 * p_ + i
                    o = o_bank[1][p_][:, i * VD:(i + 1) * VD]
                    mm(o, PT1[:, h, P:T], F[:, 0, h], start=True, stop=False, skip_group_check=True)
                    ins = mm(o, PT2[:, h], F[:, 1, h], start=False, stop=True, skip_group_check=True)
                ins.then_inc(S["o_done"], 1)
            moe_product(4)
            for b in range(NBLK):
                pe.wait_ge(S["og_ready"], 4 * (b + 1))
                if b == 1:
                    pe.wait_ge(S["wp_ready"], 5)
                for h in range(H):
                    ins = pe.transpose(turn_bank[b][:, h * P:(h + 1) * P], og[:, b, h], ident)
                ins.then_inc(S["og_turned"], 1)
                if b == 0:
                    for c in range(NBLK):
                        mm(sum_bank[c][:, 0:D], ident, y[:, c], start=True, stop=False)
            pe.wait_ge(S["ld_wo"], 16)
            for b in range(NBLK):
                pe.wait_ge(S["ogt_ready"], b + 1)
                for h in range(H):
                    ins = mm(sum_bank[b][:, 0:D], ogT[:, b, h], wo[:, h], start=False, stop=(h == H - 1))
                ins.then_inc(S["enc_done"], 1)

            def add_b2(b):
                mm(w2_bank[b][:, 0:D], ones[0:1, :], b2row[:], start=True, stop=False)

            def product_w2(b):
                pe.wait_ge(S[f"h2t{b}"], 1)
                for k in range(2):
                    ins = mm(w2_bank[b][:, 0:D], h2T[:, k, b * P:(b + 1) * P], w2[:, k], start=False, stop=(k == 1))
                ins.then_inc(S["w2_done"], 1)

            pe.wait_ge(S["ones_set"], 1)
            pe.wait_ge(S["ld_b2"], 16)
            pe.wait_ge(S["ld_w2"], 16)
            moe_product(5, (0,))
            turn_block(h2, 0, "h2_ready", "h2_turned")
            moe_product(5, (1,))
            add_b2(0)
            turn_block(h2, 1, "h2_ready", "h2_turned")
            product_w2(0)
            add_b2(1)
            product_w2(1)
            moe_product(6)
            pe.wait_ge(S["gelu_ready"], 2)
            moe_product(7, (0,))

            turn_block(x3, 0, "x3_ready", "x3_turned")
            moe_product(7, (1,))
            turn_block(x3, 1, "x3_ready", "x3_turned")

            def expert_pair(b, pair, x, wts, start=False, stop=False):
                for k in range(2):
                    ins = mm(moe_bank[pair][:].rearrange("p (e d) -> p e d", e=2), x[:, k, b * P:(b + 1) * P],
                             wts[:, 2 * pair:2 * pair + 2, k], start=(start and k == 0), stop=(stop and k == 1))
                return ins

            for b in range(NBLK):
                pe.wait_ge(S[f"x3t{b}"], 1)
                for pair in range(E // 2):
                    if b == 0:
                        pe.wait_ge(S["wp_split"], 2 * pair + 2)
                    elif pair == ACT_PAIR:
                        pe.wait_ge(S["scaled_ready"], 2)
                    else:
                        pe.wait_ge(S["moe_used"], (2, None, 4, 6)[pair])
                    if (b, pair) == (1, 3):
                        for i in range(2):
                            parts = [(k, x, wts) for x, wts in ((x3hi, wphi), (x3hi, wplo), (x3lo, wphi))
                                     for k in range(2)]
                            for j, (k, x, wts) in enumerate(parts):
                                ins = mm(last_bank[i][:, 0:D], x[:, k, b * P:(b + 1) * P], wts[:, 2 * pair + i, k],
                                         start=(j == 0), stop=(j == 5))
                            ins.then_inc(S["moe_done"], 1)
                        continue
                    expert_pair(b, pair, x3hi, wphi, start=True)
                    expert_pair(b, pair, x3hi, wplo)
                    if b == 0 and pair == 0:
                        pe.wait_ge(S["wr_split"], 1)
                        pe.wait_ge(S["wp_ready"], 7)
                        pe.wait_ge(S["x3t1"], 1)
                        for x, width in ((x3hi, 2 * E), (x3lo, E)):
                            if x is x3lo:
                                pe.wait_ge(S["x3_lo"], 2)
                            for c in range(NBLK):
                                for k in range(2):
                                    ins = mm(logit_bank[c][:, 0:width], x[:, k, c * P:(c + 1) * P],
                                             wrparts[:, k].rearrange("p x e -> p (x e)")[:, 0:width],
                                             start=(x is x3hi and k == 0), stop=(k == 1), skip_group_check=True)
                        ins.then_inc(S["logits_done"], 1)
                    expert_pair(b, pair, x3lo, wphi, stop=True).then_inc(S["moe_done"], 1)

        @block.vector
        def _(dve):
            n = [0]

            def mark(ins):
                ins.then_inc(S["dve_step"], 1)
                n[0] += 1
                return n[0]

            def need(k):
                dve.wait_ge(S["dve_step"], k)

            def link(ins):
                need(mark(ins))

            ts, tt, stt = dve.tensor_scalar, dve.tensor_tensor, dve.scalar_tensor_tensor

            dve.wait_ge(S["ld_x"], 16)
            for b in range(NBLK):
                k = mark(dve.bn_stats(st[:, b], x_in[:, b]))
            dve.wait_ge(S["ld_lens"], 16)
            ts(limb[:, 0], lens_in[:], 2047, None, ALU.bitwise_and)
            need(k)
            dve.bn_aggr(mv[:, 0], st[:, 0])
            dve.bn_aggr(mv[:, 1], st[:, 1]).then_inc(S["var_a"], 1)
            ts(limb[:, 1], lens_in[:], 11, 2047, ALU.logical_shift_right, ALU.bitwise_and)
            k = mark(ts(limb[:, 2], lens_in[:], 22, 1023, ALU.logical_shift_right, ALU.bitwise_and))
            dve.wait_ge(S["ld_first"], 16)
            need(k)
            dve.tensor_tensor_scan(lscan[:].rearrange("p l c -> p (l c)"), C("reset"),
                                   limb[:].rearrange("p l c -> p (l c)"), 0.0, ALU.mult, ALU.add)\
                .then_inc(S["limbs_summed"], 1)
            dve.wait_ge(S["sd_a"], 1)
            link(dve.reciprocal(rstd[:], sd[:]))
            dve.wait_ge(S["var_a"], 1)
            ts(xn[:, 0], x_in[:, 0], mv[:, 0, 0:1], rstd[:, 0:1], ALU.subtract, ALU.mult).then_inc(S["xn_ready"], 1)
            dve.wait_ge(S["limb_offsets"], 1)
            dve.wait_ge(S["limbs_summed"], 1)
            k = mark(tt(csum[:], lscan[:], small[:, 0:3].unsqueeze(2).broadcast_to([P, 3, LCOL]), ALU.add))
            ts(xn[:, 1], x_in[:, 1], mv[:, 1, 0:1], rstd[:, 1:2], ALU.subtract, ALU.mult).then_inc(S["xn_ready"], 1)
            need(k)
            k = mark(ts(ca0[:], csum[:, 0], 11, None, ALU.logical_shift_right))
            ts(lo0[:], csum[:, 0], 2047, None, ALU.bitwise_and)
            need(k)
            k = mark(tt(s1_[:], csum[:, 1], ca0[:], ALU.add))
            need(k)
            k = mark(ts(ca1[:], s1_[:], 11, None, ALU.logical_shift_right))
            ts(lo1[:], s1_[:], 2047, None, ALU.bitwise_and)
            need(k)
            k = mark(tt(s2_[:], csum[:, 2], ca1[:], ALU.add))
            dve.wait_ge(S["x_turned"], 1)
            dve.wait_ge(S["ld_cols"], 16)
            ts(xT[:, 0], B[0][:, 0:T], cols[:, G_RES:G_RES + 1], None, ALU.mult).then_inc(S["xT0"], 1)
            need(k)
            link(ts(lo2[:], s2_[:], 1023, None, ALU.bitwise_and))
            link(ts(tf[:, 0], lo2[:], 512.0, -1024.0, ALU.is_ge, ALU.mult))
            link(tt(tf[:, 1], tf[:, 0], lo2[:], ALU.add))
            link(stt(tf[:, 2], tf[:, 1], 2048.0, lo1[:], ALU.mult, ALU.add))
            link(stt(tf[:, 3], tf[:, 2], 2048.0, lo0[:], ALU.mult, ALU.add))
            link(ts(tf[:, 4], tf[:, 3], 0.0, float(T), ALU.is_le, ALU.mult))
            link(stt(tf[:, 0], tf[:, 3], -1.0, tf[:, 4], ALU.add, ALU.add))
            link(ts(pos[:], tf[:, 0], float(2 * T), -1.0, ALU.min, ALU.max))
            ts(pos_hi[:], pos[:], 4, None, ALU.arith_shift_right)
            link(ts(pos_lo[:], pos[:], 15, None, ALU.bitwise_and))
            for oh, p_ in ((oh_hi, pos_hi), (oh_lo, pos_lo)):
                tt(oh[:], p_[:].unsqueeze(2).broadcast_to([P, LCOL, 16]),
                   C("iota16").unsqueeze(1).broadcast_to([P, LCOL, 16]), ALU.is_equal).then_inc(S["onehots_ready"], 1)
            dve.wait_ge(S["sd_ctx"], 1)
            link(dve.reciprocal(crs[:], csd[:]))
            for b in range(NBLK):
                ts(cs[:, b], ctx_in[:, b, 0:D], crs[:, b:b + 1], None, ALU.mult).then_inc(S["cs_ready"], 1)
            dve.wait_ge(S["bound_counts"], 1)
            link(ts(bound[:], small[0:16, 0:16], 1.0, None, ALU.min))
            dve.wait_ge(S["ones_set"], 1)
            link(dve.tensor_tensor_scan(bscan[:], ones[0:16, 0:16], bound[:], 0.0, ALU.mult, ALU.add))
            link(tt(prer[:], bscan[:].unsqueeze(1).broadcast_to([16, 16, 16]),
                    C("mask_d", 16).unsqueeze(2).broadcast_to([16, 16, 16]), ALU.mult))
            stt(cumr[:], C("mask_lt", 16).unsqueeze(2).broadcast_to([16, 16, 16]), bscan[:, 15:16], prer[:],
                ALU.mult, ALU.add).then_inc(S["bounds_ready"], 1)
            dve.wait_ge(S["dep_done"], 1)
            dve.wait_ge(S["ld_rows"], 16)
            tt(dep[:], B[2][:].rearrange("p (b d) -> p b d", b=2),
               rows[:, R_GINIT:R_GINIT + D].unsqueeze(1).broadcast_to([P, 2, D]), ALU.mult).then_inc(S["dep_ready"], 1)
            dve.wait_ge(S["cum_rows"], 1)
            for k in range(2):
                ts(gT[:, k], small[:, 0:T], 1.0, C("scol")[:, k:k + 1], ALU.max, ALU.is_equal)\
                    .then_inc(S["onehot_t"], 1)
            dve.wait_ge(S["dep_split"], 1)
            dve.wait_ge(S["dep_ready"], 1)
            tt(deplo[:], dep[:], dephi[:].bitcast(f32), ALU.subtract).then_inc(S["dep_split"], 1)
            for b in range(NBLK):
                dve.wait_ge(S["x1_done"], b + 1)
                k = mark(dve.bn_stats(st1[:, b], B[3 + b][:, 0:D]))
            need(k)
            dve.bn_aggr(mv1[:, 0], st1[:, 0])
            dve.bn_aggr(mv1[:, 1], st1[:, 1]).then_inc(S["var_1"], 1)
            dve.wait_ge(S["var_1"], 1)
            for b in range(NBLK):
                stt(z0[:, b], B[3 + b][:, 0:D], mv1[:, b, 0:1], rows[:, R_LN1G:R_LN1G + D], ALU.subtract, ALU.mult)\
                    .then_inc(S["z0_ready"], 1)
            dve.wait_ge(S["sd_b"], 2)
            link(dve.reciprocal(rs1[:], sd1[:]))
            for b in range(NBLK):
                dve.wait_ge(S["z0_ready"], b + 1)
                stt(z[:, b], z0[:, b], rs1[:, 1, b:b + 1], rows[:, R_LN1B:R_LN1B + D], ALU.mult, ALU.add)\
                    .then_inc(S["z_ready"], 1)
            dve.wait_ge(S["sd_z"], 1)
            link(dve.reciprocal(zrs[:], zsd[:]))
            dve.wait_ge(S["z_ready"], 2)
            for b in range(NBLK):
                ts(hh[:, b], z[:, b], zrs[:, b:b + 1], None, ALU.mult).then_inc(S["hh_ready"], 1)
            dve.wait_ge(S["hh_turned"], 1)
            ts(hT[:, 0], B[0][:, 0:T], cols[:, RMS_W:RMS_W + 1], None, ALU.mult).then_inc(S["hT0"], 1)
            for b in range(NBLK):
                dve.wait_ge(S["x1_copied"], b + 1)
                ts(y[:, b], B[3 + b][:, 0:D], mv1[:, b, 0:1], rs1[:, 0, b:b + 1], ALU.subtract, ALU.mult)\
                    .then_inc(S["y_ready"], 1)
            dve.wait_ge(S["ab_done"], 1)
            ab = small[:, 0:16].rearrange("p (b c) -> p b c", b=NBLK)
            k = mark(tt(xa[:], ab[:, :, 0:H], rows[:, R_DTB:R_DTB + H].unsqueeze(1).broadcast_to([P, NBLK, H]), ALU.add))
            ts(ea[:, :, H:2 * H], ab[:, :, H:2 * H], -1.0, None, ALU.mult)
            need(k)
            link(ts(nx[:], xa[:], -1.0, None, ALU.mult))
            tt(ea[:, :, 0:H], xa[:], nx[:], ALU.min).then_inc(S["ea_ready"], 1)

            tap_at = {}

            def tap(tile, lag, done=None):
                if lag == 1:
                    dve.wait_ge(S["last_tapped"], TAPPED.index(tile) + 1)
                else:
                    need(tap_at[tile])
                c, at = CONV + TAPS * tile + TAPS - 1 - lag, tile_at.get(tile, 0)
                ins = stt(cv[:, tile, lag:T], tile_bank[tile][:, at:at + T - lag], cols[:, c:c + 1], cv[:, tile, lag:T],
                          ALU.mult, ALU.add)
                if lag < TAPS - 1:
                    tap_at[tile] = mark(ins)
                else:
                    ins.then_inc(S[done], 1)

            dve.wait_ge(S["exp_a"], 1)
            k = mark(ts(sp[:, 0], ex[:, :, 0:H], 2.0, None, ALU.add))
            ts(sp[:, 4], xa[:], 0.0, None, ALU.max)
            need(k)
            k = mark(dve.reciprocal(sp[:, 1], sp[:, 0]))
            tap(2, 1)
            need(k)
            k = mark(tt(sp[:, 2], ex[:, :, 0:H], sp[:, 1], ALU.mult))
            tap(3, 1)
            need(k)
            k = mark(tt(sp[:, 3], sp[:, 2], sp[:, 2], ALU.mult))
            tap(2, 2)
            need(k)
            k = mark(ts(poly[:, 0], sp[:, 3], ATANH[0], None, ALU.mult))
            tap(3, 2)
            need(k)
            k = mark(stt(poly[:, 1], poly[:, 0], ATANH[1], sp[:, 3], ALU.add, ALU.mult))
            tap(2, 3, "conv_k")
            need(k)
            k = mark(stt(poly[:, 2], poly[:, 1], ATANH[2], sp[:, 3], ALU.add, ALU.mult))
            tap(3, 3, "conv_k")
            need(k)
            for i in range(3, len(ATANH)):
                link(stt(poly[:, i], poly[:, i - 1], ATANH[i], sp[:, 3], ALU.add, ALU.mult))
            link(stt(poly[:, 7], poly[:, 6], 1.0, sp[:, 2], ALU.add, ALU.mult))
            link(stt(sp[:, 5], poly[:, 7], 2.0, sp[:, 4], ALU.mult, ALU.add))
            dve.wait_ge(S["expA_ready"], 1)
            stt(g[:], sp[:, 5], -1.0, expA[:].unsqueeze(1).broadcast_to([P, NBLK, H]), ALU.mult, ALU.mult)\
                .then_inc(S["g_ready"], 1)
            dve.wait_ge(S["g_ready"], 1)
            tt(gM[:, 0], C("tri_le").unsqueeze(1).broadcast_to([P, H, P]),
               g[:, 0].unsqueeze(2).broadcast_to([P, H, P]), ALU.mult).then_inc(S["g_masked0"], 1)
            dve.wait_ge(S["kss_done"], 1)
            ts(kse[:], small[:, 16:24].rearrange("p (b h) -> p b h", b=NBLK), QK_EPS, None, ALU.add)\
                .then_inc(S["kse_ready"], 1)
            dve.wait_ge(S["kse_ready"], 1)
            link(stt(cden[:], ex[:, :, H:2 * H], 1.0, kse[:], ALU.add, ALU.mult))
            link(dve.reciprocal(cfac[:], cden[:]))

            def scale_gram(blk, done, o, ready, parities=(0, 1)):
                dve.wait_ge(S[done], parities[-1] + 1)
                for h in range(parities[0], H, 3 - len(parities)):
                    at = (2 * blk + h // 2) * P
                    stt(o[:, h, 0:P], gram_bank[h % 2][:, at:at + P], cfac[:, blk, h:h + 1],
                        (E1, E2)[blk][:, h, 0:P], ALU.mult, ALU.mult).then_inc(S[ready], 1)

            def scale_cross(done, o, ready):
                dve.wait_ge(S[done], 4)
                for h in range(H):
                    at = h // 2 * P
                    stt(o[:, h, P:T], cross_bank[h % 2][:, at:at + P], cfac[:, 0, h:h + 1],
                        E1[:, h, P:T], ALU.mult, ALU.mult).then_inc(S[ready], 1)

            for b in range(NBLK):
                dve.wait_ge(S["decay_exp"], b + 1)
                scale_gram(b, "kk_done", (AT1, AT2)[b], "at_ready")
            dve.wait_ge(S["at_ready"], 8)
            for i in range(2):
                r = slice(64 * i, 64 * i + 64)
                k = mark(tt(U[r, 1], AT2[r, :, r], level_mask(0, r), ALU.mult))
            need(k)
            tt(XT[:, 1], U[:, 1], C("ident64").unsqueeze(1).broadcast_to([P, H, 64]), ALU.add)\
                .then_inc(S["xt_base1"], 1)
            for b in range(NBLK):
                dve.wait_ge(S[f"xt_base{b}"], 1)
                dve.transpose(X[:, b].rearrange("p h t -> p (h t)"),
                              XT[:, b].rearrange("p h t -> p (h t)")).then_inc(S[f"x_base{b}"], 1)

            def turned_v(b):
                dve.wait_ge(S["v_turned"], b + 1)
                tt(vp[:, b], v_bank[b][:].rearrange("p (h v) -> p h v", h=H),
                   ksr[:, b].unsqueeze(2).broadcast_to([P, H, VD]), ALU.mult).then_inc(S["vp_ready"], 1)

            for level in range(len(LEVELS)):
                last = level == len(LEVELS) - 1
                for b in range(NBLK):
                    dve.wait_ge(S["u_done"], 2 * level + b + 1)
                    if level >= 1:
                        dve.wait_ge(S["x_done"], 2 * (level - 1) + b + 1)
                    else:
                        dve.wait_ge(S[f"x_base{b}"], 1)
                    tt(U[:, b], UB[b][:, 0:256].rearrange("p (h t) -> p h t", h=H), level_mask(level + 1), ALU.mult)\
                        .then_inc(S["u_ready"], 1)
                if level == 0:
                    dve.wait_ge(S["decay_exp"], 3)
                    scale_cross("kk_done", AT1, "at_ready")
                if level == 1:
                    for lag in (1, 2):
                        tap(0, lag)
                        tap(1, lag)
                if level == 2:
                    tap(0, 3, "conv_q")
                    tap(1, 3, "conv_q")
                    tap(5, 1)
                if level == 3:
                    tap(5, 2)
                    tap(5, 3, "conv_v")
                if last:
                    dve.wait_ge(S["masked_e"], 2)
                    for blk in range(NBLK):
                        scale_gram(blk, "qk_done", (PT1, PT2)[blk], "pt_ready", (0,))
                    dve.wait_ge(S["ksr_ready"], 1)
                    turned_v(0)
                for b in range(NBLK):
                    if not last:
                        dve.wait_ge(S["x_ready"], 2 * level + b + 1)
                        dve.transpose(XT[:, b].rearrange("p h t -> p (h t)"),
                                      X[:, b].rearrange("p h t -> p (h t)")).then_inc(S["xt_ready"], 1)
                    else:
                        dve.wait_ge(S["xt64_done"], b + 1)
                        for i in range(2):
                            r = slice(64 * i, 64 * i + 32)
                            ins = dve.tensor_copy(XT[r, b, :, 32:64],
                                                  UB[b][r, 256:512].rearrange("p (h t) -> p h t", h=H)[:, :, 32:64])
                        ins.then_inc(S["xt64_ready"], 1)
                if level == 3:
                    for i in range(2):
                        dve.wait_ge(S["silu_q"], i + 1)
                        tt(qsq[:, i], sv[:, i], sv[:, i], ALU.mult).then_inc(S["qsq_ready"], 1)
            for b in range(NBLK):
                dve.wait_ge(S["u128_done"], b + 1)
                ts(U128[:, b], UB[b][0:64, 0:256].rearrange("p (h t) -> p h t", h=H), -1.0, None, ALU.mult)\
                    .then_inc(S["u128_ready"], 1)
            for b in range(NBLK):
                dve.wait_ge(S["xt128_done"], b + 1)
                dve.tensor_copy(XTF[0:64, b, :, 64:P], UB[b][0:64, 256:512].rearrange("p (h t) -> p h t", h=H))\
                    .then_inc(S["xt128_ready"], 1)
            dve.wait_ge(S["qss_done"], 1)
            ts(qe[:], norm_bank[:, 0:8].rearrange("p (b h) -> p b h", b=NBLK), QK_EPS, QK_EPS * KD, ALU.add,
               ALU.mult).then_inc(S["qe_ready"], 1)
            turned_v(1)
            scale_gram(0, "qk_done", PT1, "pt_ready", (1,))
            dve.wait_ge(S["vp_ready"], 2)
            for p_ in range(2):
                dve.wait_ge(S["r_done"], p_ + 1)
                tt(R2[:, 2 * p_:2 * p_ + 2], vp[:, 1, 2 * p_:2 * p_ + 2],
                   r_bank[p_][:, 0:256].rearrange("p (h v) -> p h v", h=2), ALU.subtract).then_inc(S["r_ready"], 1)
            scale_gram(1, "qk_done", PT2, "pt_ready", (1,))
            scale_cross("qk_done", PT1, "pt_ready")
            dve.wait_ge(S["qe_ready"], 1)
            dve.wait_ge(S["gate_done"], 2)
            for b in range(NBLK):
                dve.wait_ge(S["osq_ready"], 4 * (b + 1))
                stt(omv[:, b], oms[:, b], 1.0 / VD, qe[:, b], ALU.mult, ALU.add).then_inc(S["oms_ready"], 1)
                dve.wait_ge(S["sd_o"], b + 1)
                link(dve.reciprocal(ors[:, b], osd[:, b]))
                for h in range(H):
                    stt(og[:, b, h], o_bank[b][h // 2][:, h % 2 * VD:(h % 2 + 1) * VD], ors[:, b, h:h + 1], sg[:, b, h],
                        ALU.mult, ALU.mult).then_inc(S["og_ready"], 1)
            for b in range(NBLK):
                w = sum_bank[b][:, 0:D]
                dve.wait_ge(S["enc_done"], b + 1)
                link(dve.bn_stats(st2[:, b], w))
                dve.bn_aggr(mv2[:, b], st2[:, b]).then_inc(S["var_2"], 1)
                dve.wait_ge(S["var_2"], b + 1)
                stt(h0[:, b], w, mv2[:, b, 0:1], rows[:, R_LN2G:R_LN2G + D], ALU.subtract, ALU.mult)
                dve.wait_ge(S["sd_2"], b + 1)
                link(dve.reciprocal(rs2[:, b:b + 1], sd2[:, b:b + 1]))
                stt(h2[:, b], h0[:, b], rs2[:, b:b + 1], rows[:, R_LN2B:R_LN2B + D], ALU.mult, ALU.add)\
                    .then_inc(S["h2_ready"], 1)
            for b in range(NBLK):
                if b == 0:
                    dve.wait_ge(S["h2_turned"], 1)
                    dve.tensor_copy(h2T[:, :, 0:P], both_tiles(0)).then_inc(S["h2t0"], 1)
                tt(base[:, b], sum_bank[b][:, 0:D], x1[:, b], ALU.add).then_inc(S["base_ready"], 1)
            dve.wait_ge(S["base_ready"], 2)
            for b in range(NBLK):
                dve.wait_ge(S["gelu_ready"], b + 1)
                tt(x2[:, b], ge[:, b], base[:, b], ALU.add).then_inc(S["x2_ready"], 1)
                dve.wait_ge(S["x2_ready"], b + 1)
                link(dve.bn_stats(st3[:, b], x2[:, b]))
                dve.bn_aggr(mv3[:, b], st3[:, b]).then_inc(S["var_3"], 1)
            for b in range(NBLK):
                dve.wait_ge(S["var_3"], b + 1)
                dve.wait_ge(S["rs_3"], b + 1)
                ts(x3[:, b], x2[:, b], mv3[:, b, 0:1], rs3[:, b:b + 1], ALU.subtract, ALU.mult)\
                    .then_inc(S["x3_ready"], 1)
            for b in range(NBLK):
                t = slice(b * P, (b + 1) * P)
                if b == 1:
                    dve.wait_ge(S["x3_turned"], 2)
                    dve.tensor_copy(x3hi[:, :, t], both_tiles(1)).then_inc(S["x3t1"], 1)
                dve.wait_ge(S[f"x3t{b}"], 1)
                tt(x3lo[:, :, t], both_tiles(b), x3hi[:, :, t].bitcast(f32), ALU.subtract).then_inc(S["x3_lo"], 1)

            def over(a):
                return a.unsqueeze(2).broadcast_to([P, NBLK, E])

            dve.wait_ge(S["logits_done"], 1)
            for b in range(NBLK):
                k = mark(dve.tensor_copy(lparts[:, b].rearrange("p x e -> p (x e)"), logit_bank[b][:, 0:2 * E]))
            need(k)
            link(tt(logits[:], lparts[:, :, 0], lparts[:, :, 1], ALU.add))
            link(dve.tensor_reduce(lmax[:], logits[:], AX.X, ALU.max))
            tt(lsh[:], logits[:], over(lmax[:]), ALU.subtract).then_inc(S["lsh_ready"], 1)
            dve.wait_ge(S["pe_ready"], 1)
            other = pe_[:].unsqueeze(2).broadcast_to([P, NBLK, E, E])
            own = pe_[:].unsqueeze(3).broadcast_to([P, NBLK, E, E])
            dve.tensor_reduce(psum_[:], pe_[:], AX.X, ALU.add)
            k = mark(tt(equal[:], other, own, ALU.is_equal))
            tt(larger[:], other, own, ALU.is_gt)
            need(k)
            k = mark(tt(tied[:], equal[:], C("earlier").rearrange("p (e j) -> p e j", e=E).unsqueeze(1)
                        .broadcast_to([P, NBLK, E, E]), ALU.mult))
            dve.reciprocal(prec[:], psum_[:])
            need(k)
            link(tt(before[:], larger[:], tied[:], ALU.add))
            link(dve.tensor_reduce(rank[:], before[:], AX.X, ALU.add))
            link(stt(wgt0[:], rank[:], 2.0, pe_[:], ALU.is_lt, ALU.mult))
            tt(wgt[:], wgt0[:], over(prec[:]), ALU.mult).then_inc(S["wgt_ready"], 1)
            dve.wait_ge(S["wgt_ready"], 1)
            n_sums = 0
            for b in range(NBLK):
                last = {0: x2[:, b], 1: pair_sum[:, b]}
                used = {0: 0, 1: 0}
                for e, which in ((0, 0), (1, 0), (4, 0), (5, 1), (6, 0), (7, 1)):
                    pair, i = e // 2, e % 2
                    product = moe_bank[pair][:, i * D:(i + 1) * D]
                    dve.wait_ge(S["moe_done"], E // 2 * b + pair + 1)
                    if (b, pair) == (1, 3):
                        dve.wait_ge(S["moe_done"], E // 2 * b + pair + 1 + i)
                        product = last_bank[i][:, 0:D]
                    if used[which]:
                        dve.wait_ge(S["moe_used"], used[which])
                    elif which == 1:
                        dve.wait_ge(S["pair_ready"], b + 1)
                    o = (acc, acc2)[which][:, b]
                    stt(o, product, wgt[:, b, e:e + 1], last[which], ALU.mult, ALU.add).then_inc(S["moe_used"], 1)
                    n_sums += 1
                    last[which], used[which] = o, n_sums
                dve.wait_ge(S["moe_used"], n_sums)
                tt(acc[:, b], acc[:, b], acc2[:, b], ALU.add).then_inc(S["moe_used"], 1)
                n_sums += 1


def kernel(**inputs):
    import numpy as _np
    import concourse.bacc as _bacc
    from concourse import mybir as _mybir
    from concourse.bass_utils import run_bass_kernel_spmd as _run

    a = {k: _np.asarray(v) for k, v in inputs.items()}

    def tiles(m, n):
        return _np.ascontiguousarray(m.reshape(n, P, -1).transpose(1, 0, 2))

    def columns(v, n):
        return v.reshape(n, P).T

    def taps(m, n):
        return m.reshape(n, P, TAPS).transpose(1, 0, 2).reshape(P, n * TAPS)

    arrays = {
        "x": a["x"].reshape(T, D),
        "ctx": _np.ascontiguousarray(a["ctx_2048"].reshape(-1, CTXD)[:T]),
        "lens": a["mask_BxS2_if0"].reshape(LENS),
        "consts": shape_constants(),
        "cols": _np.ascontiguousarray(_np.concatenate([
            columns(a["L0_xattn_g_res"], 2), columns(a["L0_attn_rms_in_w"], 2), columns(a["L0_attn_o_norm_w"], 1),
            taps(a["L0_attn_conv_q_w"], 2), taps(a["L0_attn_conv_k_w"], 2), taps(a["L0_attn_conv_v_w"], 4)], 1)),
        "rows": _np.concatenate([a["L0_xattn_g_init"][:D], a["L0_xattn_b_in"], a["L0_attn_ln1_g"], a["L0_attn_ln1_b"],
                                 a["L0_attn_ln2_g"], a["L0_attn_ln2_b"], a["L0_attn_dt_bias"], a["L0_attn_A_log"]]),
        "b2": a["L0_attn_b2"][None],
        "win": tiles(a["L0_xattn_W_in"].T, 2),
        "wcat": tiles(_np.concatenate([a["L0_attn_Wq"], a["L0_attn_Wk"], a["L0_attn_Wv"], a["L0_attn_Wg"],
                                       a["L0_attn_Wa"], a["L0_attn_Wb"]], 1), 2),
        "wo": tiles(a["L0_attn_Wo"], H),
        "w2": tiles(a["L0_attn_W2"], 2),
        "wr": tiles(a["L0_ffn_Wr"], 2),
        "wit": _np.ascontiguousarray(a["L0_ffn_Wi"].reshape(E, D, 2, P).transpose(3, 0, 2, 1)),
        "fwo": _np.ascontiguousarray(a["L0_ffn_Wo"].reshape(E, 2, P, D).transpose(2, 0, 1, 3)),
    }
    nc = _bacc.Bacc("TRN2", target_bir_lowering=False, num_devices=1)
    args = [nc.dram_tensor(f"in_{k}", v.shape, _mybir.dt.from_np(v.dtype), kind="ExternalInput").ap()
            for k, v in arrays.items()]
    args.append(nc.dram_tensor("out_0", (T, D), _mybir.dt.float32, kind="ExternalOutput").ap())
    program(nc, *args)
    r = _run(nc, [{f"in_{k}": v for k, v in arrays.items()}], core_ids=[0])
    return r.results[0]["out_0"].reshape(1, T, D)
```
